# Optimizing a Trainium2 kernel written in Bass

```python
import numpy as np
import jax
import jax.numpy as jnp

def _softmax(x, axis=-1):
    return jax.nn.softmax(x, axis=axis)

def _gelu(x):
    return jax.nn.gelu(x, approximate=True)

def _silu(x):
    return jax.nn.silu(x)

def _sigmoid(x):
    return jax.nn.sigmoid(x)

def _layernorm(x, axis=-1, eps=1e-05):
    m = jnp.mean(x, axis=axis, keepdims=True)
    v = jnp.var(x, axis=axis, keepdims=True)
    return (x - m) / jnp.sqrt(v + eps)

def _scatter_add(tgt, idx, src, axis=0):
    return tgt.at[idx].add(src)

def _segment_sum(src, seg, n):
    return jax.ops.segment_sum(src, seg, n)
kernel_name = 'mk_perceiver_d1_seqx_r2_442ea6'

def setup_inputs(seed: int=0):
    np.random.seed(seed)
    _w = jnp.asarray

    def _rec_inputs():
        import jax
        import jax.numpy as jnp
        _rk = jax.random.key(seed)
        x = 7.22e-05 + 1 * jax.random.normal(jax.random.fold_in(_rk, 1), (64, 32, 512), jnp.float32)
        _lenS = 32 - jax.random.randint(jax.random.fold_in(_rk, 7), (64,), 0, max(1, 32 // 4) + 1, jnp.int32)
        _lenS2 = 257 - jax.random.randint(jax.random.fold_in(_rk, 8), (64,), 0, max(1, 257 // 4) + 1, jnp.int32)
        _ctx_1024P = jax.random.normal(jax.random.fold_in(_rk, 11), (64, 16, 512), jnp.float32)
        _ctx_1024c = jax.random.dirichlet(jax.random.fold_in(_rk, 511), 0.3 * jnp.ones((16,), jnp.float32), (64, 257))
        _ctx_1024t = jnp.einsum('bsk,bkd->bsd', _ctx_1024c, _ctx_1024P)
        _ctx_1024t = _ctx_1024t * jax.lax.rsqrt(jnp.mean(jnp.square(_ctx_1024t)) + 1e-12) * 0.953939
        ctx_1024 = -0.000514642 + 1.00011 * (_ctx_1024t + 0.3 * jax.random.normal(jax.random.fold_in(_rk, 611), (64, 257, 512), jnp.float32))
        return (x, ctx_1024)
    x, ctx_1024 = _rec_inputs()

    def _L0_xattn_setup():
        import jax, jax.numpy as jnp
        import numpy as np
        B, L_ENC, L_DEC, D = (16, 256, 128, 512)
        key = jax.random.key(seed)
        k1, k2, k3, k4, k5, k6 = jax.random.split(key, 6)
        encoder_hc = jax.random.normal(k1, (B, L_ENC, D), dtype=jnp.float32)
        decoder_hq = jax.random.normal(k2, (B, L_DEC, D), dtype=jnp.float32)
        w_sim = jax.random.normal(k3, (3 * D,), dtype=jnp.float32) * 0.02
        b_sim = jax.random.normal(k4, (1,), dtype=jnp.float32) * 0.02
        W_qv = jax.random.normal(k5, (4 * D, D), dtype=jnp.float32) * 0.02
        b_qv = jax.random.normal(k6, (D,), dtype=jnp.float32) * 0.02
        return {'encoder_hc': encoder_hc, 'decoder_hq': decoder_hq, 'w_sim': w_sim, 'b_sim': b_sim, 'W_qv': W_qv, 'b_qv': b_qv}
    _L0_xattn_all = _L0_xattn_setup()
    _L0_xattn_in = {k: v for k, v in _L0_xattn_all.items() if k in ('w_sim', 'b_sim', 'W_qv', 'b_qv')}
    del _L0_xattn_all

    def _L0_attn_setup():
        import jax, jax.numpy as jnp
        import numpy as np
        D_MODEL = 512
        N_HEADS = 16
        HEAD_DIM = D_MODEL // N_HEADS
        N_EXPERTS = 4
        HIDDEN = 4 * D_MODEL
        B, T = (1, 1024)

        def _apply_rope(x, sin, cos):
            x1, x2 = (x[..., ::2], x[..., 1::2])
            r1 = x1 * cos - x2 * sin
            r2 = x1 * sin + x2 * cos
            return jnp.stack((r1, r2), axis=-1).reshape(x.shape)
        key = jax.random.key(seed)
        ks = jax.random.split(key, 16)
        s = 0.02
        d, E, Hd = (D_MODEL, N_EXPERTS, HIDDEN)
        return {'x': jax.random.normal(ks[0], (B, T, d), dtype=jnp.float32), 'w_dw': jax.random.normal(ks[1], (d, 3), dtype=jnp.float32) * s, 'w_pw': jax.random.normal(ks[2], (d, d), dtype=jnp.float32) * s, 'w_qkv': jax.random.normal(ks[3], (3 * d, d), dtype=jnp.float32) * s, 'w_o': jax.random.normal(ks[4], (d, d), dtype=jnp.float32) * s, 'w_gate': jax.random.normal(ks[5], (d, d), dtype=jnp.float32) * s, 'b_gate': jnp.zeros((d,), dtype=jnp.float32), 'ln_g': jnp.ones((d,), dtype=jnp.float32), 'ln_b': jnp.zeros((d,), dtype=jnp.float32), 'w_moe_gate': jax.random.normal(ks[6], (E, d), dtype=jnp.float32) * s, 'w1': jax.random.normal(ks[7], (E, Hd, d), dtype=jnp.float32) * s, 'b1': jnp.zeros((E, Hd), dtype=jnp.float32), 'w2': jax.random.normal(ks[8], (E, d, Hd), dtype=jnp.float32) * s, 'b2': jnp.zeros((E, d), dtype=jnp.float32)}
    _L0_attn_all = _L0_attn_setup()
    _L0_attn_in = {k: v for k, v in _L0_attn_all.items() if k in ('w_dw', 'w_pw', 'w_qkv', 'w_o', 'w_gate', 'b_gate', 'ln_g', 'ln_b', 'w_moe_gate', 'w1', 'b1', 'w2', 'b2')}
    del _L0_attn_all

    def _L0_ffn_setup():
        import jax, jax.numpy as jnp
        import numpy as np
        N_BLOCKS = 16
        BLOCK = 128
        TOP_K = N_BLOCKS // 4
        key = jax.random.key(seed)
        ks = jax.random.split(key, 7)
        D, H = (512, 2048)
        s = lambda k, shape, scale: jax.random.normal(k, shape, dtype=jnp.float32) * scale
        return {'x': s(ks[0], (4, 2048, D), 1.0), 'w_router': s(ks[1], (D, N_BLOCKS), 0.03), 'b_router': s(ks[2], (N_BLOCKS,), 0.01), 'w1': s(ks[3], (H, D), 0.03), 'b1': s(ks[4], (H,), 0.01), 'w2': s(ks[5], (D, H), 0.03), 'b2': s(ks[6], (D,), 0.01)}
    _L0_ffn_all = _L0_ffn_setup()
    _L0_ffn_in = {k: v for k, v in _L0_ffn_all.items() if k in ('w_router', 'b_router', 'w1', 'b1', 'w2', 'b2')}
    del _L0_ffn_all
    return {'x': x, 'ctx_1024': ctx_1024, 'L0_xattn_w_sim': _L0_xattn_in['w_sim'], 'L0_xattn_b_sim': _L0_xattn_in['b_sim'], 'L0_xattn_W_qv': _L0_xattn_in['W_qv'], 'L0_xattn_b_qv': _L0_xattn_in['b_qv'], 'L0_attn_w_dw': _L0_attn_in['w_dw'], 'L0_attn_w_pw': _L0_attn_in['w_pw'], 'L0_attn_w_qkv': _L0_attn_in['w_qkv'], 'L0_attn_w_o': _L0_attn_in['w_o'], 'L0_attn_w_gate': _L0_attn_in['w_gate'], 'L0_attn_b_gate': _L0_attn_in['b_gate'], 'L0_attn_ln_g': _L0_attn_in['ln_g'], 'L0_attn_ln_b': _L0_attn_in['ln_b'], 'L0_attn_w_moe_gate': _L0_attn_in['w_moe_gate'], 'L0_attn_w1': _L0_attn_in['w1'], 'L0_attn_b1': _L0_attn_in['b1'], 'L0_attn_w2': _L0_attn_in['w2'], 'L0_attn_b2': _L0_attn_in['b2'], 'L0_ffn_w_router': _L0_ffn_in['w_router'], 'L0_ffn_b_router': _L0_ffn_in['b_router'], 'L0_ffn_w1': _L0_ffn_in['w1'], 'L0_ffn_b1': _L0_ffn_in['b1'], 'L0_ffn_w2': _L0_ffn_in['w2'], 'L0_ffn_b2': _L0_ffn_in['b2']}

def reference(x, ctx_1024, L0_xattn_w_sim, L0_xattn_b_sim, L0_xattn_W_qv, L0_xattn_b_qv, L0_attn_w_dw, L0_attn_w_pw, L0_attn_w_qkv, L0_attn_w_o, L0_attn_w_gate, L0_attn_b_gate, L0_attn_ln_g, L0_attn_ln_b, L0_attn_w_moe_gate, L0_attn_w1, L0_attn_b1, L0_attn_w2, L0_attn_b2, L0_ffn_w_router, L0_ffn_b_router, L0_ffn_w1, L0_ffn_b1, L0_ffn_w2, L0_ffn_b2):
    import jax
    import jax.numpy as jnp

    def _L0_xattn_ref(encoder_hc, decoder_hq, w_sim, b_sim, W_qv, b_qv):
        import jax, jax.numpy as jnp
        import numpy as np
        B, L_ENC, L_DEC, D = (16, 256, 128, 512)
        d = encoder_hc.shape[-1]
        w1, w2, w3 = (w_sim[:d], w_sim[d:2 * d], w_sim[2 * d:])
        Sim = (encoder_hc @ w1)[:, :, None] + (decoder_hq @ w2)[:, None, :] + jnp.einsum('bid,bjd->bij', encoder_hc * w3, decoder_hq) + b_sim[0]
        A = jax.nn.softmax(Sim, axis=2)
        hq_hat = jnp.einsum('bij,bjd->bid', A, decoder_hq)
        Batt = jax.nn.softmax(jnp.max(Sim, axis=2), axis=1)
        hc_bar = jnp.einsum('bi,bid->bd', Batt, encoder_hc)[:, None, :]
        hc_hat = jnp.broadcast_to(hc_bar, encoder_hc.shape)
        feats = jnp.concatenate([encoder_hc, hq_hat, encoder_hc * hq_hat, encoder_hc * hc_hat], axis=-1)
        hcq = feats @ W_qv + b_qv
        return hcq

    def _L0_attn_ref(x, w_dw, w_pw, w_qkv, w_o, w_gate, b_gate, ln_g, ln_b, w_moe_gate, w1, b1, w2, b2):
        import jax, jax.numpy as jnp
        import numpy as np
        D_MODEL = 512
        N_HEADS = 16
        HEAD_DIM = D_MODEL // N_HEADS
        N_EXPERTS = 4
        HIDDEN = 4 * D_MODEL
        B, T = (1, 1024)

        def _apply_rope(x, sin, cos):
            x1, x2 = (x[..., ::2], x[..., 1::2])
            r1 = x1 * cos - x2 * sin
            r2 = x1 * sin + x2 * cos
            return jnp.stack((r1, r2), axis=-1).reshape(x.shape)
        Bv, Tv, d = x.shape
        H, Dh = (N_HEADS, HEAD_DIM)
        dt = x.dtype
        xp = jnp.pad(x, ((0, 0), (2, 0), (0, 0)))
        y = xp[:, 0:Tv] * w_dw[:, 0] + xp[:, 1:Tv + 1] * w_dw[:, 1] + xp[:, 2:Tv + 2] * w_dw[:, 2]
        y = jnp.einsum('btd,ed->bte', y, w_pw)
        x = x + y
        qkv = jnp.einsum('btd,ed->bte', x, w_qkv).reshape(Bv, Tv, 3, H, Dh)
        q, k, v = (qkv[:, :, 0], qkv[:, :, 1], qkv[:, :, 2])
        inv_freq = 1.0 / 10000.0 ** (jnp.arange(0, Dh, 2, dtype=dt) / Dh)
        pos = jnp.arange(Tv, dtype=dt)
        theta = pos[:, None] * inv_freq[None, :]
        sin = jnp.sin(theta)[None, :, None, :]
        cos = jnp.cos(theta)[None, :, None, :]
        q = _apply_rope(q, sin, cos)
        k = _apply_rope(k, sin, cos)
        q_phi = jax.nn.elu(q) + 1.0
        k_phi = jax.nn.elu(k) + 1.0
        kv = k_phi[..., :, None] * v[..., None, :]
        kv_prefix = jnp.cumsum(kv, axis=1)
        k_prefix = jnp.cumsum(k_phi, axis=1)
        num = jnp.einsum('bthd,bthdm->bthm', q_phi, kv_prefix)
        denom = jnp.sum(q_phi * k_prefix, axis=-1, keepdims=True)
        attn = num / (denom + 1e-06)
        attn = attn.reshape(Bv, Tv, d)
        attn = jnp.einsum('btd,ed->bte', attn, w_o)
        delta = x - jnp.concatenate([x[:, :1], x[:, :-1]], axis=1)
        gate = jax.nn.sigmoid(jnp.einsum('btd,ed->bte', delta, w_gate) + b_gate)
        x = x + gate * attn
        mu = jnp.mean(x, axis=-1, keepdims=True)
        var = jnp.mean((x - mu) ** 2, axis=-1, keepdims=True)
        h = (x - mu) / jnp.sqrt(var + 1e-05) * ln_g + ln_b
        gw = jax.nn.softmax(jnp.einsum('btd,ed->bte', h, w_moe_gate), axis=-1)
        hid = jax.nn.silu(jnp.einsum('btd,efd->btef', h, w1) + b1)
        eo = jnp.einsum('btef,edf->bted', hid, w2) + b2
        ffn = jnp.einsum('bte,bted->btd', gw, eo)
        return x + ffn

    def _L0_ffn_ref(x, w_router, b_router, w1, b1, w2, b2):
        import jax, jax.numpy as jnp
        import numpy as np
        N_BLOCKS = 16
        BLOCK = 128
        TOP_K = N_BLOCKS // 4
        orig_shape = x.shape
        D = orig_shape[-1]
        xf = x.reshape(-1, D)
        prob = jax.nn.softmax(xf @ w_router + b_router, axis=-1)
        _, idx = jax.lax.top_k(prob, TOP_K)
        mask = (idx[:, :, None] == jnp.arange(N_BLOCKS)[None, None, :]).any(axis=1)
        mask = mask.astype(x.dtype)
        w1b = w1.reshape(N_BLOCKS, BLOCK, D)
        b1b = b1.reshape(N_BLOCKS, BLOCK)
        w2b = jnp.transpose(w2.reshape(D, N_BLOCKS, BLOCK), (1, 2, 0))
        h = jax.nn.relu(jnp.einsum('nd,ebd->neb', xf, w1b) + b1b[None])
        y = jnp.einsum('neb,ebd,ne->nd', h, w2b, mask)
        y = y + b2[None, :]
        return y.reshape(orig_shape)
    x = x + _L0_xattn_ref(_layernorm(x, axis=-1), ctx_1024, L0_xattn_w_sim, L0_xattn_b_sim, L0_xattn_W_qv, L0_xattn_b_qv)
    x = x + _L0_attn_ref(_layernorm(x, axis=-1), L0_attn_w_dw, L0_attn_w_pw, L0_attn_w_qkv, L0_attn_w_o, L0_attn_w_gate, L0_attn_b_gate, L0_attn_ln_g, L0_attn_ln_b, L0_attn_w_moe_gate, L0_attn_w1, L0_attn_b1, L0_attn_w2, L0_attn_b2)
    x = x + _L0_ffn_ref(_layernorm(x, axis=-1), L0_ffn_w_router, L0_ffn_b_router, L0_ffn_w1, L0_ffn_b1, L0_ffn_w2, L0_ffn_b2)
    return x

_drawn_inputs = setup_inputs


def setup_inputs(seed=0):
    import zlib

    import numpy as np

    out = dict(_drawn_inputs(seed))
    spreads = {'L0_attn_b_gate': (0.0, 2.0),
     'L0_attn_ln_g': (1.0, 0.6),
     'L0_attn_ln_b': (0.0, 0.516),
     'L0_attn_b1': (0.0, 0.324),
     'L0_attn_b2': (0.0, 0.1)}
    factors = {'L0_attn_w_dw': 3.623,
     'L0_attn_w_pw': 3.745,
     'L0_attn_w_gate': 12.12,
     'L0_ffn_b_router': 3.177,
     'L0_ffn_b1': 26.622,
     'L0_ffn_b2': 8.0}
    for name, (base, spread) in spreads.items():
        noise = np.random.default_rng([zlib.crc32(name.encode()), seed]).standard_normal(out[name].shape)
        drawn = base * np.exp(spread * noise) if base else spread * noise
        out[name] = jnp.asarray(drawn.astype(out[name].dtype))
    for name, factor in factors.items():
        out[name] = (out[name] * factor).astype(out[name].dtype)
    return out
```

```python
from contextlib import ExitStack

import concourse.bass as bass
import numpy as np
from concourse import mybir

F32 = mybir.dt.float32
F32R = mybir.dt.float32r
BF16 = mybir.dt.bfloat16
U32 = mybir.dt.uint32
ALU = mybir.AluOpType
ACT = mybir.ActivationFunctionType
AX = mybir.AxisListType

P = 128
D = 512
DC = D // P
SEQ = 32
BATCH = 64
TOKENS = BATCH * SEQ
TILES = TOKENS // P
PER_TILE = P // SEQ
CTX = 257
CTX_CHUNKS = CTX // P
GROUP = 512
GROUPS = TOKENS // GROUP
TILES_PER_GROUP = GROUP // P
FEATS = 4 * D
FEAT_CHUNKS = FEATS // P
HEADS = 16
HEAD = D // HEADS
HEADS_PER_CHUNK = P // HEAD
CHUNK = 256
CHUNKS = TOKENS // CHUNK
CT = CHUNK // P
CSEQ = CHUNK // SEQ
EXPERTS = 4
HIDDEN = 2048
SUB = 512
FC = SUB // P
SUBS_PER_EXPERT = HIDDEN // SUB
MOE_SUBS = EXPERTS * SUBS_PER_EXPERT
FFN_SUBS = HIDDEN // SUB
SUBS = MOE_SUBS + FFN_SUBS
BLOCKS = 16
TOP_K = 4
EPS = 1e-5
DEN_EPS = 1e-6
SHUT = -(2.0 ** 127)


class Frame:

    def __init__(self, nc, stack, tag=""):
        self.nc, self.stack, self.tag = nc, stack, tag

    def sbuf(self, name, shape, dt=F32):
        return self.stack.enter_context(self.nc.sbuf_tensor(self.tag + name, shape, dt))

    def psum(self, name, shape=(P, 512)):
        return self.stack.enter_context(self.nc.psum_tensor(self.tag + name, list(shape), F32))

    def sem(self, name):
        return self.stack.enter_context(self.nc.semaphore(self.tag + name))


def three_products(pe, out, w_hi, w_lo, m_hi, m_lo, first, last):
    pe.matmul(out, w_hi, m_hi, start=first, stop=False)
    pe.matmul(out, w_hi, m_lo, start=False, stop=False)
    return pe.matmul(out, w_lo, m_hi, start=False, stop=last)


def cross_attention(nc, dram, keep):
    with ExitStack() as stack:
        fr = Frame(nc, stack, "xa_")
        x, wq_hi, wq_lo = keep["x"], keep["r_hi"], keep["r_lo"]
        ident = keep["ident"]
        ctxT = [fr.sbuf(f"ctxT{i}", [P, DC, PER_TILE, CTX]) for i in range(2)]
        ctxN = [fr.sbuf(f"ctxN{i}", [P, PER_TILE, CTX_CHUNKS, D]) for i in range(2)]
        ctxR = [fr.sbuf(f"ctxR{i}", [PER_TILE, D]) for i in range(2)]
        feats = fr.sbuf("feats", [P, FEAT_CHUNKS, P])
        feats_hi = fr.sbuf("feats_hi", [P, FEAT_CHUNKS, P], F32R)
        feats_lo = fr.sbuf("feats_lo", [P, FEAT_CHUNKS, P], F32R)
        xn = fr.sbuf("xn", [P, D])
        hq = fr.sbuf("hq", [P, D])
        sim_w = fr.sbuf("sim_w", [P, DC, P])
        probs = fr.sbuf("probs", [P, CTX])
        probs_rest = fr.sbuf("probs_rest", [P, PER_TILE])
        probsT = fr.sbuf("probsT", [P, CTX_CHUNKS, P])
        probsT_rest = fr.sbuf("probsT_rest", [PER_TILE, P])
        b_qv = fr.sbuf("b_qv", [P, D])
        w_sim = fr.sbuf("w_sim", [P, 3, DC])
        b_sim = fr.sbuf("b_sim", [P, 1])
        seq_of = fr.sbuf("seq_of", [P, PER_TILE])
        stats = fr.sbuf("stats", [P, 6])
        mean_var = fr.sbuf("mean_var", [P, TILES, 2])
        rstd = fr.sbuf("rstd", [P, TILES])
        neg_max = fr.sbuf("neg_max", [P, 1])
        row_sum = fr.sbuf("row_sum", [P, 1])
        row_rec = fr.sbuf("row_rec", [P, 1])
        top = fr.sbuf("top", [P, 1])
        top_wide = fr.sbuf("top_wide", [P, SEQ])
        top_seq = fr.sbuf("top_seq", [P, SEQ])
        neg_top = fr.sbuf("neg_top", [P, 1])
        top_exp = fr.sbuf("top_exp", [P, SEQ])
        own_exp = fr.sbuf("own_exp", [P, 1])
        top_sum = fr.sbuf("top_sum", [P, 1])
        top_rec = fr.sbuf("top_rec", [P, 1])
        batt = fr.sbuf("batt", [P, PER_TILE])
        bar = fr.sbuf("bar", [P, DC, PER_TILE])
        eps = fr.sbuf("eps", [P, 1])

        ps_t = fr.psum("ps_t")
        ps_sim = fr.psum("ps_sim")
        ps_p = fr.psum("ps_p")
        ps_hq = fr.psum("ps_hq")
        ps_hqt = fr.psum("ps_hqt")
        ps_m = fr.psum("ps_m")
        ps_out = [fr.psum(f"ps_out{i}") for i in range(2)]

        x_in = [fr.sem(f"x_in{g}") for g in range(GROUPS)]
        small_in = fr.sem("small_in")
        wq_in = fr.sem("wq_in")
        wq_hi_done = fr.sem("wq_hi_done")
        wq_split = fr.sem("wq_split")
        ctx_in = [fr.sem(f"ctx_in{i}") for i in range(2)]
        stats_done = fr.sem("stats_done")
        aggr_done = fr.sem("aggr_done")
        eps_set = fr.sem("eps_set")
        std_done = fr.sem("std_done")
        rstd_done = fr.sem("rstd_done")
        xn_done = fr.sem("xn_done")
        xnT_done = fr.sem("xnT_done")
        hcT_done = fr.sem("hcT_done")
        sim_w_done = fr.sem("sim_w_done")
        sim_done = fr.sem("sim_done")
        neg_max_done = fr.sem("neg_max_done")
        probs_done = fr.sem("probs_done")
        rest_done = fr.sem("rest_done")
        probsT_ps = fr.sem("probsT_ps")
        probsT_done = fr.sem("probsT_done")
        hq_ps = fr.sem("hq_ps")
        hq_done = fr.sem("hq_done")
        hqT_ps = fr.sem("hqT_ps")
        hqT_done = fr.sem("hqT_done")
        top_step = fr.sem("top_step")
        own_done = fr.sem("own_done")
        batt_done = fr.sem("batt_done")
        bar_ps = fr.sem("bar_ps")
        bar_done = fr.sem("bar_done")
        prod_done = fr.sem("prod_done")
        hi_done = fr.sem("hi_done")
        split_done = fr.sem("split_done")
        quarter_used = fr.sem("quarter_used")
        out_done = fr.sem("out_done")
        rec_done = fr.sem("rec_done")
        bias_done = fr.sem("bias_done")
        x_done = fr.sem("x_done")
        block = stack.enter_context(nc.Block())

        QUARTERS = 4

        @block.sync
        def _(sp):
            sp.dma_start(ident[:], dram["ident"]).then_inc(small_in, 16)
            sp.dma_start(w_sim[:], dram["w_sim"]).then_inc(small_in, 16)
            sp.dma_start(b_sim[:], dram["b_sim"].partition_broadcast(P)).then_inc(small_in, 16)
            sp.dma_start(seq_of[:], dram["seq_of"]).then_inc(small_in, 16)
            sp.dma_start(b_qv[:], dram["b_qv"].partition_broadcast(P)).then_inc(small_in, 16)
            for g in range(GROUPS):
                rows = slice(g * GROUP, (g + 1) * GROUP)
                sp.dma_start(x[:, g * TILES_PER_GROUP:(g + 1) * TILES_PER_GROUP, :],
                             dram["x"][rows, :].rearrange("(t p) d -> p t d", p=P)).then_inc(x_in[g], 16)

            def load_ctx(t, par):
                sp.dma_start(ctxT[par][:], dram["ctxT"][bass.ds(t, 1)].rearrange("o p c b j -> p (o c) b j")).then_inc(ctx_in[par], 16)
                sp.dma_start(ctxN[par][:], dram["ctxN"][bass.ds(t, 1)].rearrange("o p b c d -> p (o b) c d")).then_inc(ctx_in[par], 16)
                sp.dma_start(ctxR[par][:], dram["ctxR"][bass.ds(t, 1)].rearrange("o b d -> (o b) d")).then_inc(ctx_in[par], 16)

            load_ctx(0, 0)
            for q in range(QUARTERS):
                if q:
                    sp.wait_ge(wq_split, q)
                sp.dma_start(feats[:].rearrange("p k n -> p (k n)").rearrange("p (k n) -> p k n", n=D),
                             dram["W_qv"][q * D:(q + 1) * D, :].rearrange("(k p) n -> p k n", p=P)).then_inc(wq_in, 16)
            load_ctx(1, 1)
            with sp.Fori(0, TILES // 2 - 1) as pair:
                for par in range(2):
                    sp.wait_ge(hq_ps, 2 * pair + par + 1)
                    load_ctx(2 * pair + par + 2, par)

        def in_pairs(eng, tile):
            tile(0, 0, True)
            with eng.Fori(0, TILES // 2 - 1) as pair:
                tile(2 * pair + 1, 1, False)
                tile(2 * pair + 2, 0, False)
            tile(TILES - 1, 1, False)

        @block.tensor
        def _(pe):
            pe.wait_ge(small_in, 16 * 5)
            pe.wait_ge(wq_split, QUARTERS)

            def project(t, par, q):
                pe.wait_ge(split_done, QUARTERS * t + q + 1)
                for k in range(DC * q, DC * q + DC):
                    last = three_products(pe, ps_out[par][:], feats_hi[:, k, :], feats_lo[:, k, :],
                                          wq_hi[:, k, :], wq_lo[:, k, :], k == 0, k == FEAT_CHUNKS - 1)
                last.then_inc(quarter_used, 1)

            def tile(t, par, first):
                pe.wait_ge(xn_done, t + 1)
                for c in range(DC):
                    last = pe.transpose(ps_t[:, c * P:(c + 1) * P], xn[:, c * P:(c + 1) * P], ident[:])
                last.then_inc(xnT_done, 1)
                if not first:
                    project(t - 1, 1 - par, 1)
                pe.wait_ge(sim_w_done, t + 1)
                pe.wait_ge(ctx_in[par], 24 * (t - par) + 48)
                for c in range(DC):
                    for b in range(PER_TILE):
                        rows = slice(b * SEQ, (b + 1) * SEQ)
                        pe.matmul(ps_sim[rows, 0:CTX], sim_w[:, c, rows], ctxT[par][:, c, b, :],
                                  start=c == 0, stop=c == DC - 1)
                for c in range(DC):
                    last = pe.matmul(ps_m[:, 0:1], feats[:, c, :], w_sim[:, 0, c:c + 1],
                                     start=c == 0, stop=c == DC - 1)
                last.then_inc(sim_done, 1)
                if not first:
                    project(t - 1, 1 - par, 2)
                pe.wait_ge(rest_done, t + 1)
                for c in range(CTX_CHUNKS):
                    pe.transpose(ps_p[:, c * P:(c + 1) * P], probs[:, c * P:(c + 1) * P], ident[:])
                pe.transpose(ps_p[0:PER_TILE, CTX_CHUNKS * P:(CTX_CHUNKS + 1) * P], probs_rest[:], ident[:]).then_inc(probsT_ps, 1)
                if not first:
                    project(t - 1, 1 - par, 3)
                pe.wait_ge(probsT_done, t + 1)
                for c in range(CTX_CHUNKS):
                    for b in range(PER_TILE):
                        rows = slice(b * SEQ, (b + 1) * SEQ)
                        pe.matmul(ps_hq[rows, :], probsT[:, c, rows], ctxN[par][:, b, c, :],
                                  start=c == 0, stop=False)
                pe.matmul(ps_hq[:], probsT_rest[:], ctxR[par][:], start=False, stop=True).then_inc(hq_ps, 1)
                project(t, par, 0)
                pe.wait_ge(batt_done, t + 1)
                for c in range(DC):
                    last = pe.matmul(ps_m[:, 4 * c:4 * c + 4], xn[:, c * P:(c + 1) * P], batt[:], start=True, stop=True)
                last.then_inc(bar_ps, 1)
                pe.wait_ge(hq_done, t + 1)
                for c in range(DC):
                    last = pe.transpose(ps_hqt[:, c * P:(c + 1) * P], hq[:, c * P:(c + 1) * P], ident[:])
                last.then_inc(hqT_ps, 1)

            in_pairs(pe, tile)
            for q in range(1, QUARTERS):
                project(TILES - 1, 1, q)

        @block.scalar
        def _(act):
            for q in range(QUARTERS):
                act.wait_ge(wq_in, 16 * (q + 1))
                act.activation(wq_hi[:, DC * q:DC * (q + 1), :], feats[:].rearrange("p k n -> p (k n)").rearrange("p (k n) -> p k n", n=D), ACT.Copy).then_inc(wq_hi_done, 1)
            act.wait_ge(eps_set, 1)
            act.wait_ge(aggr_done, TILES)
            act.activation(rstd[:], mean_var[:, :, 1], ACT.Sqrt, bias=eps[:]).then_inc(std_done, 1)

            def split_hi(t, q, first):
                if not first:
                    act.wait_ge(quarter_used, QUARTERS * (t - 1) + q + 1)
                act.activation(feats_hi[:, DC * q:DC * (q + 1), :], feats[:, DC * q:DC * (q + 1), :], ACT.Copy).then_inc(hi_done, 1)

            def tile(t, par, first):
                act.wait_ge(xnT_done, t + 1)
                if not first:
                    act.wait_ge(split_done, QUARTERS * t)
                else:
                    act.wait_ge(wq_split, QUARTERS)
                act.activation(feats[:, 0:DC, :], ps_t[:].rearrange("p (c n) -> p c n", c=DC), ACT.Copy).then_inc(hcT_done, 1)
                act.wait_ge(hcT_done, t + 1)
                split_hi(t, 0, first)
                act.wait_ge(neg_max_done, t + 1)
                act.activation(probs[:], ps_sim[:, 0:CTX], ACT.Exp, bias=neg_max[:], accum_out=row_sum[:]).then_inc(probs_done, 1)
                act.wait_ge(probsT_ps, t + 1)
                act.activation(probsT[:], ps_p[:, 0:CTX_CHUNKS * P].rearrange("p (c n) -> p c n", c=CTX_CHUNKS), ACT.Copy)
                act.activation(probsT_rest[:], ps_p[0:PER_TILE, CTX_CHUNKS * P:(CTX_CHUNKS + 1) * P], ACT.Copy).then_inc(probsT_done, 1)
                act.wait_ge(top_step, 4 * t + 4)
                act.activation(top_exp[:], top_seq[:], ACT.Exp, bias=neg_top[:], accum_out=top_sum[:]).then_inc(own_done, 1)
                act.activation(own_exp[:], top[:], ACT.Exp, bias=neg_top[:]).then_inc(own_done, 1)
                act.wait_ge(bar_ps, t + 1)
                act.activation(bar[:], ps_m[:, 0:DC * PER_TILE].rearrange("p (c b) -> p c b", c=DC), ACT.Copy).then_inc(bar_done, 1)
                act.wait_ge(hq_ps, t + 1)
                act.activation(hq[:], ps_hq[:], ACT.Copy, scale=row_rec[:]).then_inc(hq_done, 1)
                act.wait_ge(hqT_ps, t + 1)
                act.activation(feats[:, DC:2 * DC, :], ps_hqt[:].rearrange("p (c n) -> p c n", c=DC), ACT.Copy).then_inc(hqT_done, 1)
                act.wait_ge(hqT_done, t + 1)
                split_hi(t, 1, first)
                act.wait_ge(prod_done, 2 * t + 1)
                split_hi(t, 2, first)
                act.wait_ge(prod_done, 2 * t + 2)
                split_hi(t, 3, first)

            in_pairs(act, tile)

        @block.vector
        def _(dve):
            dve.memset(eps[:], EPS).then_inc(eps_set, 1)

            def split_lo(t, q):
                dve.wait_ge(hi_done, QUARTERS * t + q + 1)
                quarter = slice(DC * q, DC * (q + 1))
                dve.tensor_tensor(feats_lo[:, quarter, :], feats[:, quarter, :], feats_hi[:, quarter, :].bitcast(F32), ALU.subtract).then_inc(split_done, 1)

            for g in range(GROUPS):
                dve.wait_ge(x_in[g], 16)
                for t in range(g * TILES_PER_GROUP, (g + 1) * TILES_PER_GROUP):
                    if t:
                        dve.wait_ge(aggr_done, t)
                    dve.bn_stats(stats[:], x[:, t, :]).then_inc(stats_done, 1)
                    dve.wait_ge(stats_done, t + 1)
                    dve.bn_aggr(mean_var[:, t, :], stats[:]).then_inc(aggr_done, 1)
            for q in range(QUARTERS):
                dve.wait_ge(wq_hi_done, q + 1)
                dve.tensor_tensor(wq_lo[:, DC * q:DC * (q + 1), :], feats[:].rearrange("p k n -> p (k n)").rearrange("p (k n) -> p k n", n=D),
                                  wq_hi[:, DC * q:DC * (q + 1), :].bitcast(F32), ALU.subtract).then_inc(wq_split, 1)
            dve.wait_ge(std_done, 1)
            dve.reciprocal(rstd[:], rstd[:]).then_inc(rstd_done, 1)
            dve.wait_ge(rstd_done, 1)
            dve.wait_ge(small_in, 16 * 5)

            def finish(t, par):
                dve.wait_ge(quarter_used, QUARTERS * (t + 1))
                dve.tensor_tensor(x[:, bass.ds(t, 1), :], ps_out[par][:].rearrange("p (o n) -> p o n", o=1), x[:, bass.ds(t, 1), :], ALU.add).then_inc(x_done, 1)

            def tile(t, par, first):
                if not first:
                    dve.wait_ge(hqT_ps, t)
                dve.tensor_scalar(xn[:].rearrange("p (o n) -> p o n", o=1), x[:, bass.ds(t, 1), :], mean_var[:, bass.ds(t, 1), 0], rstd[:, bass.ds(t, 1)], ALU.subtract, ALU.mult).then_inc(xn_done, 1)
                dve.wait_ge(xn_done, t + 1)
                dve.tensor_tensor(x[:, bass.ds(t, 1), :], x[:, bass.ds(t, 1), :], b_qv[:].rearrange("p (o n) -> p o n", o=1), ALU.add).then_inc(bias_done, 1)
                dve.wait_ge(hcT_done, t + 1)
                for c in range(DC):
                    last = dve.tensor_scalar(sim_w[:, c, :], feats[:, c, :], w_sim[:, 2, c:c + 1], w_sim[:, 1, c:c + 1], ALU.mult, ALU.add)
                last.then_inc(sim_w_done, 1)
                split_lo(t, 0)
                dve.wait_ge(sim_done, t + 1)
                dve.tensor_reduce(neg_max[:], ps_sim[:, 0:CTX], AX.X, ALU.max, negate=True).then_inc(neg_max_done, 1)
                dve.wait_ge(neg_max_done, t + 1)
                dve.scalar_tensor_tensor(top[:], ps_m[:, 0:1], b_sim[:], neg_max[:], ALU.add, ALU.subtract).then_inc(top_step, 1)
                dve.wait_ge(probs_done, t + 1)
                dve.reciprocal(row_rec[:], row_sum[:])
                dve.tensor_scalar(probs_rest[:], seq_of[:], probs[:, CTX - 1:CTX], None, ALU.mult).then_inc(rest_done, 1)
                dve.wait_ge(top_step, 4 * t + 1)
                dve.tensor_copy(top_wide[:], top[:].to_broadcast([P, SEQ])).then_inc(top_step, 1)
                dve.wait_ge(top_step, 4 * t + 2)
                dve.transpose(top_seq[:], top_wide[:]).then_inc(top_step, 1)
                dve.wait_ge(top_step, 4 * t + 3)
                dve.tensor_reduce(neg_top[:], top_seq[:], AX.X, ALU.max, negate=True).then_inc(top_step, 1)
                dve.wait_ge(own_done, 2 * t + 2)
                dve.reciprocal(top_rec[:], top_sum[:]).then_inc(rec_done, 1)
                dve.wait_ge(rec_done, t + 1)
                dve.tensor_scalar(batt[:], seq_of[:], own_exp[:], top_rec[:], ALU.mult, ALU.mult).then_inc(batt_done, 1)
                if not first:
                    finish(t - 1, 1 - par)
                dve.wait_ge(bar_done, t + 1)
                dve.wait_ge(hqT_done, t + 1)
                dve.tensor_tensor(feats[:, 2 * DC:3 * DC, :], feats[:, 0:DC, :], feats[:, DC:2 * DC, :], ALU.mult).then_inc(prod_done, 1)
                split_lo(t, 1)
                bars = bar[:].rearrange("p c b -> p (c b)").unsqueeze(2).to_broadcast([P, DC * PER_TILE, SEQ])
                dve.tensor_tensor(feats[:, 3 * DC:4 * DC, :].rearrange("p c (b s) -> p (c b) s", s=SEQ),
                                  feats[:, 0:DC, :].rearrange("p c (b s) -> p (c b) s", s=SEQ), bars, ALU.mult).then_inc(prod_done, 1)
                split_lo(t, 2)
                split_lo(t, 3)

            in_pairs(dve, tile)
            finish(TILES - 1, 1)
            dve.wait_ge(x_done, TILES)


def linear_attention(nc, dram, keep):
    with ExitStack() as stack:
        fr = Frame(nc, stack, "la_")
        x, ident = keep["x"], keep["ident"]
        PW, WQ, WK, WV, WG, WO = range(6)
        late_hi = fr.sbuf("late_hi", [P, 2 * DC, D], F32R)
        late_lo = fr.sbuf("late_lo", [P, 2 * DC, D], F32R)

        def weight(n):
            if n < WG:
                return keep["r_hi"][:, DC * n:DC * (n + 1), :], keep["r_lo"][:, DC * n:DC * (n + 1), :]
            n -= WG
            return late_hi[:, DC * n:DC * (n + 1), :], late_lo[:, DC * n:DC * (n + 1), :]

        xn = fr.sbuf("xn", [P, CT, D])
        xc = [fr.sbuf(f"xc{i}", [P, DC, CHUNK]) for i in range(2)]
        xc_hi = fr.sbuf("xc_hi", [P, DC, CHUNK], F32R)
        xc_lo = fr.sbuf("xc_lo", [P, DC, CHUNK], F32R)
        part = fr.sbuf("part", [P, DC, CHUNK])
        turn_hi = fr.sbuf("turn_hi", [P, DC, CHUNK], F32R)
        turn_lo = fr.sbuf("turn_lo", [P, DC, CHUNK], F32R)
        q = fr.sbuf("q", [P, DC, CHUNK])
        k = fr.sbuf("k", [P, DC, CHUNK])
        swap = fr.sbuf("swap", [P, DC, CHUNK])
        exq = fr.sbuf("exq", [P, DC, CHUNK])
        gate = fr.sbuf("gate", [P, DC, CHUNK])
        heads = fr.sbuf("heads", [P, DC, CT, HEADS_PER_CHUNK, P])
        v_ext = fr.sbuf("v_ext", [P, CT, HEADS, HEAD + 1])
        scores = [fr.sbuf(f"scores{i}", [P, HEADS_PER_CHUNK, P]) for i in range(2)]
        causal = fr.sbuf("causal", [P, P])
        cos = fr.sbuf("cos", [P, SEQ])
        sin = fr.sbuf("sin", [P, SEQ])
        w_dw = fr.sbuf("w_dw", [P, DC, 3])
        b_gate = fr.sbuf("b_gate", [P, DC])
        half_b_gate = fr.sbuf("half_b_gate", [P, DC])
        stats = fr.sbuf("stats", [P, 6])
        mean_var = fr.sbuf("mean_var", [P, TILES, 2])
        rstd = fr.sbuf("rstd", [P, TILES])
        eps = fr.sbuf("eps", [P, 1])
        x2_mv = fr.sbuf("x2_mv", [P, CT, 2])
        x2_stats = fr.sbuf("x2_stats", [P, CT, 6])
        den = fr.sbuf("den", [P, HEADS])
        den_rec = fr.sbuf("den_rec", [P, HEADS])
        attn = swap[:].rearrange("p c n -> p (c n)").rearrange("p (t n) -> p t n", t=CT)
        stage = [heads[:, 2 * i:2 * i + 2].rearrange("p a b c d -> p (a b c d)").rearrange("p (k n) -> p k n", n=D) for i in range(2)]

        ps_a = fr.psum("ps_a", [P, 2, 512])
        ps_b = fr.psum("ps_b", [P, 2, 512])
        ps_c = fr.psum("ps_c", [P, 2, 512])
        ps_d = fr.psum("ps_d", [P, 2, 512])

        def wide(ps):
            return ps[:].rearrange("p a n -> p (a n)").rearrange("p (c n) -> p c n", c=DC)

        names = ("small_in stage_hi stage_lo stats_done aggr_done eps_set std_done rstd_done ones_set heads_zero "
                 "half_done xn_done xnT_ps xT_done conv_step y_hi_done y_lo_done pw_ps xc_done xc_hi_done xc_lo_done "
                 "delta_done d_hi_done d_lo_done q_ps q_raw k_ps k_raw v_ps v_done rope_step rope_q rope_k exq_step exk_step "
                 "phi_q phi_k gate_ps gate_done scores_ps masked heads_ps den_done norm_done attnT_ps attnT_done "
                 "a_hi_done a_lo_done wo_ps mix_step x2_ps x2_stats x2_done x2_out x_done").split()
        s = {n: fr.sem(n) for n in names}
        stage_in = [fr.sem(f"stage_in{i}") for i in range(2)]
        block = stack.enter_context(nc.Block())
        STEPS = CT * DC

        def chunks(eng, step):
            step(0, 0, True, False)
            with eng.Fori(0, CHUNKS // 2 - 1) as pair:
                step(2 * pair + 1, 1, False, False)
                step(2 * pair + 2, 0, False, False)
            step(CHUNKS - 1, 1, False, True)

        @block.sync
        def _(sp):
            for n in range(6):
                if n >= 2:
                    sp.wait_ge(s["stage_lo"], n - 1)
                sp.dma_start(stage[n % 2], dram["attn_w"][n].rearrange("(k p) n -> p k n", p=P)).then_inc(stage_in[n % 2], 16)
                if n == 1:
                    for t, name in ((causal, "causal"), (cos, "cos"), (sin, "sin"), (w_dw, "w_dw"), (b_gate, "b_gate")):
                        sp.dma_start(t[:], dram[name]).then_inc(s["small_in"], 16)

            def step(i, par, first, last):
                sp.wait_ge(s["x2_done"], i + 1)
                sp.dma_start(dram["x2"][bass.ds(CT * i, CT)].rearrange("t p d -> p t d"), xn[:]).then_inc(s["x2_out"], 16)

            chunks(sp, step)
            sp.wait_ge(s["x2_out"], 16 * CHUNKS)

        @block.gpsimd
        def _(pool):
            nc.gpsimd.memset(v_ext[:, :, :, HEAD:HEAD + 1], 1.0).then_inc(s["ones_set"], 1)
            pool.wait_ge(s["stage_lo"], 6)
            nc.gpsimd.memset(heads[:], 0.0).then_inc(s["heads_zero"], 1)

        @block.tensor
        def _(pe):
            def transpose_norm(i):
                pe.wait_ge(s["xn_done"], i + 1)
                for c in range(DC):
                    for t in range(CT):
                        last = pe.transpose(wide(ps_a)[:, c, t * P:(t + 1) * P], xn[:, t, c * P:(c + 1) * P], ident[:])
                last.then_inc(s["xnT_ps"], 1)

            def project(n, ps, m_hi, m_lo, done):
                w_hi, w_lo = weight(n)
                for e in range(DC):
                    cols = slice(e * P, (e + 1) * P)
                    for c in range(DC):
                        last = three_products(pe, wide(ps)[:, e, :], w_hi[:, c, cols], w_lo[:, c, cols],
                                              m_hi[:, c, :], m_lo[:, c, :], c == 0, c == DC - 1)
                last.then_inc(done, 1)

            def pointwise(i):
                pe.wait_ge(s["y_lo_done"], i + 1)
                project(PW, ps_b, turn_hi, turn_lo, s["pw_ps"])

            pe.wait_ge(s["stage_lo"], 6)
            transpose_norm(0)
            pointwise(0)

            def step(i, par, first, last):
                pe.wait_ge(s["xc_lo_done"], i + 1)
                project(WQ, ps_b, xc_hi, xc_lo, s["q_ps"])
                project(WK, ps_c, xc_hi, xc_lo, s["k_ps"])
                w_hi, w_lo = weight(WV)
                for t in range(CT):
                    toks = slice(t * P, (t + 1) * P)
                    for c in range(DC):
                        mm = three_products(pe, ps_d[:, t, :], xc_hi[:, c, toks], xc_lo[:, c, toks],
                                            w_hi[:, c, :], w_lo[:, c, :], c == 0, c == DC - 1)
                mm.then_inc(s["v_ps"], 1)
                pe.wait_ge(s["d_lo_done"], i + 1)
                pe.wait_ge(s["q_raw"], i + 1)
                project(WG, ps_b, turn_hi, turn_lo, s["gate_ps"])
                if not last:
                    if not first:
                        pe.wait_ge(s["x_done"], i)
                        pe.wait_ge(s["x2_done"], i)
                    transpose_norm(i + 1)
                pe.wait_ge(s["phi_q"], i + 1)
                pe.wait_ge(s["phi_k"], i + 1)
                pe.wait_ge(s["v_done"], i + 1)

                def score(n):
                    t, c = n // DC, n % DC
                    pe.matmul(ps_c[:, n % 2, :], k[:, c, t * P:(t + 1) * P], heads[:, c, t].rearrange("p j n -> p (j n)"),
                              start=True, stop=True).then_inc(s["scores_ps"], 1)

                score(0)
                score(1)
                for n in range(STEPS):
                    t, c = n // DC, n % DC
                    pe.wait_ge(s["masked"], STEPS * i + n + 1)
                    if n == DC and not last:
                        pe.wait_ge(s["xT_done"], i + 2)
                    ps = (ps_d, ps_a)[t]
                    for j in range(HEADS_PER_CHUNK):
                        h = HEADS_PER_CHUNK * c + j
                        at = (h % (HEADS // 2)) * (HEAD + 1)
                        mm = pe.matmul(ps[:, h // (HEADS // 2), at:at + HEAD + 1], scores[n % 2][:, j, :],
                                       v_ext[:, t, h, :], start=True, stop=True)
                    mm.then_inc(s["heads_ps"], 1)
                    if n + 2 < STEPS:
                        score(n + 2)
                if not last:
                    pe.wait_ge(s["gate_done"], i + 1)
                    pointwise(i + 1)
                pe.wait_ge(s["norm_done"], i + 1)
                for c in range(DC):
                    for t in range(CT):
                        mm = pe.transpose(wide(ps_c)[:, c, t * P:(t + 1) * P], attn[:, t, c * P:(c + 1) * P], ident[:])
                mm.then_inc(s["attnT_ps"], 1)
                pe.wait_ge(s["a_lo_done"], i + 1)
                project(WO, ps_d, turn_hi, turn_lo, s["wo_ps"])
                pe.wait_ge(s["mix_step"], 2 * i + 2)
                for t in range(CT):
                    for c in range(DC):
                        mm = pe.transpose(ps_a[:, t, c * P:(c + 1) * P], k[:, c, t * P:(t + 1) * P], ident[:])
                mm.then_inc(s["x2_ps"], 1)

            chunks(pe, step)

        @block.scalar
        def _(act):
            copy = ACT.Copy
            for n in range(6):
                act.wait_ge(stage_in[n % 2], 16 * (n // 2 + 1))
                act.activation(weight(n)[0], stage[n % 2], copy).then_inc(s["stage_hi"], 1)
            act.wait_ge(s["eps_set"], 1)
            act.wait_ge(s["aggr_done"], TILES)
            act.activation(rstd[:], mean_var[:, :, 1], ACT.Sqrt, bias=eps[:]).then_inc(s["std_done"], 1)
            act.wait_ge(s["half_done"], 1)

            def front(i, par):
                act.wait_ge(s["xnT_ps"], i + 1)
                act.activation(xc[par][:], wide(ps_a), copy).then_inc(s["xT_done"], 1)
                act.wait_ge(s["conv_step"], 3 * i + 3)
                act.activation(turn_hi[:], part[:], copy).then_inc(s["y_hi_done"], 1)
                act.wait_ge(s["xc_done"], i + 1)
                act.activation(xc_hi[:], xc[par][:], copy).then_inc(s["xc_hi_done"], 1)

            def negative_exp(buf, src, ready, steps, i):
                act.wait_ge(ready, i + 1)
                act.activation(buf[:], src[:], ACT.Relu, scale=-1.0).then_inc(steps, 1)
                act.wait_ge(steps, 2 * i + 1)
                act.activation(buf[:], buf[:], ACT.Exp, scale=-1.0).then_inc(steps, 1)

            front(0, 0)

            def step(i, par, first, last):
                act.wait_ge(s["delta_done"], i + 1)
                act.activation(turn_hi[:], part[:], copy).then_inc(s["d_hi_done"], 1)
                act.wait_ge(s["q_ps"], i + 1)
                act.activation(q[:], wide(ps_b), copy).then_inc(s["q_raw"], 1)
                act.wait_ge(s["k_ps"], i + 1)
                act.activation(k[:], wide(ps_c), copy).then_inc(s["k_raw"], 1)
                act.wait_ge(s["v_ps"], i + 1)
                if first:
                    act.wait_ge(s["ones_set"], 1)
                for t in range(CT):
                    a = act.activation(v_ext[:, t, :, 0:HEAD], ps_d[:, t, :].rearrange("p (h m) -> p h m", h=HEADS), copy)
                a.then_inc(s["v_done"], 1)
                negative_exp(exq, q, s["rope_q"], s["exq_step"], i)
                negative_exp(swap, k, s["rope_k"], s["exk_step"], i)
                act.wait_ge(s["gate_ps"], i + 1)
                for c in range(DC):
                    a = act.activation(gate[:, c, :], wide(ps_b)[:, c, :], ACT.Tanh, bias=half_b_gate[:, c:c + 1], scale=0.5)
                a.then_inc(s["gate_done"], 1)
                if not last:
                    front(i + 1, 1 - par)
                act.wait_ge(s["attnT_ps"], i + 1)
                act.activation(q[:], wide(ps_c), copy).then_inc(s["attnT_done"], 1)
                act.wait_ge(s["attnT_done"], i + 1)
                act.activation(turn_hi[:], q[:], copy).then_inc(s["a_hi_done"], 1)
                act.wait_ge(s["x2_ps"], i + 1)
                if last:
                    act.wait_ge(s["x2_out"], 16 * i)
                act.activation(xn[:], ps_a[:], copy).then_inc(s["x2_done"], 1)

            chunks(act, step)

        @block.vector
        def _(dve):
            dve.memset(eps[:], EPS).then_inc(s["eps_set"], 1)
            for t in range(TILES):
                if t:
                    dve.wait_ge(s["aggr_done"], t)
                dve.bn_stats(stats[:], x[:, t, :]).then_inc(s["stats_done"], 1)
                dve.wait_ge(s["stats_done"], t + 1)
                dve.bn_aggr(mean_var[:, t, :], stats[:]).then_inc(s["aggr_done"], 1)
            dve.wait_ge(s["small_in"], 16 * 5)
            dve.tensor_scalar(half_b_gate[:], b_gate[:], 0.5, None, ALU.mult).then_inc(s["half_done"], 1)

            def lo(out, raw, hi, ready, count, done):
                dve.wait_ge(ready, count)
                dve.tensor_tensor(out[:], raw[:], hi[:].bitcast(F32), ALU.subtract).then_inc(done, 1)

            for n in range(6):
                w_hi, w_lo = weight(n)
                dve.wait_ge(s["stage_hi"], n + 1)
                dve.tensor_tensor(w_lo, stage[n % 2], w_hi.bitcast(F32), ALU.subtract).then_inc(s["stage_lo"], 1)
            dve.wait_ge(s["std_done"], 1)
            dve.reciprocal(rstd[:], rstd[:]).then_inc(s["rstd_done"], 1)
            dve.wait_ge(s["rstd_done"], 1)

            def by_seq(buf, c):
                return buf[:, c, :].rearrange("p (q s) -> p q s", s=SEQ)

            def all_seq(buf):
                return buf[:].rearrange("p c n -> p (c n)").rearrange("p (q s) -> p q s", s=SEQ)

            def front(i, par, first):
                if not first:
                    dve.wait_ge(s["x2_out"], 16 * (i - 1))
                for t in range(CT):
                    tile = CT * i + t
                    a = dve.tensor_scalar(xn[:, t:t + 1, :], x[:, bass.ds(tile, 1), :], mean_var[:, bass.ds(tile, 1), 0],
                                          rstd[:, bass.ds(tile, 1)], ALU.subtract, ALU.mult)
                a.then_inc(s["xn_done"], 1)
                dve.wait_ge(s["xT_done"], i + 1)
                for tap in range(3):
                    if tap:
                        dve.wait_ge(s["conv_step"], 3 * i + tap)
                    for c in range(DC):
                        y, z = by_seq(part, c), by_seq(xc[par], c)
                        w = w_dw[:, c, 2 - tap:3 - tap]
                        if tap == 0:
                            a = dve.tensor_scalar(y, z, w, None, ALU.mult)
                        else:
                            a = dve.scalar_tensor_tensor(y[:, :, tap:], z[:, :, :SEQ - tap], w, y[:, :, tap:], ALU.mult, ALU.add)
                    a.then_inc(s["conv_step"], 1)
                lo(turn_lo, part, turn_hi, s["y_hi_done"], i + 1, s["y_lo_done"])

            def residual(i, par):
                dve.wait_ge(s["pw_ps"], i + 1)
                dve.tensor_tensor(xc[par][:], wide(ps_b), xc[par][:], ALU.add).then_inc(s["xc_done"], 1)
                lo(xc_lo, xc[par], xc_hi, s["xc_hi_done"], i + 1, s["xc_lo_done"])

            front(0, 0, True)
            residual(0, 0)

            def step(i, par, first, last):
                d, z = all_seq(part), all_seq(xc[par])
                dve.memset(d[:, :, 0:1], 0.0)
                dve.tensor_tensor(d[:, :, 1:], z[:, :, 1:], z[:, :, :SEQ - 1], ALU.subtract).then_inc(s["delta_done"], 1)
                lo(turn_lo, part, turn_hi, s["d_hi_done"], i + 1, s["d_lo_done"])
                for n, (z, raw, done) in enumerate(((q, "q_raw", "rope_q"), (k, "k_raw", "rope_k"))):
                    base = 4 * i + 2 * n
                    dve.wait_ge(s[raw], i + 1)
                    if n:
                        dve.wait_ge(s["rope_q"], i + 1)
                    turn = [t[:].unsqueeze(1).to_broadcast([P, DC * CSEQ, SEQ]) for t in (cos, sin)]
                    dve.tensor_tensor(all_seq(gate), all_seq(z), turn[0], ALU.mult)
                    dve.stream_shuffle(swap[:], z[:], [a ^ 1 for a in range(32)]).then_inc(s["rope_step"], 1)
                    dve.wait_ge(s["rope_step"], base + 1)
                    dve.tensor_tensor(all_seq(swap), all_seq(swap), turn[1], ALU.mult).then_inc(s["rope_step"], 1)
                    dve.wait_ge(s["rope_step"], base + 2)
                    dve.tensor_tensor(z[:], gate[:], swap[:], ALU.add).then_inc(s[done], 1)
                dve.wait_ge(s["exq_step"], 2 * i + 2)
                if first:
                    dve.wait_ge(s["heads_zero"], 1)
                for j in range(HEADS_PER_CHUNK):
                    rows = slice(j * HEAD, (j + 1) * HEAD)
                    a = dve.scalar_tensor_tensor(
                        heads[rows, :, :, j, :].rearrange("p c t n -> p (c t) n"),
                        q[rows].rearrange("p c (t n) -> p (c t) n", n=P), 0.0,
                        exq[rows].rearrange("p c (t n) -> p (c t) n", n=P), ALU.max, ALU.add)
                a.then_inc(s["phi_q"], 1)
                dve.wait_ge(s["exk_step"], 2 * i + 2)
                dve.scalar_tensor_tensor(k[:], k[:], 0.0, swap[:], ALU.max, ALU.add).then_inc(s["phi_k"], 1)
                if not last:
                    front(i + 1, 1 - par, first)
                for n in range(STEPS):
                    dve.wait_ge(s["scores_ps"], STEPS * i + n + 1)
                    if n >= 2:
                        dve.wait_ge(s["heads_ps"], STEPS * i + n - 1)
                    dve.tensor_tensor(scores[n % 2][:], ps_c[:, n % 2, :].rearrange("p (j n) -> p j n", n=P),
                                      causal[:].unsqueeze(1).to_broadcast([P, HEADS_PER_CHUNK, P]), ALU.mult).then_inc(s["masked"], 1)
                for t in range(CT):
                    dve.wait_ge(s["heads_ps"], STEPS * i + DC * (t + 1))
                    ext = (ps_d, ps_a)[t][:, :, 0:HEADS // 2 * (HEAD + 1)].rearrange("p a (h m) -> p a h m", m=HEAD + 1)
                    by_half = "p (a h) -> p a h"
                    dve.tensor_scalar(den[:].rearrange(by_half, a=2), ext[:, :, :, HEAD], DEN_EPS, None, ALU.add).then_inc(s["den_done"], 1)
                    dve.wait_ge(s["den_done"], 2 * CT * i + 2 * t + 1)
                    dve.reciprocal(den_rec[:], den[:]).then_inc(s["den_done"], 1)
                    dve.wait_ge(s["den_done"], 2 * CT * i + 2 * t + 2)
                    for half in range(2):
                        hs = slice(half * HEADS // 2, (half + 1) * HEADS // 2)
                        a = dve.tensor_tensor(attn[:, t, half * D // 2:(half + 1) * D // 2].rearrange("p (h m) -> p h m", m=HEAD),
                                              ext[:, half, :, 0:HEAD], den_rec[:, hs].unsqueeze(2).to_broadcast([P, HEADS // 2, HEAD]), ALU.mult)
                a.then_inc(s["norm_done"], 1)
                if not last:
                    residual(i + 1, 1 - par)
                lo(turn_lo, q, turn_hi, s["a_hi_done"], i + 1, s["a_lo_done"])
                dve.wait_ge(s["wo_ps"], i + 1)
                dve.wait_ge(s["gate_done"], i + 1)
                dve.scalar_tensor_tensor(gate[:], gate[:], 1.0, wide(ps_d), ALU.add, ALU.mult).then_inc(s["mix_step"], 1)
                dve.wait_ge(s["mix_step"], 2 * i + 1)
                dve.scalar_tensor_tensor(k[:], gate[:], 0.5, xc[par][:], ALU.mult, ALU.add).then_inc(s["mix_step"], 1)
                dve.wait_ge(s["x2_done"], i + 1)
                for t in range(CT):
                    dve.bn_stats(x2_stats[:, t, :], xn[:, t, :]).then_inc(s["x2_stats"], 1)
                tiles = bass.ds(CT * i, CT)
                dve.wait_ge(s["x2_stats"], 2 * CT * i + CT)
                dve.tensor_tensor(x[:, tiles, :], xn[:], x[:, tiles, :], ALU.add).then_inc(s["x_done"], 1)
                for t in range(CT):
                    dve.bn_aggr(x2_mv[:, t, :], x2_stats[:, t, :]).then_inc(s["x2_stats"], 1)
                dve.wait_ge(s["x2_stats"], 2 * CT * (i + 1))
                dve.tensor_copy(keep["mean_var"][:, tiles, :], x2_mv[:])

            chunks(dve, step)
            dve.wait_ge(s["x_done"], CHUNKS)


def feed_forwards(nc, dram, keep, out, experts_only=False):
    with ExitStack() as stack:
        fr = Frame(nc, stack, "ff_")
        x, ident, mean_var = keep["x"], keep["ident"], keep["mean_var"]
        h_hi, h_lo = keep["r_hi"], keep["r_lo"]
        up_hi = [fr.sbuf(f"up_hi{i}", [P, DC, SUB], F32R) for i in range(2)]
        up_lo = [fr.sbuf(f"up_lo{i}", [P, DC, SUB], F32R) for i in range(2)]
        down_hi = [fr.sbuf(f"down_hi{i}", [P, FC, D], F32R) for i in range(2)]
        down_lo = [fr.sbuf(f"down_lo{i}", [P, FC, D], F32R) for i in range(2)]
        up_raw = fr.sbuf("up_raw", [P, DC, SUB])
        down_raw = fr.sbuf("down_raw", [P, FC, D])
        hid = fr.sbuf("hid", [P, FC, GROUP])
        hid_hi = fr.sbuf("hid_hi", [P, FC, GROUP], F32R)
        hid_lo = fr.sbuf("hid_lo", [P, FC, GROUP], F32R)
        up_bias = fr.sbuf("up_bias", [P, SUBS * FC])
        down_bias = fr.sbuf("down_bias", [P, D])
        ln_g = fr.sbuf("ln_g", [P, DC])
        ln_b = fr.sbuf("ln_b", [P, DC])
        w_moe = fr.sbuf("w_moe", [P, DC, EXPERTS])
        w_router = fr.sbuf("w_router", [P, DC, BLOCKS])
        b_router = fr.sbuf("b_router", [P, BLOCKS])
        rstd = fr.sbuf("rstd", [P, TILES])
        stats = fr.sbuf("stats", [P, 6])
        eps = fr.sbuf("eps", [P, 1])
        share = fr.sbuf("share", [P, TILES, EXPERTS])
        share_by = fr.sbuf("share_by", [P, EXPERTS, TILES])
        soft = fr.sbuf("soft", [P, 2, TILES])
        shut_in = fr.sbuf("shut_in", [P, GROUPS, BLOCKS])
        shut = fr.sbuf("shut", [P, GROUPS * BLOCKS], BF16)
        left_outT = fr.sbuf("left_outT", [P, GROUP], BF16)
        block_no = fr.sbuf("block_no", [P, BLOCKS])
        prob = fr.sbuf("prob", [P, TILES, BLOCKS])
        best = fr.sbuf("best", [P, 8])
        best_at = fr.sbuf("best_at", [P, TILES, 8], U32)
        left_out = prob
        xn = hid[:, 0:2, :]
        h_raw = hid[:, 2:4, :].rearrange("p r (c n) -> p r c n", c=DC)

        ps_up = [fr.psum(f"ps_up{f}") for f in range(FC)]
        ps_down = [fr.psum(f"ps_down{t}") for t in range(TILES_PER_GROUP)]

        names = ("small_in w_in w_hi_done w_split b2_in b2_used xn_done xT_ps h_raw_done h_hi_done h_lo_done logit_ps "
                 "logit_done soft_step exp_done share_done up_done hid_hi_done hid_done down_done acc_done eps_set "
                 "std_done rstd_done stats_done aggr_done top_done out_left left_ps leftT_done leftT_zero x_out").split()
        s = {n: fr.sem(n) for n in names}
        x_in = [fr.sem(f"x_in{i}") for i in range(4)]
        block = stack.enter_context(nc.Block())
        last_sub = MOE_SUBS if experts_only else SUBS
        SMALL = 9

        def weights_in(sp, sub):
            sp.dma_start(up_raw[:], dram["up_w"][bass.ds(sub, 1)].rearrange("o p c f -> p (o c) f")).then_inc(s["w_in"], 16)
            sp.dma_start(down_raw[:], dram["down_w"][bass.ds(sub, 1)].rearrange("o p c d -> p (o c) d")).then_inc(s["w_in"], 16)

        @block.sync
        def _(sp):
            for t in range(4):
                sp.dma_start(up_raw[:, t, :], dram["x2"][t]).then_inc(x_in[t], 16)
            for t, name in ((up_bias, "up_bias"), (ln_g, "ln_g"), (ln_b, "ln_b"), (w_moe, "w_moe"), (w_router, "w_router"),
                            (shut_in, "shut"), (block_no, "block_no")):
                sp.dma_start(t[:], dram[name]).then_inc(s["small_in"], 16)
            sp.dma_start(b_router[:], dram["b_router"].partition_broadcast(P)).then_inc(s["small_in"], 16)
            sp.dma_start(down_bias[:], dram["down_bias"][0].partition_broadcast(P)).then_inc(s["small_in"], 16)
            with sp.Fori(0, GROUPS - 1) as g:
                for t in range(TILES_PER_GROUP):
                    sp.wait_ge(s["xn_done"], TILES_PER_GROUP * g + t + 1)
                    sp.dma_start(up_raw[:, t, :], dram["x2"][bass.ds(TILES_PER_GROUP * g + t + TILES_PER_GROUP, 1)].rearrange("o p d -> p (o d)")).then_inc(x_in[t], 16)
            sp.wait_ge(s["xn_done"], TILES)
            weights_in(sp, 0)
            sp.wait_ge(s["w_split"], DC)
            weights_in(sp, 1)
            with sp.Fori(0, EXPERTS) as e:
                for j in range(SUBS_PER_EXPERT):
                    sub = SUBS_PER_EXPERT * e + j
                    sp.wait_ge(s["w_split"], DC * sub + 2 * DC)
                    weights_in(sp, sub + 2)
                    if j == 1:
                        sp.wait_ge(s["b2_used"], TILES * e + TILES)
                        sp.dma_start(down_bias[:], dram["down_bias"][bass.ds(e + 1, 1)].rearrange("o d -> (o d)").partition_broadcast(P)).then_inc(s["b2_in"], 16)
            if not experts_only:
                for sub in range(MOE_SUBS, SUBS - 2):
                    sp.wait_ge(s["w_split"], DC * sub + 2 * DC)
                    weights_in(sp, sub + 2)
            sp.wait_ge(s["acc_done"], TILES * last_sub)
            sp.dma_start(out.rearrange("(t p) d -> p t d", p=P), x[:]).then_inc(s["x_out"], 16)
            sp.wait_ge(s["x_out"], 16)

        @block.gpsimd
        def _(pool):
            nc.gpsimd.memset(left_outT[:], 0.0).then_inc(s["leftT_zero"], 1)

        def sub_loops(eng, group):
            with eng.Fori(0, EXPERTS) as e:
                for j in range(SUBS_PER_EXPERT):
                    with eng.Fori(0, GROUPS) as g:
                        group(SUBS_PER_EXPERT * e + j, j, g, e)

        def ffn_loops(eng, group):
            for j in range(FFN_SUBS):
                with eng.Fori(0, GROUPS) as g:
                    group(MOE_SUBS + j, j, g, None)

        @block.tensor
        def _(pe):
            pe.wait_ge(s["small_in"], 16 * SMALL)

            def lead(n, logits, w):
                with pe.Fori(0, GROUPS) as g:
                    for t in range(TILES_PER_GROUP):
                        i = TILES * n + TILES_PER_GROUP * g + t
                        pe.wait_ge(s["xn_done"], i + 1)
                        for c in range(DC):
                            mm = pe.transpose(ps_up[t][:, c * P:(c + 1) * P], xn[:, t % 2, c * P:(c + 1) * P], ident[:])
                        mm.then_inc(s["xT_ps"], 1)
                        pe.wait_ge(s["h_raw_done"], i + 1)
                        for c in range(DC):
                            mm = pe.matmul(ps_down[t][:, 0:logits], h_raw[:, t % 2, c, :], w[:, c, :], start=c == 0, stop=c == DC - 1)
                        mm.then_inc(s["logit_ps"], 1)

            def group(sub, j, g, e):
                par = j % 2
                n = GROUPS * sub + g
                pe.wait_ge(s["w_split"], DC * sub + DC)

                def up(f):
                    cols = slice(f * P, (f + 1) * P)
                    if e is None:
                        pe.matmul(ps_up[f][:], shut[:, bass.ds(BLOCKS * g + FC * j + f, 1)].to_broadcast([P, P]),
                                  left_outT[:], start=True, stop=False)
                    for c in range(DC):
                        at = bass.ds(DC * g + c, 1)
                        mm = three_products(pe, ps_up[f][:], up_hi[par][:, c, cols], up_lo[par][:, c, cols],
                                            h_hi[:, at, :].rearrange("p o n -> p (o n)"), h_lo[:, at, :].rearrange("p o n -> p (o n)"),
                                            c == 0 and e is not None, c == DC - 1)
                    mm.then_inc(s["up_done"], 1)

                def down(f):
                    pe.wait_ge(s["hid_done"], FC * n + f + 1)
                    for t in range(TILES_PER_GROUP):
                        toks = slice(t * P, (t + 1) * P)
                        mm = three_products(pe, ps_down[t][:], hid_hi[:, f, toks], hid_lo[:, f, toks],
                                            down_hi[par][:, f, :], down_lo[par][:, f, :], f == 0, f == FC - 1)
                        if f == FC - 1:
                            mm.then_inc(s["down_done"], 1)

                up(0)
                up(1)
                up(2)
                down(0)
                up(3)
                down(1)
                down(2)
                down(3)

            lead(0, EXPERTS, w_moe)
            pe.wait_ge(s["h_lo_done"], TILES)
            pe.wait_ge(s["share_done"], 1)
            sub_loops(pe, group)
            if experts_only:
                return
            lead(1, BLOCKS, w_router)
            pe.wait_ge(s["out_left"], 1)
            for t in range(TILES):
                g, u = divmod(t, TILES_PER_GROUP)
                mm = pe.transpose(ps_up[g][0:BLOCKS, u * P:(u + 1) * P], left_out[:, t, :], ident[:])
            mm.then_inc(s["left_ps"], 1)
            pe.wait_ge(s["leftT_done"], 1)
            pe.wait_ge(s["h_lo_done"], 2 * TILES)
            ffn_loops(pe, group)

        @block.scalar
        def _(act):
            copy = ACT.Copy

            def split_weights(sub, c, par):
                at = bass.ds(c, 1)
                act.wait_ge(s["w_in"], 32 * sub + 32)
                act.activation(up_hi[par][:, at, :], up_raw[:, at, :], copy)
                act.activation(down_hi[par][:, at, :], down_raw[:, at, :], copy).then_inc(s["w_hi_done"], 1)

            def lead(n):
                act.wait_ge(s["eps_set"], 1)
                if n:
                    act.wait_ge(s["aggr_done"], TILES)
                act.activation(rstd[:], mean_var[:, :, 1], ACT.Sqrt, bias=eps[:]).then_inc(s["std_done"], 1)
                with act.Fori(0, GROUPS) as g:
                    for t in range(TILES_PER_GROUP):
                        i = TILES * n + TILES_PER_GROUP * g + t
                        act.wait_ge(s["xT_ps"], i + 1)
                        if t >= 2:
                            act.wait_ge(s["h_lo_done"], i - 1)
                            act.wait_ge(s["logit_ps"], i - 1)
                        if n == 0:
                            for c in range(DC):
                                a = act.activation(h_raw[:, t % 2, c, :], ps_up[t][:, c * P:(c + 1) * P], ACT.Identity,
                                                   bias=ln_b[:, c:c + 1], scale=ln_g[:, c:c + 1])
                        else:
                            a = act.activation(h_raw[:, t % 2], ps_up[t][:].rearrange("p (c n) -> p c n", c=DC), copy)
                        a.then_inc(s["h_raw_done"], 1)
                        act.wait_ge(s["h_raw_done"], i + 1)
                        act.activation(h_hi[:, bass.ds(DC * g, DC), t * P:(t + 1) * P], h_raw[:, t % 2], copy).then_inc(s["h_hi_done"], 1)

            def group(sub, j, g, e):
                n = GROUPS * sub + g
                for f in range(FC):
                    act.wait_ge(s["up_done"], FC * n + f + 1)
                    func = ACT.Relu if e is None else ACT.Silu
                    bias = up_bias[:, bass.ds(FC * sub + f, 1)]
                    act.activation(hid[:, f, :], ps_up[f][:], func, bias=bias)
                    act.activation(hid_hi[:, f, :], ps_up[f][:], func, bias=bias).then_inc(s["hid_hi_done"], 1)
                    if f == 1 and not (sub_is_last(sub)):
                        split_weights(sub + 1, g, 1 - j % 2)

            def sub_is_last(sub):
                return isinstance(sub, int) and sub == SUBS - 1

            act.wait_ge(s["small_in"], 16 * SMALL)
            act.activation(shut[:], shut_in[:].rearrange("p g b -> p (g b)"), copy)
            lead(0)
            act.wait_ge(s["soft_step"], 2)
            act.activation(share[:], share[:], ACT.Exp).then_inc(s["exp_done"], 1)
            for c in range(DC):
                split_weights(0, c, 0)
            sub_loops(act, group)
            if experts_only:
                return
            lead(1)
            act.wait_ge(s["soft_step"], 6)
            act.activation(prob[:], prob[:], ACT.Exp).then_inc(s["exp_done"], 1)
            act.wait_ge(s["leftT_zero"], 1)
            act.wait_ge(s["left_ps"], 1)
            for g in range(GROUPS):
                a = act.activation(left_outT[SEQ * g:SEQ * g + BLOCKS, :], ps_up[g][0:BLOCKS, :], copy)
            a.then_inc(s["leftT_done"], 1)
            ffn_loops(act, group)

        @block.vector
        def _(dve):
            dve.memset(eps[:], EPS).then_inc(s["eps_set"], 1)
            dve.wait_ge(s["small_in"], 16 * SMALL)

            def split_weights(sub, c, par):
                at = bass.ds(c, 1)
                dve.wait_ge(s["w_hi_done"], DC * sub + c + 1)
                dve.tensor_tensor(up_lo[par][:, at, :], up_raw[:, at, :], up_hi[par][:, at, :].bitcast(F32), ALU.subtract)
                dve.tensor_tensor(down_lo[par][:, at, :], down_raw[:, at, :], down_hi[par][:, at, :].bitcast(F32), ALU.subtract).then_inc(s["w_split"], 1)

            def lead(n, logits, to, bias):
                if n:
                    for t in range(TILES):
                        dve.wait_ge(s["acc_done"], TILES * MOE_SUBS)
                        if t:
                            dve.wait_ge(s["aggr_done"], t)
                        dve.bn_stats(stats[:], x[:, t, :]).then_inc(s["stats_done"], 1)
                        dve.wait_ge(s["stats_done"], t + 1)
                        dve.bn_aggr(mean_var[:, t, :], stats[:]).then_inc(s["aggr_done"], 1)
                dve.wait_ge(s["std_done"], n + 1)
                dve.reciprocal(rstd[:], rstd[:]).then_inc(s["rstd_done"], 1)
                dve.wait_ge(s["rstd_done"], n + 1)
                with dve.Fori(0, GROUPS) as g:
                    for t in range(TILES_PER_GROUP):
                        tile = TILES_PER_GROUP * g + t
                        i = TILES * n + tile
                        at = bass.ds(tile, 1)
                        if n == 0:
                            dve.wait_ge(x_in[t], 16 * g + 16)
                            src = up_raw[:, t:t + 1, :]
                        else:
                            src = x[:, at, :]
                        dve.tensor_scalar(xn[:, t % 2:t % 2 + 1, :], src, mean_var[:, at, 0], rstd[:, at], ALU.subtract, ALU.mult).then_inc(s["xn_done"], 1)
                        dve.wait_ge(s["h_hi_done"], i + 1)
                        rows = (slice(None), bass.ds(DC * g, DC), slice(t * P, (t + 1) * P))
                        dve.tensor_tensor(h_lo[rows], h_raw[:, t % 2], h_hi[rows].bitcast(F32), ALU.subtract).then_inc(s["h_lo_done"], 1)
                        dve.wait_ge(s["logit_ps"], i + 1)
                        if bias is None:
                            dve.tensor_copy(to[:, at, :], ps_down[t][:, 0:logits].unsqueeze(1)).then_inc(s["logit_done"], 1)
                        else:
                            dve.tensor_tensor(to[:, at, :], ps_down[t][:, 0:logits].unsqueeze(1), bias[:].unsqueeze(1), ALU.add).then_inc(s["logit_done"], 1)

            def softmax(n, z, width):
                step = 4 * n
                dve.wait_ge(s["logit_done"], TILES * (n + 1))
                dve.tensor_reduce(soft[:, 0, :], z[:], AX.X, ALU.max).then_inc(s["soft_step"], 1)
                dve.wait_ge(s["soft_step"], step + 1)
                dve.tensor_tensor(z[:], z[:], soft[:, 0, :].unsqueeze(2).to_broadcast([P, TILES, width]), ALU.subtract).then_inc(s["soft_step"], 1)
                dve.wait_ge(s["exp_done"], n + 1)
                dve.tensor_reduce(soft[:, 1, :], z[:], AX.X, ALU.add).then_inc(s["soft_step"], 1)
                dve.wait_ge(s["soft_step"], step + 3)
                dve.reciprocal(soft[:, 1, :], soft[:, 1, :]).then_inc(s["soft_step"], 1)
                dve.wait_ge(s["soft_step"], step + 4)
                return soft[:, 1, :].unsqueeze(2).to_broadcast([P, TILES, width])

            def group(sub, j, g, e):
                n = GROUPS * sub + g
                for f in range(FC):
                    dve.wait_ge(s["hid_hi_done"], FC * n + f + 1)
                    dve.tensor_tensor(hid_lo[:, f, :], hid[:, f, :], hid_hi[:, f, :].bitcast(F32), ALU.subtract).then_inc(s["hid_done"], 1)
                    if f == 1 and not (isinstance(sub, int) and sub == SUBS - 1):
                        split_weights(sub + 1, g, 1 - j % 2)
                for t in range(TILES_PER_GROUP):
                    tile = TILES_PER_GROUP * g + t
                    row = x[:, bass.ds(tile, 1), :]
                    if j == 0:
                        if e is None:
                            dve.wait_ge(s["b2_in"], 16 * EXPERTS)
                            dve.tensor_tensor(row, down_bias[:].unsqueeze(1), row, ALU.add).then_inc(s["b2_used"], 1)
                            dve.wait_ge(s["b2_used"], TILES * EXPERTS + tile + 1)
                        else:
                            dve.scalar_tensor_tensor(row, down_bias[:].unsqueeze(1), share_by[:, bass.ds(e, 1), bass.ds(tile, 1)].rearrange("p a b -> p (a b)"), row, ALU.mult, ALU.add).then_inc(s["b2_used"], 1)
                            dve.wait_ge(s["b2_used"], TILES * e + tile + 1)
                    dve.wait_ge(s["down_done"], TILES_PER_GROUP * n + t + 1)
                    ps = ps_down[t][:].unsqueeze(1)
                    if e is None:
                        a = dve.tensor_tensor(row, ps, row, ALU.add)
                    else:
                        a = dve.scalar_tensor_tensor(row, ps, share_by[:, bass.ds(e, 1), bass.ds(tile, 1)].rearrange("p a b -> p (a b)"), row, ALU.mult, ALU.add)
                    a.then_inc(s["acc_done"], 1)

            lead(0, EXPERTS, share, None)
            rec = softmax(0, share, EXPERTS)
            dve.tensor_tensor(share_by[:].rearrange("p e t -> p t e"), share[:], rec, ALU.mult).then_inc(s["share_done"], 1)
            for c in range(DC):
                split_weights(0, c, 0)
            dve.wait_ge(s["share_done"], 1)
            sub_loops(dve, group)
            if experts_only:
                return
            lead(1, BLOCKS, prob, b_router)
            rec = softmax(1, prob, BLOCKS)
            dve.tensor_tensor(prob[:], prob[:], rec, ALU.mult).then_inc(s["top_done"], 1)
            dve.wait_ge(s["top_done"], 1)
            for t in range(TILES):
                dve.max(best[:], prob[:, t, :]).then_inc(s["top_done"], 1)
                dve.wait_ge(s["top_done"], 2 * t + 2)
                dve.max_index(best_at[:, t, :], best[:], prob[:, t, :]).then_inc(s["top_done"], 1)
                dve.wait_ge(s["top_done"], 2 * t + 3)
            done = 2 * TILES + 1
            spot = hid[:, 0, 0:TILES * 8].rearrange("p (t k) -> p t k", k=8)
            chosen = hid[:, 1:3, :].rearrange("p a n -> p (a n)").rearrange("p (t j k) -> p t j k", t=TILES, j=BLOCKS)
            dve.tensor_copy(spot, best_at[:]).then_inc(s["top_done"], 1)
            dve.wait_ge(s["top_done"], done + 1)
            for k in range(TOP_K):
                a = dve.tensor_tensor(chosen[:, :, :, k], spot[:, :, k:k + 1].to_broadcast([P, TILES, BLOCKS]),
                                      block_no[:].unsqueeze(1).to_broadcast([P, TILES, BLOCKS]), ALU.is_equal)
            a.then_inc(s["top_done"], 1)
            dve.wait_ge(s["top_done"], done + 2)
            dve.tensor_reduce(left_out[:], chosen, AX.X, ALU.add).then_inc(s["top_done"], 1)
            dve.wait_ge(s["top_done"], done + 3)
            dve.tensor_scalar(left_out[:], left_out[:], -1.0, 1.0, ALU.mult, ALU.add).then_inc(s["out_left"], 1)
            ffn_loops(dve, group)


def build(nc, dram, out, phases=4):
    with ExitStack() as stack:
        fr = Frame(nc, stack)
        dram = {**dram, "x2": nc.dram_tensor("x2_scratch", [TILES, P, D], F32, kind="Internal").ap()}
        keep = {
            "x": fr.sbuf("x_res", [P, TILES, D]),
            "r_hi": fr.sbuf("r_hi", [P, FEAT_CHUNKS, D], F32R),
            "r_lo": fr.sbuf("r_lo", [P, FEAT_CHUNKS, D], F32R),
            "mean_var": fr.sbuf("x2_mean_var", [P, TILES, 2]),
            "ident": fr.sbuf("identity", [P, P]),
        }
        cross_attention(nc, dram, keep)
        if phases == 1:
            dump(nc, keep["x"], out)
            return
        linear_attention(nc, dram, keep)
        if phases == 2:
            dump(nc, keep["x"], out)
            return
        feed_forwards(nc, dram, keep, out, phases == 3)


def dump(nc, x, out):
    with nc.semaphore("dump") as s, nc.Block() as block:
        @block.sync
        def _(sp):
            sp.dma_start(out.rearrange("(t p) d -> p t d", p=P), x[:]).then_inc(s, 16)
            sp.wait_ge(s, 16)


def layouts(v):
    c = np.ascontiguousarray
    ctx = v["ctx_1024"]
    tiles = ctx.reshape(TILES, PER_TILE, CTX, D)
    full = CTX_CHUNKS * P
    a = {
        "x": c(v["x"].reshape(TOKENS, D)),
        "ctxT": c(tiles.reshape(TILES, PER_TILE, CTX, DC, P).transpose(0, 4, 3, 1, 2)),
        "ctxN": c(tiles[:, :, :full].reshape(TILES, PER_TILE, CTX_CHUNKS, P, D).transpose(0, 3, 1, 2, 4)),
        "ctxR": c(tiles[:, :, full]),
        "w_sim": c(v["L0_xattn_w_sim"].reshape(3, DC, P).transpose(2, 0, 1)),
        "b_sim": c(v["L0_xattn_b_sim"]),
        "W_qv": c(v["L0_xattn_W_qv"]),
        "b_qv": c(v["L0_xattn_b_qv"]),
        "ident": np.eye(P, dtype=np.float32),
        "seq_of": np.repeat(np.eye(PER_TILE, dtype=np.float32), SEQ, axis=0),
    }
    pos = np.arange(SEQ, dtype=np.float32)
    inv_freq = np.float32(1.0) / np.float32(10000.0) ** (np.arange(0, HEAD, 2, dtype=np.float32) / np.float32(HEAD))
    theta = pos[:, None] * inv_freq[None, :].astype(np.float32)
    pair = np.arange(P) % HEAD // 2
    sign = np.where(np.arange(P) % 2 == 0, -1.0, 1.0).astype(np.float32)
    at = np.arange(P)
    qkv = v["L0_attn_w_qkv"].reshape(3, D, D)
    a |= {
        "attn_w": c(np.stack([v["L0_attn_w_pw"], qkv[0], qkv[1], qkv[2], v["L0_attn_w_gate"], v["L0_attn_w_o"]]).transpose(0, 2, 1)),
        "cos": c(np.cos(theta).astype(np.float32).T[pair]),
        "sin": c(np.sin(theta).astype(np.float32).T[pair] * sign[:, None]),
        "causal": ((at[:, None] // SEQ == at[None, :] // SEQ) & (at[:, None] <= at[None, :])).astype(np.float32),
        "w_dw": c(v["L0_attn_w_dw"].reshape(DC, P, 3).transpose(1, 0, 2)),
        "b_gate": c(v["L0_attn_b_gate"].reshape(DC, P).T),
    }
    moe_up = v["L0_attn_w1"].reshape(MOE_SUBS, SUB, DC, P)
    ffn_up = v["L0_ffn_w1"].reshape(FFN_SUBS, SUB, DC, P)
    moe_down = v["L0_attn_w2"].reshape(EXPERTS, D, SUBS_PER_EXPERT, FC, P).transpose(0, 2, 4, 3, 1).reshape(MOE_SUBS, P, FC, D)
    ffn_down = v["L0_ffn_w2"].reshape(D, FFN_SUBS, FC, P).transpose(1, 3, 2, 0)
    a |= {
        "up_w": c(np.concatenate([moe_up, ffn_up]).transpose(0, 3, 2, 1)),
        "down_w": c(np.concatenate([moe_down, ffn_down])),
        "up_bias": c(np.concatenate([v["L0_attn_b1"].reshape(-1), v["L0_ffn_b1"]]).reshape(SUBS * FC, P).T),
        "down_bias": c(np.concatenate([v["L0_attn_b2"], v["L0_ffn_b2"][None]])),
        "ln_g": c(v["L0_attn_ln_g"].reshape(DC, P).T),
        "ln_b": c(v["L0_attn_ln_b"].reshape(DC, P).T),
        "w_moe": c(v["L0_attn_w_moe_gate"].reshape(EXPERTS, DC, P).transpose(2, 1, 0)),
        "w_router": c(v["L0_ffn_w_router"].reshape(DC, P, BLOCKS).transpose(1, 0, 2)),
        "b_router": c(v["L0_ffn_b_router"]),
        "shut": c((np.arange(P)[:, None, None] == SEQ * np.arange(GROUPS)[:, None] + np.arange(BLOCKS)).astype(np.float32) * np.float32(SHUT)),
        "block_no": np.tile(np.arange(BLOCKS, dtype=np.float32), (P, 1)),
    }
    return a


def kernel(**inputs):
    import concourse.bacc as bacc
    from concourse.bass_utils import run_bass_kernel_spmd

    arrays = layouts({name: np.asarray(a) for name, a in inputs.items()})
    nc = bacc.Bacc("TRN2", target_bir_lowering=False, num_devices=1)
    dram = {name: nc.dram_tensor(name, a.shape, mybir.dt.from_np(a.dtype), kind="ExternalInput").ap()
            for name, a in arrays.items()}
    out = nc.dram_tensor("out", (TOKENS, D), F32, kind="ExternalOutput").ap()
    build(nc, dram, out)
    r = run_bass_kernel_spmd(nc, [arrays], core_ids=[0])
    return r.results[0]["out"].reshape(BATCH, SEQ, D)
```

```python
from contextlib import ExitStack

import concourse.bass as bass
import numpy as np
from concourse import mybir

F32 = mybir.dt.float32
F32R = mybir.dt.float32r
BF16 = mybir.dt.bfloat16
U32 = mybir.dt.uint32
ALU = mybir.AluOpType
ACT = mybir.ActivationFunctionType
AX = mybir.AxisListType

P = 128
D = 512
DC = D // P
SEQ = 32
BATCH = 64
TOKENS = BATCH * SEQ
TILES = TOKENS // P
PER_TILE = P // SEQ
CTX = 257
CTX_CHUNKS = CTX // P
GROUP = 512
GROUPS = TOKENS // GROUP
TILES_PER_GROUP = GROUP // P
FEATS = 4 * D
FEAT_CHUNKS = FEATS // P
HEADS = 16
HEAD = D // HEADS
HEADS_PER_CHUNK = P // HEAD
CHUNK = 256
CHUNKS = TOKENS // CHUNK
CT = CHUNK // P
CSEQ = CHUNK // SEQ
EXPERTS = 4
HIDDEN = 2048
SUB = 512
FC = SUB // P
SUBS_PER_EXPERT = HIDDEN // SUB
MOE_SUBS = EXPERTS * SUBS_PER_EXPERT
FFN_SUBS = HIDDEN // SUB
SUBS = MOE_SUBS + FFN_SUBS
BLOCKS = 16
TOP_K = 4
EPS = 1e-5
DEN_EPS = 1e-6
SHUT = -(2.0 ** 127)


class Frame:

    def __init__(self, nc, stack, tag=""):
        self.nc, self.stack, self.tag = nc, stack, tag

    def sbuf(self, name, shape, dt=F32):
        return self.stack.enter_context(self.nc.sbuf_tensor(self.tag + name, shape, dt))

    def psum(self, name, shape=(P, 512)):
        return self.stack.enter_context(self.nc.psum_tensor(self.tag + name, list(shape), F32))

    def sem(self, name):
        return self.stack.enter_context(self.nc.semaphore(self.tag + name))


def three_products(pe, out, w_hi, w_lo, m_hi, m_lo, first, last):
    pe.matmul(out, w_hi, m_hi, start=first, stop=False)
    pe.matmul(out, w_hi, m_lo, start=False, stop=False)
    return pe.matmul(out, w_lo, m_hi, start=False, stop=last)


def cross_attention(nc, dram, keep):
    with ExitStack() as stack:
        fr = Frame(nc, stack, "xa_")
        x, wq_hi, wq_lo = keep["x"], keep["r_hi"], keep["r_lo"]
        ident = keep["ident"]
        ctxT = [fr.sbuf(f"ctxT{i}", [P, DC, PER_TILE, CTX]) for i in range(2)]
        ctxN = [fr.sbuf(f"ctxN{i}", [P, PER_TILE, CTX_CHUNKS, D]) for i in range(2)]
        ctxR = [fr.sbuf(f"ctxR{i}", [PER_TILE, D]) for i in range(2)]
        hcT = [fr.sbuf(f"hcT{i}", [P, DC, P]) for i in range(2)]
        feats = fr.sbuf("feats", [P, FEAT_CHUNKS - DC, P])
        feats_hi = fr.sbuf("feats_hi", [P, FEAT_CHUNKS, P], F32R)
        feats_lo = fr.sbuf("feats_lo", [P, FEAT_CHUNKS, P], F32R)
        xn = [fr.sbuf(f"xn{i}", [P, D]) for i in range(2)]
        hq = fr.sbuf("hq", [P, D])
        sim_w = fr.sbuf("sim_w", [P, DC, P])
        probs = fr.sbuf("probs", [P, CTX])
        probs_rest = fr.sbuf("probs_rest", [P, PER_TILE])
        probsT = fr.sbuf("probsT", [P, CTX_CHUNKS, P])
        probsT_rest = fr.sbuf("probsT_rest", [PER_TILE, P])
        b_qv = fr.sbuf("b_qv", [P, D])
        w_sim = fr.sbuf("w_sim", [P, 3, DC])
        b_sim = fr.sbuf("b_sim", [P, 1])
        seq_of = fr.sbuf("seq_of", [P, PER_TILE])
        stats = fr.sbuf("stats", [P, 6])
        mean_var = fr.sbuf("mean_var", [P, TILES, 2])
        rstd = fr.sbuf("rstd", [P, TILES])
        neg_max = fr.sbuf("neg_max", [P, 1])
        row_sum = fr.sbuf("row_sum", [P, 1])
        row_rec = fr.sbuf("row_rec", [P, 1])
        top = fr.sbuf("top", [P, 1])
        top_wide = fr.sbuf("top_wide", [P, SEQ])
        top_seq = fr.sbuf("top_seq", [P, SEQ])
        neg_top = fr.sbuf("neg_top", [P, 1])
        top_exp = fr.sbuf("top_exp", [P, SEQ])
        own_exp = fr.sbuf("own_exp", [P, 1])
        top_sum = fr.sbuf("top_sum", [P, 1])
        top_rec = fr.sbuf("top_rec", [P, 1])
        batt = fr.sbuf("batt", [P, PER_TILE])
        bar = fr.sbuf("bar", [P, DC, PER_TILE])
        eps = fr.sbuf("eps", [P, 1])

        ps_t = fr.psum("ps_t")
        ps_sim = fr.psum("ps_sim")
        ps_p = fr.psum("ps_p")
        ps_hq = fr.psum("ps_hq")
        ps_hqt = fr.psum("ps_hqt")
        ps_m = fr.psum("ps_m")
        ps_out = [fr.psum(f"ps_out{i}") for i in range(2)]

        x_in = [fr.sem(f"x_in{g}") for g in range(GROUPS)]
        small_in = fr.sem("small_in")
        wq_in = [fr.sem(f"wq_in{q}") for q in range(4)]
        wq_hi_done = fr.sem("wq_hi_done")
        wq_split = fr.sem("wq_split")
        ctx_in = [fr.sem(f"ctx_in{i}") for i in range(2)]
        stats_done = fr.sem("stats_done")
        aggr_done = fr.sem("aggr_done")
        eps_set = fr.sem("eps_set")
        std_done = fr.sem("std_done")
        rstd_done = fr.sem("rstd_done")
        xn_done = fr.sem("xn_done")
        xnT_done = fr.sem("xnT_done")
        hcT_done = fr.sem("hcT_done")
        sim_w_done = fr.sem("sim_w_done")
        sim_done = fr.sem("sim_done")
        neg_max_done = fr.sem("neg_max_done")
        probs_done = fr.sem("probs_done")
        rest_done = fr.sem("rest_done")
        probsT_ps = fr.sem("probsT_ps")
        probsT_done = fr.sem("probsT_done")
        hq_ps = fr.sem("hq_ps")
        hq_done = fr.sem("hq_done")
        hqT_ps = fr.sem("hqT_ps")
        hqT_done = fr.sem("hqT_done")
        top_step = fr.sem("top_step")
        own_done = fr.sem("own_done")
        batt_done = fr.sem("batt_done")
        bar_ps = fr.sem("bar_ps")
        bar_done = fr.sem("bar_done")
        prod_done = fr.sem("prod_done")
        hi_done = fr.sem("hi_done")
        split_done = fr.sem("split_done")
        quarter_used = fr.sem("quarter_used")
        out_done = fr.sem("out_done")
        rec_done = fr.sem("rec_done")
        bias_done = fr.sem("bias_done")
        x_done = fr.sem("x_done")
        block = stack.enter_context(nc.Block())

        QUARTERS = 4
        halves = [ctxN[1][:].rearrange("p b c d -> p (b c d)"), ctxT[1][:].rearrange("p c b j -> p (c b j)")]
        wq_raw = [halves[q // 2][:, q % 2 * DC * D:(q % 2 + 1) * DC * D].rearrange("p (k n) -> p k n", n=D) for q in range(QUARTERS)]
        w1_at = CTX_CHUNKS * P + P

        def raw(q, par):
            return hcT[par][:] if q == 0 else feats[:, DC * (q - 1):DC * q, :]

        @block.sync
        def _(sp):
            sp.dma_start(x[:, 0:TILES_PER_GROUP, :],
                         dram["x"][0:GROUP, :].rearrange("(t p) d -> p t d", p=P)).then_inc(x_in[0], 16)
            sp.dma_start(ident[:], dram["ident"]).then_inc(small_in, 16)
            sp.dma_start(w_sim[:], dram["w_sim"]).then_inc(small_in, 16)
            sp.dma_start(b_sim[:], dram["b_sim"].partition_broadcast(P)).then_inc(small_in, 16)
            sp.dma_start(seq_of[:], dram["seq_of"]).then_inc(small_in, 16)
            sp.dma_start(b_qv[:], dram["b_qv"].partition_broadcast(P)).then_inc(small_in, 16)

            def load_ctx(t, par):
                sp.dma_start(ctxT[par][:], dram["ctxT"][bass.ds(t, 1)].rearrange("o p c b j -> p (o c) b j")).then_inc(ctx_in[par], 16)
                sp.dma_start(ctxN[par][:], dram["ctxN"][bass.ds(t, 1)].rearrange("o p b c d -> p (o b) c d")).then_inc(ctx_in[par], 16)
                sp.dma_start(ctxR[par][:], dram["ctxR"][bass.ds(t, 1)].rearrange("o b d -> (o b) d")).then_inc(ctx_in[par], 16)

            load_ctx(0, 0)
            for q in range(QUARTERS):
                sp.dma_start(wq_raw[q], dram["W_qv"][q * D:(q + 1) * D, :].rearrange("(k p) n -> p k n", p=P)).then_inc(wq_in[q], 16)
            for g in range(1, GROUPS):
                rows = slice(g * GROUP, (g + 1) * GROUP)
                sp.dma_start(x[:, g * TILES_PER_GROUP:(g + 1) * TILES_PER_GROUP, :],
                             dram["x"][rows, :].rearrange("(t p) d -> p t d", p=P)).then_inc(x_in[g], 16)
            sp.wait_ge(wq_split, QUARTERS)
            load_ctx(1, 1)
            with sp.Fori(0, TILES // 2 - 1) as pair:
                for par in range(2):
                    sp.wait_ge(hq_ps, 2 * pair + par + 1)
                    load_ctx(2 * pair + par + 2, par)

        def in_pairs(eng, tile):
            tile(0, 0, True, False)
            with eng.Fori(0, TILES // 2 - 1) as pair:
                tile(2 * pair + 1, 1, False, False)
                tile(2 * pair + 2, 0, False, False)
            tile(TILES - 1, 1, False, True)

        @block.tensor
        def _(pe):
            pe.wait_ge(small_in, 16 * 5)

            def project(t, par, q, first=False):
                pe.wait_ge(split_done, QUARTERS * t + q + 1)
                if first:
                    pe.wait_ge(wq_split, QUARTERS if q else 1)
                for k in range(DC * q, DC * q + DC):
                    last = three_products(pe, ps_out[par][:], feats_hi[:, k, :], feats_lo[:, k, :],
                                          wq_hi[:, k, :], wq_lo[:, k, :], k == 0, k == FEAT_CHUNKS - 1)
                last.then_inc(quarter_used, 1)

            def norm_transposed(t, par):
                pe.wait_ge(xn_done, t + 1)
                for c in range(DC):
                    last = pe.transpose(ps_t[:, c * P:(c + 1) * P], xn[par][:, c * P:(c + 1) * P], ident[:])
                last.then_inc(xnT_done, 1)

            def similarities(t, par):
                pe.wait_ge(sim_w_done, t + 1)
                pe.wait_ge(ctx_in[par], 24 * (t - par) + 48)
                for c in range(DC):
                    for b in range(PER_TILE):
                        rows = slice(b * SEQ, (b + 1) * SEQ)
                        pe.matmul(ps_sim[rows, 0:CTX], sim_w[:, c, rows], ctxT[par][:, c, b, :],
                                  start=c == 0, stop=c == DC - 1)
                for c in range(DC):
                    last = pe.matmul(ps_p[:, w1_at:w1_at + 1], hcT[par][:, c, :], w_sim[:, 0, c:c + 1],
                                     start=c == 0, stop=c == DC - 1)
                last.then_inc(sim_done, 1)

            norm_transposed(0, 0)
            similarities(0, 0)

            def tile(t, par, first, last_tile):
                if not first:
                    project(t - 1, 1 - par, 1)
                pe.wait_ge(rest_done, t + 1)
                for c in range(CTX_CHUNKS):
                    pe.transpose(ps_p[:, c * P:(c + 1) * P], probs[:, c * P:(c + 1) * P], ident[:])
                pe.transpose(ps_p[0:PER_TILE, CTX_CHUNKS * P:(CTX_CHUNKS + 1) * P], probs_rest[:], ident[:]).then_inc(probsT_ps, 1)
                if not first:
                    project(t - 1, 1 - par, 2)
                    project(t - 1, 1 - par, 3)
                pe.wait_ge(probsT_done, t + 1)
                for c in range(CTX_CHUNKS):
                    for b in range(PER_TILE):
                        rows = slice(b * SEQ, (b + 1) * SEQ)
                        pe.matmul(ps_hq[rows, :], probsT[:, c, rows], ctxN[par][:, b, c, :],
                                  start=c == 0, stop=False)
                pe.matmul(ps_hq[:], probsT_rest[:], ctxR[par][:], start=False, stop=True).then_inc(hq_ps, 1)
                if not last_tile:
                    norm_transposed(t + 1, 1 - par)
                project(t, par, 0, first)
                pe.wait_ge(hq_done, t + 1)
                for c in range(DC):
                    last = pe.transpose(ps_hqt[:, c * P:(c + 1) * P], hq[:, c * P:(c + 1) * P], ident[:])
                last.then_inc(hqT_ps, 1)
                pe.wait_ge(batt_done, t + 1)
                for c in range(DC):
                    last = pe.matmul(ps_m[:, 4 * c:4 * c + 4], xn[par][:, c * P:(c + 1) * P], batt[:], start=True, stop=True)
                last.then_inc(bar_ps, 1)
                if not last_tile:
                    similarities(t + 1, 1 - par)
                if first:
                    pe.wait_ge(wq_split, QUARTERS)

            in_pairs(pe, tile)
            for q in range(1, QUARTERS):
                project(TILES - 1, 1, q)

        @block.scalar
        def _(act):
            def deviations(tiles):
                act.wait_ge(aggr_done, tiles.stop)
                act.activation(rstd[:, tiles], mean_var[:, tiles, 1], ACT.Sqrt, bias=eps[:]).then_inc(std_done, 1)

            def split_hi(t, par, q, fresh=False):
                if not fresh:
                    act.wait_ge(quarter_used, QUARTERS * (t - 1) + q + 1)
                act.activation(feats_hi[:, DC * q:DC * (q + 1), :], raw(q, par), ACT.Copy).then_inc(hi_done, 1)

            def norm_copy(t, par):
                act.wait_ge(xnT_done, t + 1)
                act.activation(hcT[par][:], ps_t[:].rearrange("p (c n) -> p c n", c=DC), ACT.Copy).then_inc(hcT_done, 1)

            act.wait_ge(eps_set, 1)
            deviations(slice(0, TILES_PER_GROUP))
            norm_copy(0, 0)
            act.wait_ge(hcT_done, 1)
            split_hi(0, 0, 0, True)

            def tile(t, par, first, last_tile):
                act.wait_ge(neg_max_done, t + 1)
                act.activation(probs[:], ps_sim[:, 0:CTX], ACT.Exp, bias=neg_max[:], accum_out=row_sum[:]).then_inc(probs_done, 1)
                act.wait_ge(probsT_ps, t + 1)
                act.activation(probsT[:], ps_p[:, 0:CTX_CHUNKS * P].rearrange("p (c n) -> p c n", c=CTX_CHUNKS), ACT.Copy)
                act.activation(probsT_rest[:], ps_p[0:PER_TILE, CTX_CHUNKS * P:(CTX_CHUNKS + 1) * P], ACT.Copy).then_inc(probsT_done, 1)
                act.wait_ge(top_step, 4 * t + 4)
                act.activation(top_exp[:], top_seq[:], ACT.Exp, bias=neg_top[:], accum_out=top_sum[:]).then_inc(own_done, 1)
                act.activation(own_exp[:], top[:], ACT.Exp, bias=neg_top[:]).then_inc(own_done, 1)
                act.wait_ge(hq_ps, t + 1)
                act.activation(hq[:], ps_hq[:], ACT.Copy, scale=row_rec[:]).then_inc(hq_done, 1)
                if not first:
                    act.wait_ge(split_done, QUARTERS * t)
                if not last_tile:
                    norm_copy(t + 1, 1 - par)
                if first:
                    for q in range(QUARTERS):
                        act.wait_ge(wq_in[q], 16)
                        act.activation(wq_hi[:, DC * q:DC * (q + 1), :], wq_raw[q], ACT.Copy).then_inc(wq_hi_done, 1)
                    deviations(slice(TILES_PER_GROUP, TILES))
                act.wait_ge(hqT_ps, t + 1)
                act.activation(raw(1, par), ps_hqt[:].rearrange("p (c n) -> p c n", c=DC), ACT.Copy).then_inc(hqT_done, 1)
                act.wait_ge(hqT_done, t + 1)
                split_hi(t, par, 1, first)
                act.wait_ge(bar_ps, t + 1)
                act.activation(bar[:], ps_m[:, 0:DC * PER_TILE].rearrange("p (c b) -> p c b", c=DC), ACT.Copy).then_inc(bar_done, 1)
                act.wait_ge(prod_done, 2 * t + 1)
                split_hi(t, par, 2, first)
                act.wait_ge(prod_done, 2 * t + 2)
                split_hi(t, par, 3, first)
                if not last_tile:
                    split_hi(t + 1, 1 - par, 0)

            in_pairs(act, tile)

        @block.vector
        def _(dve):
            dve.memset(eps[:], EPS).then_inc(eps_set, 1)

            def statistics(g):
                dve.wait_ge(x_in[g], 16)
                for t in range(g * TILES_PER_GROUP, (g + 1) * TILES_PER_GROUP):
                    if t:
                        dve.wait_ge(aggr_done, t)
                    dve.bn_stats(stats[:], x[:, t, :]).then_inc(stats_done, 1)
                    dve.wait_ge(stats_done, t + 1)
                    dve.bn_aggr(mean_var[:, t, :], stats[:]).then_inc(aggr_done, 1)

            def deviations(tiles, count):
                dve.wait_ge(std_done, count)
                dve.reciprocal(rstd[:, tiles], rstd[:, tiles]).then_inc(rstd_done, 1)
                dve.wait_ge(rstd_done, count)

            def split_lo(t, par, q):
                dve.wait_ge(hi_done, QUARTERS * t + q + 1)
                quarter = slice(DC * q, DC * (q + 1))
                dve.tensor_tensor(feats_lo[:, quarter, :], raw(q, par), feats_hi[:, quarter, :].bitcast(F32), ALU.subtract).then_inc(split_done, 1)

            def norm(t, par):
                dve.tensor_scalar(xn[par][:].rearrange("p (o n) -> p o n", o=1), x[:, bass.ds(t, 1), :], mean_var[:, bass.ds(t, 1), 0], rstd[:, bass.ds(t, 1)], ALU.subtract, ALU.mult).then_inc(xn_done, 1)
                dve.wait_ge(xn_done, t + 1)
                dve.tensor_tensor(x[:, bass.ds(t, 1), :], x[:, bass.ds(t, 1), :], b_qv[:].rearrange("p (o n) -> p o n", o=1), ALU.add).then_inc(bias_done, 1)

            def weigh(t, par):
                dve.wait_ge(hcT_done, t + 1)
                for c in range(DC):
                    last = dve.tensor_scalar(sim_w[:, c, :], hcT[par][:, c, :], w_sim[:, 2, c:c + 1], w_sim[:, 1, c:c + 1], ALU.mult, ALU.add)
                last.then_inc(sim_w_done, 1)

            def finish(t, par):
                dve.wait_ge(quarter_used, QUARTERS * (t + 1))
                dve.tensor_tensor(x[:, bass.ds(t, 1), :], ps_out[par][:].rearrange("p (o n) -> p o n", o=1), x[:, bass.ds(t, 1), :], ALU.add).then_inc(x_done, 1)

            statistics(0)
            deviations(slice(0, TILES_PER_GROUP), 1)
            dve.wait_ge(small_in, 16 * 5)
            norm(0, 0)
            weigh(0, 0)
            split_lo(0, 0, 0)

            def tile(t, par, first, last_tile):
                dve.wait_ge(sim_done, t + 1)
                dve.tensor_reduce(neg_max[:], ps_sim[:, 0:CTX], AX.X, ALU.max, negate=True).then_inc(neg_max_done, 1)
                dve.wait_ge(neg_max_done, t + 1)
                dve.scalar_tensor_tensor(top[:], ps_p[:, w1_at:w1_at + 1], b_sim[:], neg_max[:], ALU.add, ALU.subtract).then_inc(top_step, 1)
                dve.wait_ge(probs_done, t + 1)
                dve.reciprocal(row_rec[:], row_sum[:])
                dve.tensor_scalar(probs_rest[:], seq_of[:], probs[:, CTX - 1:CTX], None, ALU.mult).then_inc(rest_done, 1)
                dve.wait_ge(top_step, 4 * t + 1)
                dve.tensor_copy(top_wide[:], top[:].to_broadcast([P, SEQ])).then_inc(top_step, 1)
                dve.wait_ge(top_step, 4 * t + 2)
                dve.transpose(top_seq[:], top_wide[:]).then_inc(top_step, 1)
                dve.wait_ge(top_step, 4 * t + 3)
                dve.tensor_reduce(neg_top[:], top_seq[:], AX.X, ALU.max, negate=True).then_inc(top_step, 1)
                if not last_tile:
                    norm(t + 1, 1 - par)
                dve.wait_ge(own_done, 2 * t + 2)
                dve.reciprocal(top_rec[:], top_sum[:]).then_inc(rec_done, 1)
                dve.wait_ge(rec_done, t + 1)
                dve.tensor_scalar(batt[:], seq_of[:], own_exp[:], top_rec[:], ALU.mult, ALU.mult).then_inc(batt_done, 1)
                if not first:
                    finish(t - 1, 1 - par)
                if not last_tile:
                    weigh(t + 1, 1 - par)
                if first:
                    for q in range(QUARTERS):
                        dve.wait_ge(wq_hi_done, q + 1)
                        dve.tensor_tensor(wq_lo[:, DC * q:DC * (q + 1), :], wq_raw[q], wq_hi[:, DC * q:DC * (q + 1), :].bitcast(F32), ALU.subtract).then_inc(wq_split, 1)
                    for g in range(1, GROUPS):
                        statistics(g)
                    deviations(slice(TILES_PER_GROUP, TILES), 2)
                dve.wait_ge(hqT_done, t + 1)
                dve.tensor_tensor(raw(2, par), raw(0, par), raw(1, par), ALU.mult).then_inc(prod_done, 1)
                split_lo(t, par, 1)
                dve.wait_ge(bar_done, t + 1)
                bars = bar[:].rearrange("p c b -> p (c b)").unsqueeze(2).to_broadcast([P, DC * PER_TILE, SEQ])
                dve.tensor_tensor(raw(3, par).rearrange("p c (b s) -> p (c b) s", s=SEQ),
                                  raw(0, par).rearrange("p c (b s) -> p (c b) s", s=SEQ), bars, ALU.mult).then_inc(prod_done, 1)
                split_lo(t, par, 2)
                split_lo(t, par, 3)
                if not last_tile:
                    split_lo(t + 1, 1 - par, 0)

            in_pairs(dve, tile)
            finish(TILES - 1, 1)
            dve.wait_ge(x_done, TILES)


def linear_attention(nc, dram, keep):
    with ExitStack() as stack:
        fr = Frame(nc, stack, "la_")
        x, ident = keep["x"], keep["ident"]
        PW, WQ, WK, WV, WG, WO = range(6)
        late_hi = fr.sbuf("late_hi", [P, 2 * DC, D], F32R)
        late_lo = fr.sbuf("late_lo", [P, 2 * DC, D], F32R)

        def weight(n):
            if n < WG:
                return keep["r_hi"][:, DC * n:DC * (n + 1), :], keep["r_lo"][:, DC * n:DC * (n + 1), :]
            n -= WG
            return late_hi[:, DC * n:DC * (n + 1), :], late_lo[:, DC * n:DC * (n + 1), :]

        xn = fr.sbuf("xn", [P, CT, D])
        xc = [fr.sbuf(f"xc{i}", [P, DC, CHUNK]) for i in range(2)]
        main_hi = fr.sbuf("main_hi", [P, DC, CHUNK], F32R)
        main_lo = fr.sbuf("main_lo", [P, DC, CHUNK], F32R)
        part = fr.sbuf("part", [P, DC, CHUNK])
        side_hi = fr.sbuf("side_hi", [P, DC, CHUNK], F32R)
        side_lo = fr.sbuf("side_lo", [P, DC, CHUNK], F32R)
        q = fr.sbuf("q", [P, DC, CHUNK])
        k = fr.sbuf("k", [P, DC, CHUNK])
        exq = fr.sbuf("exq", [P, DC, CHUNK])
        swap = fr.sbuf("swap", [P, DC, CHUNK])
        gate = fr.sbuf("gate", [P, DC, CHUNK])
        heads = fr.sbuf("heads", [P, DC, CT, HEADS_PER_CHUNK, P])
        v = fr.sbuf("v", [P, CT, D])
        scores = [fr.sbuf(f"scores{i}", [P, HEADS_PER_CHUNK, P]) for i in range(2)]
        causal = fr.sbuf("causal", [P, P])
        cos = fr.sbuf("cos", [P, SEQ])
        sin = fr.sbuf("sin", [P, SEQ])
        w_dw = fr.sbuf("w_dw", [P, DC, 3])
        ones_strip = fr.sbuf("ones_strip", [P, HEAD + DC - 1])
        spread = fr.sbuf("spread", [P, DC, P])
        half_b_gate = fr.sbuf("half_b_gate", [P, DC])
        mean_var = keep["mean_var"]
        rstd = fr.sbuf("rstd", [P, TILES])
        eps = fr.sbuf("eps", [P, 1])
        x2_mv = fr.sbuf("x2_mv", [P, CT, 2])
        x2_stats = fr.sbuf("x2_stats", [P, CT, 6])
        stats = x2_stats[:, 0, :]
        den = scores[0][:, 0:CT, :].rearrange("p t n -> p (t n)")
        stage = [heads[:, 2 * i:2 * i + 2].rearrange("p a b c d -> p (a b c d)").rearrange("p (k n) -> p k n", n=D) for i in range(2)]

        ps_a = fr.psum("ps_a", [P, 2, 512])
        ps_b = fr.psum("ps_b", [P, 2, 512])
        ps_c = fr.psum("ps_c", [P, 2, 512])
        ps_d = fr.psum("ps_d", [P, 2, 512])

        def wide(ps):
            return ps[:].rearrange("p a n -> p (a n)").rearrange("p (c n) -> p c n", c=DC)

        names = ("small_in stage_hi stage_lo stats_done aggr_done eps_set std_done rstd_done heads_zero "
                 "half_done xn_done xnT_ps xT_done conv_step y_hi_done y_lo_done pw_ps xc_done xc_hi_done xc_lo_done "
                 "delta_done d_hi_done d_lo_done q_ps q_raw k_ps k_raw v_ps v_done rope_step cos_done rope_q rope_k "
                 "relu_k exq_step exk_step phi_q phi_k gate_ps gate_done scores_ps masked heads_ps den_done rec_done spread_ps "
                 "num_done norm_done a_hi_done a_lo_done wo_ps mix_step x2_ps x2_stats x2_done x2_out x_done").split()
        s = {n: fr.sem(n) for n in names}
        stage_in = [fr.sem(f"stage_in{i}") for i in range(2)]
        block = stack.enter_context(nc.Block())
        STEPS = CT * DC
        SMALL = 7

        def chunks(eng, step):
            step(0, 0, True, False)
            with eng.Fori(0, CHUNKS // 2 - 1) as pair:
                step(2 * pair + 1, 1, False, False)
                step(2 * pair + 2, 0, False, False)
            step(CHUNKS - 1, 1, False, True)

        def by_seq(buf, c):
            return buf[:, c, :].rearrange("p (q s) -> p q s", s=SEQ)

        def all_seq(buf):
            return buf[:, :, :].rearrange("p c n -> p (c n)").rearrange("p (q s) -> p q s", s=SEQ)

        def every_seq(table):
            return table[:].unsqueeze(1).to_broadcast([P, DC * CSEQ, SEQ])

        def z_cos(eng, z, cs):
            n = (cs.stop - cs.start) * CSEQ
            return eng.tensor_tensor(part[:, cs, :].rearrange("p c n -> p (c n)").rearrange("p (q s) -> p q s", s=SEQ),
                                     z[:, cs, :].rearrange("p c n -> p (c n)").rearrange("p (q s) -> p q s", s=SEQ),
                                     cos[:].unsqueeze(1).to_broadcast([P, n, SEQ]), ALU.mult)

        def phi_heads(eng, j):
            rows = slice(j * HEAD, (j + 1) * HEAD)
            return eng.scalar_tensor_tensor(
                heads[rows, :, :, j, :].rearrange("p c t n -> p (c t) n"),
                q[rows].rearrange("p c (t n) -> p (c t) n", n=P), 0.0,
                exq[rows].rearrange("p c (t n) -> p (c t) n", n=P), ALU.max, ALU.add)

        @block.sync
        def _(sp):
            for n in range(6):
                if n >= 2:
                    sp.wait_ge(s["stage_lo"], n - 1)
                sp.dma_start(stage[n % 2], dram["attn_w"][n].rearrange("(k p) n -> p k n", p=P)).then_inc(stage_in[n % 2], 16)
                if n == 0:
                    for t, name in ((w_dw, "w_dw"), (cos, "cos"), (sin, "sin"), (half_b_gate, "b_gate"), (causal, "causal"),
                                    (ones_strip, "ones_strip"), (spread, "spread")):
                        sp.dma_start(t[:], dram[name]).then_inc(s["small_in"], 16)

            def x2_out(i):
                sp.wait_ge(s["x2_done"], i + 1)
                sp.dma_start(dram["x2"][bass.ds(CT * i, CT)].rearrange("t p d -> p t d"), xn[:]).then_inc(s["x2_out"], 16)

            with sp.Fori(0, CHUNKS) as i:
                x2_out(i)
            sp.wait_ge(s["x2_out"], 16 * CHUNKS)

        @block.gpsimd
        def _(pool):
            pool.wait_ge(s["small_in"], 16 * SMALL)

            def step(i, par, first, last):
                pool.wait_ge(s["xc_done"], i + 1)
                pool.wait_ge(s["y_lo_done"], i + 1)
                d, z = all_seq(part), all_seq(xc[par])
                nc.gpsimd.tensor_tensor(d[:, :, 1:], z[:, :, 1:], z[:, :, :SEQ - 1], ALU.subtract).then_inc(s["delta_done"], 1)
                nc.gpsimd.memset(d[:, :, 0:1], 0.0).then_inc(s["delta_done"], 1)
                pool.wait_ge(s["d_hi_done"], i + 1)
                pool.wait_ge(s["delta_done"], 2 * i + 2)
                nc.gpsimd.tensor_tensor(side_lo[:], part[:], side_hi[:].bitcast(F32), ALU.subtract).then_inc(s["d_lo_done"], 1)
                if first:
                    pool.wait_ge(s["stage_lo"], 6)
                    nc.gpsimd.memset(heads[:], 0.0).then_inc(s["heads_zero"], 1)
                pool.wait_ge(s["q_raw"], i + 1)
                pool.wait_ge(s["d_lo_done"], i + 1)
                z_cos(nc.gpsimd, q, slice(1, DC)).then_inc(s["cos_done"], 1)
                pool.wait_ge(s["k_raw"], i + 1)
                pool.wait_ge(s["rope_q"], i + 1)
                z_cos(nc.gpsimd, k, slice(1, DC)).then_inc(s["cos_done"], 1)
                pool.wait_ge(s["relu_k"], i + 1)
                pool.wait_ge(s["exk_step"], 2 * i + 2)
                nc.gpsimd.tensor_tensor(k[:], k[:], swap[:], ALU.add).then_inc(s["phi_k"], 1)

            chunks(pool, step)

        @block.tensor
        def _(pe):
            def transpose_norm(i):
                pe.wait_ge(s["xn_done"], i + 1)
                for c in range(DC):
                    for t in range(CT):
                        last = pe.transpose(wide(ps_a)[:, c, t * P:(t + 1) * P], xn[:, t, c * P:(c + 1) * P], ident[:])
                last.then_inc(s["xnT_ps"], 1)

            def project_part(n, ps, m_hi, m_lo, e):
                w_hi, w_lo = weight(n)
                cols = slice(e * P, (e + 1) * P)
                for c in range(DC):
                    last = three_products(pe, wide(ps)[:, e, :], w_hi[:, c, cols], w_lo[:, c, cols],
                                          m_hi[:, c, :], m_lo[:, c, :], c == 0, c == DC - 1)
                return last

            def project(n, ps, m_hi, m_lo, done):
                for e in range(DC):
                    last = project_part(n, ps, m_hi, m_lo, e)
                last.then_inc(done, 1)

            def spread_reciprocals(i):
                pe.wait_ge(s["rec_done"], i + 1)
                for c in range(DC):
                    mm = pe.matmul(wide(ps_c)[:, c, :], spread[:, c, :], den, start=True, stop=True)
                mm.then_inc(s["spread_ps"], 1)

            def x2_transposed(i):
                pe.wait_ge(s["mix_step"], 2 * i + 2)
                for t in range(CT):
                    for c in range(DC):
                        mm = pe.transpose(ps_a[:, t, c * P:(c + 1) * P], gate[:, c, t * P:(t + 1) * P], ident[:])
                mm.then_inc(s["x2_ps"], 1)

            transpose_norm(0)
            pe.wait_ge(s["stage_lo"], PW + 1)
            pe.wait_ge(s["y_lo_done"], 1)
            project(PW, ps_b, main_hi, main_lo, s["pw_ps"])

            def step(i, par, first, last):
                def weight_split(n):
                    if first:
                        pe.wait_ge(s["stage_lo"], n + 1)

                pe.wait_ge(s["xc_lo_done"], i + 1)
                weight_split(WQ)
                project(WQ, ps_b, main_hi, main_lo, s["q_ps"])
                if not first:
                    x2_transposed(i - 1)
                weight_split(WK)
                project(WK, ps_c, main_hi, main_lo, s["k_ps"])
                weight_split(WV)
                w_hi, w_lo = weight(WV)
                for t in range(CT):
                    toks = slice(t * P, (t + 1) * P)
                    for c in range(DC):
                        mm = three_products(pe, ps_d[:, t, :], main_hi[:, c, toks], main_lo[:, c, toks],
                                            w_hi[:, c, :], w_lo[:, c, :], c == 0, c == DC - 1)
                mm.then_inc(s["v_ps"], 1)
                if not last:
                    transpose_norm(i + 1)
                pe.wait_ge(s["d_lo_done"], i + 1)
                pe.wait_ge(s["q_raw"], i + 1)
                weight_split(WG)
                project(WG, ps_b, side_hi, side_lo, s["gate_ps"])
                pe.wait_ge(s["phi_q"], i + 1)
                pe.wait_ge(s["phi_k"], i + 1)
                for t in range(CT):
                    for c in range(DC):
                        for b in range(PER_TILE):
                            rows = slice(b * SEQ, (b + 1) * SEQ)
                            mm = pe.matmul(ps_c[rows, t, c * P:(c + 1) * P], k[:, c, t * P + b * SEQ:t * P + (b + 1) * SEQ],
                                           heads[:, c, t, :, rows], start=True, stop=True)
                    mm.then_inc(s["scores_ps"], 1)
                pe.wait_ge(s["v_done"], i + 1)
                for n in range(STEPS):
                    t, c = n // DC, n % DC
                    toks = slice(t * P, (t + 1) * P)
                    pe.wait_ge(s["masked"], STEPS * i + n + 1)
                    if n == 0 and not last:
                        pe.wait_ge(s["xT_done"], i + 2)
                        pe.wait_ge(s["conv_step"], 3 * i + 4)
                    for j in range(HEADS_PER_CHUNK):
                        h = HEADS_PER_CHUNK * c + j
                        rows = slice(j * HEAD, (j + 1) * HEAD)
                        pe.matmul(wide(ps_d)[rows, c, toks], v[:, t, h * HEAD:(h + 1) * HEAD], scores[n % 2][:, j, :],
                                  start=True, stop=True)
                    for j in range(HEADS_PER_CHUNK):
                        rows = slice(j * HEAD, (j + 1) * HEAD)
                        mm = pe.matmul(ps_a[rows, 0, toks], ones_strip[:, DC - 1 - c:DC - 1 - c + HEAD], scores[n % 2][:, j, :],
                                       start=c == 0, stop=c == DC - 1)
                    mm.then_inc(s["heads_ps"], 1)
                if last:
                    spread_reciprocals(i)
                else:
                    pe.wait_ge(s["y_lo_done"], i + 2)
                    pe.wait_ge(s["gate_done"], i + 1)
                    for e in range(DC):
                        mm = project_part(PW, ps_b, main_hi, main_lo, e)
                        if e == 1:
                            spread_reciprocals(i)
                    mm.then_inc(s["pw_ps"], 1)
                pe.wait_ge(s["a_lo_done"], i + 1)
                weight_split(WO)
                project(WO, ps_d, side_hi, side_lo, s["wo_ps"])

            chunks(pe, step)
            x2_transposed(CHUNKS - 1)

        @block.scalar
        def _(act):
            copy = ACT.Copy

            def weight_hi(n):
                act.wait_ge(stage_in[n % 2], 16 * (n // 2 + 1))
                act.activation(weight(n)[0], stage[n % 2], copy).then_inc(s["stage_hi"], 1)

            def deviations(tiles):
                act.wait_ge(s["aggr_done"], tiles.stop)
                act.activation(rstd[:, tiles], mean_var[:, tiles, 1], ACT.Sqrt, bias=eps[:]).then_inc(s["std_done"], 1)

            def front(i, par):
                act.wait_ge(s["xnT_ps"], i + 1)
                act.activation(xc[par][:], wide(ps_a), copy).then_inc(s["xT_done"], 1)
                for c in range(DC):
                    a = act.activation(part[:, c, :], wide(ps_a)[:, c, :], copy, scale=w_dw[:, c, 2:3])
                a.then_inc(s["conv_step"], 1)

            def conv_hi(i):
                act.wait_ge(s["conv_step"], 3 * i + 3)
                act.activation(main_hi[:], part[:], copy).then_inc(s["y_hi_done"], 1)

            def xc_high(i, par):
                act.wait_ge(s["xc_done"], i + 1)
                act.activation(main_hi[:], xc[par][:], copy).then_inc(s["xc_hi_done"], 1)

            def x2_copy(i):
                act.wait_ge(s["x2_ps"], i + 1)
                act.activation(xn[:], ps_a[:], copy).then_inc(s["x2_done"], 1)

            def negative_exp(buf, src, ready, steps, i):
                act.wait_ge(ready, i + 1)
                act.activation(buf[:], src[:], ACT.Relu, scale=-1.0).then_inc(steps, 1)
                act.wait_ge(steps, 2 * i + 1)
                act.activation(buf[:], buf[:], ACT.Exp, scale=-1.0).then_inc(steps, 1)

            act.wait_ge(s["eps_set"], 1)
            deviations(slice(0, CT))
            act.wait_ge(s["small_in"], 16 * SMALL)
            front(0, 0)
            weight_hi(PW)
            conv_hi(0)
            weight_hi(WQ)
            xc_high(0, 0)
            act.wait_ge(s["half_done"], 1)

            def step(i, par, first, last):
                if first:
                    weight_hi(WK)
                act.wait_ge(s["delta_done"], 2 * i + 2)
                if not first:
                    act.wait_ge(s["wo_ps"], i)
                act.activation(side_hi[:], part[:], copy).then_inc(s["d_hi_done"], 1)
                if first:
                    for n in (WV, WG, WO):
                        weight_hi(n)
                    deviations(slice(CT, TILES))
                act.wait_ge(s["q_ps"], i + 1)
                act.activation(q[:], wide(ps_b), copy).then_inc(s["q_raw"], 1)
                if not first:
                    x2_copy(i - 1)
                negative_exp(exq, q, s["rope_q"], s["exq_step"], i)
                act.wait_ge(s["k_ps"], i + 1)
                act.activation(k[:], wide(ps_c), copy).then_inc(s["k_raw"], 1)
                act.wait_ge(s["v_ps"], i + 1)
                act.activation(v[:], ps_d[:], copy).then_inc(s["v_done"], 1)
                negative_exp(swap, k, s["rope_k"], s["exk_step"], i)
                act.activation(k[:], k[:], ACT.Relu).then_inc(s["relu_k"], 1)
                if not last:
                    front(i + 1, 1 - par)
                act.wait_ge(s["gate_ps"], i + 1)
                for c in range(DC):
                    a = act.activation(gate[:, c, :], wide(ps_b)[:, c, :], ACT.Tanh, bias=half_b_gate[:, c:c + 1], scale=0.5)
                a.then_inc(s["gate_done"], 1)
                if not last:
                    conv_hi(i + 1)
                act.wait_ge(s["heads_ps"], STEPS * (i + 1))
                act.activation(q[:], wide(ps_d), copy).then_inc(s["num_done"], 1)
                act.wait_ge(s["norm_done"], i + 1)
                act.activation(side_hi[:], q[:], copy).then_inc(s["a_hi_done"], 1)
                if not last:
                    xc_high(i + 1, 1 - par)

            chunks(act, step)
            act.wait_ge(s["x2_out"], 16 * (CHUNKS - 1))
            x2_copy(CHUNKS - 1)

        @block.vector
        def _(dve):
            def statistics(t):
                if t:
                    dve.wait_ge(s["aggr_done"], t)
                dve.bn_stats(stats, x[:, t, :]).then_inc(s["stats_done"], 1)
                dve.wait_ge(s["stats_done"], t + 1)
                dve.bn_aggr(mean_var[:, t, :], stats).then_inc(s["aggr_done"], 1)

            def deviations(tiles, count):
                dve.wait_ge(s["std_done"], count)
                dve.reciprocal(rstd[:, tiles], rstd[:, tiles]).then_inc(s["rstd_done"], 1)
                dve.wait_ge(s["rstd_done"], count)

            def lo(out, raw, hi, ready, count, done):
                dve.wait_ge(ready, count)
                dve.tensor_tensor(out[:], raw[:], hi[:].bitcast(F32), ALU.subtract).then_inc(done, 1)

            def weight_lo(n):
                w_hi, w_lo = weight(n)
                dve.wait_ge(s["stage_hi"], n + 1)
                dve.tensor_tensor(w_lo, stage[n % 2], w_hi.bitcast(F32), ALU.subtract).then_inc(s["stage_lo"], 1)

            def norm(i):
                for t in range(CT):
                    tile = CT * i + t
                    a = dve.tensor_scalar(xn[:, t:t + 1, :], x[:, bass.ds(tile, 1), :], mean_var[:, bass.ds(tile, 1), 0],
                                          rstd[:, bass.ds(tile, 1)], ALU.subtract, ALU.mult)
                a.then_inc(s["xn_done"], 1)

            def taps(i, par):
                dve.wait_ge(s["xT_done"], i + 1)
                for tap in range(1, 3):
                    dve.wait_ge(s["conv_step"], 3 * i + tap)
                    for c in range(DC):
                        y, z = by_seq(part, c), by_seq(xc[par], c)
                        w = w_dw[:, c, 2 - tap:3 - tap]
                        a = dve.scalar_tensor_tensor(y[:, :, tap:], z[:, :, :SEQ - tap], w, y[:, :, tap:], ALU.mult, ALU.add)
                    a.then_inc(s["conv_step"], 1)

            def residual(i, par):
                dve.wait_ge(s["pw_ps"], i + 1)
                dve.tensor_tensor(xc[par][:], wide(ps_b), xc[par][:], ALU.add).then_inc(s["xc_done"], 1)
                lo(main_lo, xc[par], main_hi, s["xc_hi_done"], i + 1, s["xc_lo_done"])

            def rope(i, z, n):
                dve.wait_ge(s[("q_raw", "k_raw")[n]], i + 1)
                if n:
                    dve.wait_ge(s["rope_q"], i + 1)
                dve.wait_ge(s["d_lo_done"], i + 1)
                z_cos(dve, z, slice(0, 1)).then_inc(s["cos_done"], 1)
                dve.stream_shuffle(swap[:], z[:], [a ^ 1 for a in range(32)]).then_inc(s["rope_step"], 1)
                dve.wait_ge(s["rope_step"], 4 * i + 2 * n + 1)
                dve.tensor_tensor(all_seq(swap), all_seq(swap), every_seq(sin), ALU.mult).then_inc(s["rope_step"], 1)
                dve.wait_ge(s["rope_step"], 4 * i + 2 * n + 2)
                dve.wait_ge(s["cos_done"], 4 * i + 2 * n + 2)
                dve.tensor_tensor(z[:], part[:], swap[:], ALU.add).then_inc(s[("rope_q", "rope_k")[n]], 1)

            def mix(i, par):
                dve.wait_ge(s["wo_ps"], i + 1)
                dve.wait_ge(s["gate_done"], i + 1)
                dve.scalar_tensor_tensor(gate[:], gate[:], 1.0, wide(ps_d), ALU.add, ALU.mult).then_inc(s["mix_step"], 1)
                dve.wait_ge(s["mix_step"], 2 * i + 1)
                dve.scalar_tensor_tensor(gate[:], gate[:], 0.5, xc[par][:], ALU.mult, ALU.add).then_inc(s["mix_step"], 1)

            def x2_sum(i):
                dve.wait_ge(s["x2_done"], i + 1)
                for t in range(CT):
                    dve.bn_stats(x2_stats[:, t, :], xn[:, t, :]).then_inc(s["x2_stats"], 1)
                tiles = bass.ds(CT * i, CT)
                dve.wait_ge(s["x2_stats"], 2 * CT * i + CT)
                dve.tensor_tensor(x[:, tiles, :], xn[:], x[:, tiles, :], ALU.add).then_inc(s["x_done"], 1)
                for t in range(CT):
                    dve.bn_aggr(x2_mv[:, t, :], x2_stats[:, t, :]).then_inc(s["x2_stats"], 1)
                dve.wait_ge(s["x2_stats"], 2 * CT * (i + 1))
                dve.tensor_copy(keep["mean_var"][:, tiles, :], x2_mv[:])

            dve.memset(eps[:], EPS).then_inc(s["eps_set"], 1)
            for t in range(CT):
                statistics(t)
            deviations(slice(0, CT), 1)
            norm(0)
            dve.wait_ge(s["small_in"], 16 * SMALL)
            dve.tensor_scalar(half_b_gate[:], half_b_gate[:], 0.5, None, ALU.mult).then_inc(s["half_done"], 1)
            taps(0, 0)
            weight_lo(PW)
            lo(main_lo, part, main_hi, s["y_hi_done"], 1, s["y_lo_done"])
            weight_lo(WQ)
            residual(0, 0)

            def step(i, par, first, last):
                if first:
                    for n in (WK, WV, WG, WO):
                        weight_lo(n)
                    for t in range(CT, TILES):
                        statistics(t)
                    deviations(slice(CT, TILES), 2)
                else:
                    mix(i - 1, 1 - par)
                rope(i, q, 0)
                if not first:
                    x2_sum(i - 1)
                if not last:
                    if not first:
                        dve.wait_ge(s["x2_out"], 16 * i)
                        dve.wait_ge(s["x_done"], i)
                    norm(i + 1)
                rope(i, k, 1)
                dve.wait_ge(s["exq_step"], 2 * i + 2)
                if first:
                    dve.wait_ge(s["heads_zero"], 1)
                for j in range(HEADS_PER_CHUNK):
                    a = phi_heads(dve, j)
                a.then_inc(s["phi_q"], 1)
                if not last:
                    taps(i + 1, 1 - par)
                for n in range(STEPS):
                    t, c = divmod(n, DC)
                    dve.wait_ge(s["scores_ps"], CT * i + t + 1)
                    if n >= 2:
                        dve.wait_ge(s["heads_ps"], STEPS * i + n - 1)
                    dve.tensor_tensor(scores[n % 2][:].rearrange("p j (b s) -> p j b s", b=PER_TILE),
                                      ps_c[:, t, c * P:(c + 1) * P].rearrange("p (j s) -> p j s", s=SEQ).unsqueeze(2).to_broadcast([P, HEADS_PER_CHUNK, PER_TILE, SEQ]),
                                      causal[:].rearrange("p (b s) -> p b s", b=PER_TILE).unsqueeze(1).to_broadcast([P, HEADS_PER_CHUNK, PER_TILE, SEQ]),
                                      ALU.mult).then_inc(s["masked"], 1)
                    if n == DC - 1 and not last:
                        lo(main_lo, part, main_hi, s["y_hi_done"], i + 2, s["y_lo_done"])
                dve.wait_ge(s["heads_ps"], STEPS * (i + 1))
                dve.tensor_scalar(den, ps_a[:, 0, 0:CHUNK], DEN_EPS, None, ALU.add).then_inc(s["den_done"], 1)
                dve.wait_ge(s["den_done"], i + 1)
                dve.reciprocal(den, den).then_inc(s["rec_done"], 1)
                dve.wait_ge(s["spread_ps"], i + 1)
                dve.wait_ge(s["num_done"], i + 1)
                dve.tensor_tensor(q[:], wide(ps_c), q[:], ALU.mult).then_inc(s["norm_done"], 1)
                lo(side_lo, q, side_hi, s["a_hi_done"], i + 1, s["a_lo_done"])
                if not last:
                    residual(i + 1, 1 - par)

            chunks(dve, step)
            mix(CHUNKS - 1, 1)
            x2_sum(CHUNKS - 1)
            dve.wait_ge(s["x_done"], CHUNKS)


def feed_forwards(nc, dram, keep, out, experts_only=False):
    with ExitStack() as stack:
        fr = Frame(nc, stack, "ff_")
        x, ident, mean_var = keep["x"], keep["ident"], keep["mean_var"]
        h_hi, h_lo = keep["r_hi"], keep["r_lo"]
        up_hi = [fr.sbuf(f"up_hi{i}", [P, DC, SUB], F32R) for i in range(2)]
        up_lo = [fr.sbuf(f"up_lo{i}", [P, DC, SUB], F32R) for i in range(2)]
        down_hi = [fr.sbuf(f"down_hi{i}", [P, FC, D], F32R) for i in range(2)]
        down_lo = [fr.sbuf(f"down_lo{i}", [P, FC, D], F32R) for i in range(2)]
        up_raw = fr.sbuf("up_raw", [P, DC, SUB])
        down_raw = fr.sbuf("down_raw", [P, FC, D])
        hid = fr.sbuf("hid", [P, FC, GROUP])
        hid_hi = fr.sbuf("hid_hi", [P, FC, GROUP], F32R)
        hid_lo = fr.sbuf("hid_lo", [P, FC, GROUP], F32R)
        up_bias = fr.sbuf("up_bias", [P, SUBS * FC])
        down_bias = fr.sbuf("down_bias", [P, D])
        ln_g = fr.sbuf("ln_g", [P, DC])
        ln_b = fr.sbuf("ln_b", [P, DC])
        w_moe = fr.sbuf("w_moe", [P, DC, EXPERTS])
        w_router = fr.sbuf("w_router", [P, DC, BLOCKS])
        b_router = fr.sbuf("b_router", [P, BLOCKS])
        rstd = fr.sbuf("rstd", [P, TILES])
        stats = fr.sbuf("stats", [P, 6])
        eps = fr.sbuf("eps", [P, 1])
        share = fr.sbuf("share", [P, TILES, EXPERTS])
        share_by = fr.sbuf("share_by", [P, EXPERTS, TILES])
        soft = fr.sbuf("soft", [P, 2, TILES])
        shut_in = fr.sbuf("shut_in", [P, GROUPS, BLOCKS])
        shut = fr.sbuf("shut", [P, GROUPS * BLOCKS], BF16)
        left_outT = fr.sbuf("left_outT", [P, GROUP], BF16)
        block_no = fr.sbuf("block_no", [P, BLOCKS])
        prob = fr.sbuf("prob", [P, TILES_PER_GROUP, BLOCKS])
        best = fr.sbuf("best", [P, TILES_PER_GROUP, 8])
        best_at = fr.sbuf("best_at", [P, TILES_PER_GROUP, 8], U32)
        spot = fr.sbuf("spot", [P, TILES_PER_GROUP, 8])
        chosen = fr.sbuf("chosen", [P, TILES_PER_GROUP, BLOCKS, TOP_K])
        left_out = prob
        def slot(i):
            return 0 if i % TILES in (1, 3) else 2

        def xn(i):
            return hid[:, slot(i), :]

        def h_raw(i):
            return hid[:, slot(i) + 1, :].rearrange("p (c n) -> p c n", c=DC)

        def x2_arrival(t):
            return (x_in[0], 16 * (t // 2 + 1)) if slot(t) == 0 else (x_in[1], 16 * (t // 2 + 1 if t <= TILES_PER_GROUP else t - 1))

        ps_up = [fr.psum(f"ps_up{f}") for f in range(FC)]
        ps_down = [fr.psum(f"ps_down{t}") for t in range(TILES_PER_GROUP)]

        names = ("small_in w_in w_hi_done w_split b2_in b2_used xn_done xT_ps h_raw_done h_hi_done h_lo_done logit_ps "
                 "logit_done soft_step exp_done share_done up_done hid_hi_done hid_done down_done acc_done eps_set "
                 "std_done rstd_done stats_done aggr_done top_done out_left left_ps leftT_done leftT_zero x_out").split()
        s = {n: fr.sem(n) for n in names}
        x_in = [fr.sem(f"x_in{i}") for i in range(2)]
        block = stack.enter_context(nc.Block())
        last_sub = MOE_SUBS if experts_only else SUBS
        SMALL = 9

        def weights_in(sp, sub):
            sp.dma_start(up_raw[:], dram["up_w"][bass.ds(sub, 1)].rearrange("o p c f -> p (o c) f")).then_inc(s["w_in"], 16)
            sp.dma_start(down_raw[:], dram["down_w"][bass.ds(sub, 1)].rearrange("o p c d -> p (o c) d")).then_inc(s["w_in"], 16)

        @block.sync
        def _(sp):
            for t in range(2):
                sp.dma_start(xn(t), dram["x2"][t]).then_inc(x2_arrival(t)[0], 16)
            for t, name in ((up_bias, "up_bias"), (ln_g, "ln_g"), (ln_b, "ln_b"), (w_moe, "w_moe"), (w_router, "w_router"),
                            (shut_in, "shut"), (block_no, "block_no")):
                sp.dma_start(t[:], dram[name]).then_inc(s["small_in"], 16)
            sp.dma_start(b_router[:], dram["b_router"].partition_broadcast(P)).then_inc(s["small_in"], 16)
            sp.dma_start(down_bias[:], dram["down_bias"][0].partition_broadcast(P)).then_inc(s["small_in"], 16)
            weights_in(sp, 0)
            for t in range(2, TILES):
                sp.wait_ge(s["xT_ps"], t - 1 if t <= TILES_PER_GROUP else t)
                sp.dma_start(xn(t), dram["x2"][t]).then_inc(x2_arrival(t)[0], 16)
                if t == TILES_PER_GROUP:
                    sp.wait_ge(s["w_split"], DC)
                    weights_in(sp, 1)
            with sp.Fori(0, EXPERTS) as e:
                for j in range(SUBS_PER_EXPERT):
                    sub = SUBS_PER_EXPERT * e + j
                    sp.wait_ge(s["w_split"], DC * sub + 2 * DC)
                    weights_in(sp, sub + 2)
                    if j == 1:
                        sp.wait_ge(s["b2_used"], TILES * e + TILES)
                        sp.dma_start(down_bias[:], dram["down_bias"][bass.ds(e + 1, 1)].rearrange("o d -> (o d)").partition_broadcast(P)).then_inc(s["b2_in"], 16)
            if not experts_only:
                for sub in range(MOE_SUBS, SUBS - 2):
                    sp.wait_ge(s["w_split"], DC * sub + 2 * DC)
                    weights_in(sp, sub + 2)
            sp.wait_ge(s["acc_done"], TILES * last_sub)
            sp.dma_start(out.rearrange("(t p) d -> p t d", p=P), x[:]).then_inc(s["x_out"], 16)
            sp.wait_ge(s["x_out"], 16)

        @block.gpsimd
        def _(pool):
            nc.gpsimd.memset(left_outT[:], 0.0).then_inc(s["leftT_zero"], 1)

        def sub_loops(eng, group):
            for j in range(1, SUBS_PER_EXPERT):
                with eng.Fori(0, GROUPS) as g:
                    group(j, j, g, 0)
            with eng.Fori(1, EXPERTS) as e:
                for j in range(SUBS_PER_EXPERT):
                    with eng.Fori(0, GROUPS) as g:
                        group(SUBS_PER_EXPERT * e + j, j, g, e)

        def ffn_loops(eng, group):
            for j in range(1, FFN_SUBS):
                with eng.Fori(0, GROUPS) as g:
                    group(MOE_SUBS + j, j, g, None)

        def up_bank(f, mixed):
            return ps_up[f % (FC - 1)] if mixed else ps_up[f]

        def lead_bank(i):
            return ps_up[min(i % TILES, TILES_PER_GROUP - 1)]

        @block.tensor
        def _(pe):
            routers = ((EXPERTS, w_moe), (BLOCKS, w_router))

            def lead_turn(i):
                pe.wait_ge(s["xn_done"], i + 1)
                if i % TILES >= TILES_PER_GROUP:
                    pe.wait_ge(s["logit_done"], i)
                for c in range(DC):
                    mm = pe.transpose(lead_bank(i)[:, c * P:(c + 1) * P], xn(i)[:, c * P:(c + 1) * P], ident[:])
                mm.then_inc(s["xT_ps"], 1)

            def lead_logits(i):
                logits, w = routers[i // TILES]
                pe.wait_ge(s["h_raw_done"], i + 1)
                for c in range(DC):
                    mm = pe.matmul(lead_bank(i)[:, 0:logits], h_raw(i)[:, c, :], w[:, c, :], start=c == 0, stop=c == DC - 1)
                mm.then_inc(s["logit_ps"], 1)

            def left_transposed(g):
                pe.wait_ge(s["out_left"], g + 1)
                for u in range(TILES_PER_GROUP):
                    mm = pe.transpose(ps_up[3][0:BLOCKS, u * P:(u + 1) * P], left_out[:, u, :], ident[:])
                mm.then_inc(s["left_ps"], 1)

            def group(sub, j, g, e, mixed=False, ahead=None):
                par = j % 2
                n = GROUPS * sub + g
                pe.wait_ge(s["w_split"], DC * sub + DC)
                if mixed:
                    pe.wait_ge(s["h_lo_done"], TILES * (e is None) + TILES_PER_GROUP * (g + 1))

                def up(f):
                    cols = slice(f * P, (f + 1) * P)
                    bank = up_bank(f, mixed)
                    for c in range(DC):
                        at = bass.ds(DC * g + c, 1)
                        mm = three_products(pe, bank[:], up_hi[par][:, c, cols], up_lo[par][:, c, cols],
                                            h_hi[:, at, :].rearrange("p o n -> p (o n)"), h_lo[:, at, :].rearrange("p o n -> p (o n)"),
                                            c == 0, c == DC - 1 and e is not None)
                    if e is None:
                        if mixed and f == 0:
                            if g == 0:
                                left_transposed(g)
                            pe.wait_ge(s["leftT_done"], g + 1)
                        mm = pe.matmul(bank[:], shut[:, bass.ds(BLOCKS * g + FC * j + f, 1)].to_broadcast([P, P]),
                                       left_outT[:], start=False, stop=True)
                    mm.then_inc(s["up_done"], 1)

                def down(f):
                    pe.wait_ge(s["hid_done"], FC * n + f + 1)
                    for t in range(TILES_PER_GROUP):
                        if mixed and f == 0 and (g or e is None):
                            pe.wait_ge(s["acc_done"], TILES_PER_GROUP * (n - 1) + t + 1)
                        toks = slice(t * P, (t + 1) * P)
                        mm = three_products(pe, ps_down[t][:], hid_hi[:, f, toks], hid_lo[:, f, toks],
                                            down_hi[par][:, f, :], down_lo[par][:, f, :], f == 0, f == FC - 1)
                        if f == FC - 1:
                            mm.then_inc(s["down_done"], 1)

                def lead(step, t):
                    if ahead is not None:
                        step(ahead + t)

                up(0)
                lead(lead_turn, 0)
                up(1)
                lead(lead_logits, 0)
                lead(lead_turn, 1)
                up(2)
                lead(lead_logits, 1)
                lead(lead_turn, 2)
                down(0)
                lead(lead_logits, 2)
                lead(lead_turn, 3)
                up(3)
                lead(lead_logits, 3)
                down(1)
                down(2)
                down(3)

            def first_subset(n, sub, e):
                lead_turn(TILES * n)
                for t in range(TILES_PER_GROUP):
                    if t + 1 < TILES_PER_GROUP:
                        lead_turn(TILES * n + t + 1)
                    lead_logits(TILES * n + t)
                pe.wait_ge(s["logit_done"], TILES * n + TILES_PER_GROUP)
                for g in range(GROUPS):
                    if e is None and g:
                        left_transposed(g)
                    group(sub, 0, g, e, True, TILES * n + TILES_PER_GROUP * (g + 1) if g < GROUPS - 1 else None)

            pe.wait_ge(s["small_in"], 16 * SMALL)
            first_subset(0, 0, 0)
            pe.wait_ge(s["logit_done"], TILES)
            sub_loops(pe, group)
            if experts_only:
                return
            first_subset(1, MOE_SUBS, None)
            ffn_loops(pe, group)

        @block.scalar
        def _(act):
            copy = ACT.Copy

            def split_weights(sub, c, par):
                at = bass.ds(c, 1)
                act.wait_ge(s["w_in"], 32 * sub + 32)
                act.activation(up_hi[par][:, at, :], up_raw[:, at, :], copy)
                act.activation(down_hi[par][:, at, :], down_raw[:, at, :], copy).then_inc(s["w_hi_done"], 1)

            def deviations(tiles):
                act.activation(rstd[:, tiles], mean_var[:, tiles, 1], ACT.Sqrt, bias=eps[:]).then_inc(s["std_done"], 1)

            def group_deviations(g):
                act.wait_ge(s["aggr_done"], TILES_PER_GROUP * (g + 1))
                deviations(slice(TILES_PER_GROUP * g, TILES_PER_GROUP * (g + 1)))

            def lead(i):
                g, t = divmod(i % TILES, TILES_PER_GROUP)
                act.wait_ge(s["xT_ps"], i + 1)
                before = i - 2 if i % TILES <= TILES_PER_GROUP else i - 1
                if before >= 0:
                    act.wait_ge(s["h_lo_done"], before + 1)
                    act.wait_ge(s["logit_ps"], before + 1)
                if i < TILES:
                    for c in range(DC):
                        a = act.activation(h_raw(i)[:, c, :], lead_bank(i)[:, c * P:(c + 1) * P], ACT.Identity,
                                           bias=ln_b[:, c:c + 1], scale=ln_g[:, c:c + 1])
                else:
                    a = act.activation(h_raw(i), lead_bank(i)[:].rearrange("p (c n) -> p c n", c=DC), copy)
                a.then_inc(s["h_raw_done"], 1)
                act.wait_ge(s["h_raw_done"], i + 1)
                act.activation(h_hi[:, DC * g:DC * (g + 1), t * P:(t + 1) * P], h_raw(i), copy).then_inc(s["h_hi_done"], 1)

            def router_exp(n, g):
                tiles = slice(TILES_PER_GROUP * g, TILES_PER_GROUP * (g + 1))
                act.wait_ge(s["soft_step"], 4 * (GROUPS * n + g) + 2)
                z = prob[:] if n else share[:, tiles, :]
                act.activation(z, z, ACT.Exp).then_inc(s["exp_done"], 1)

            def left_transposed(g):
                act.wait_ge(s["left_ps"], g + 1)
                act.activation(left_outT[SEQ * g:SEQ * g + BLOCKS, :], ps_up[3][0:BLOCKS, :], copy).then_inc(s["leftT_done"], 1)

            def group(sub, j, g, e, mixed=False, ahead=None):
                n = GROUPS * sub + g

                def hidden(f):
                    act.wait_ge(s["up_done"], FC * n + f + 1)
                    func = ACT.Relu if e is None else ACT.Silu
                    bias = up_bias[:, bass.ds(FC * sub + f, 1)]
                    bank = up_bank(f, mixed)
                    if mixed and f >= 2:
                        act.wait_ge(s["hid_done"], FC * n + f - 1)
                    act.activation(hid[:, f % 2 if mixed else f, :], bank[:], func, bias=bias)
                    act.activation(hid_hi[:, f, :], bank[:], func, bias=bias).then_inc(s["hid_hi_done"], 1)

                def lead_tile(t):
                    if ahead is not None:
                        lead(ahead + t)

                if mixed:
                    act.wait_ge(s["h_lo_done"], TILES * (e is None) + TILES_PER_GROUP)
                hidden(0)
                lead_tile(0)
                hidden(1)
                lead_tile(1)
                if not sub_is_last(sub):
                    if mixed and g == GROUPS - 1:
                        act.wait_ge(s["logit_ps"], TILES * (1 + (e is None)))
                        act.wait_ge(s["h_lo_done"], TILES * (1 + (e is None)))
                    split_weights(sub + 1, g, 1 - j % 2)
                hidden(2)
                lead_tile(2)
                lead_tile(3)
                hidden(3)
                if ahead is not None:
                    router_exp(ahead // TILES, g + 1)
                if mixed and e is None and g < GROUPS - 2:
                    group_deviations(g + 2)

            def sub_is_last(sub):
                return isinstance(sub, int) and sub == SUBS - 1

            def first_subset(n, sub, e):
                for t in range(TILES_PER_GROUP):
                    lead(TILES * n + t)
                    if n == 0:
                        split_weights(0, t, 0)
                if n:
                    group_deviations(1)
                router_exp(n, 0)
                for g in range(GROUPS):
                    if e is None:
                        left_transposed(g)
                    group(sub, 0, g, e, True, TILES * n + TILES_PER_GROUP * (g + 1) if g < GROUPS - 1 else None)

            act.wait_ge(s["eps_set"], 1)
            deviations(slice(0, TILES))
            act.wait_ge(s["small_in"], 16 * SMALL)
            act.activation(shut[:], shut_in[:].rearrange("p g b -> p (g b)"), copy)
            first_subset(0, 0, 0)
            sub_loops(act, group)
            if experts_only:
                return
            act.wait_ge(s["leftT_zero"], 1)
            group_deviations(0)
            first_subset(1, MOE_SUBS, None)
            ffn_loops(act, group)

        @block.vector
        def _(dve):
            dve.memset(eps[:], EPS).then_inc(s["eps_set"], 1)

            def split_weights(sub, c, par):
                at = bass.ds(c, 1)
                dve.wait_ge(s["w_hi_done"], DC * sub + c + 1)
                dve.tensor_tensor(up_lo[par][:, at, :], up_raw[:, at, :], up_hi[par][:, at, :].bitcast(F32), ALU.subtract)
                dve.tensor_tensor(down_lo[par][:, at, :], down_raw[:, at, :], down_hi[par][:, at, :].bitcast(F32), ALU.subtract).then_inc(s["w_split"], 1)

            def deviations(tiles, count):
                dve.wait_ge(s["std_done"], count)
                dve.reciprocal(rstd[:, tiles], rstd[:, tiles]).then_inc(s["rstd_done"], 1)

            def statistics(t):
                if t:
                    dve.wait_ge(s["aggr_done"], t)
                dve.bn_stats(stats[:], x[:, t, :]).then_inc(s["stats_done"], 1)
                dve.wait_ge(s["stats_done"], t + 1)
                dve.bn_aggr(mean_var[:, t, :], stats[:]).then_inc(s["aggr_done"], 1)

            def norm(i):
                n, t = divmod(i, TILES)
                if n == 0:
                    dve.wait_ge(s["rstd_done"], 1)
                    dve.wait_ge(*x2_arrival(i))
                    src = xn(i)
                else:
                    dve.wait_ge(s["rstd_done"], 2 + t // TILES_PER_GROUP)
                    dve.wait_ge(s["xT_ps"], i - 1 if t <= TILES_PER_GROUP else i)
                    src = x[:, t, :]
                dve.tensor_scalar(xn(i), src, mean_var[:, t, 0:1], rstd[:, t:t + 1], ALU.subtract, ALU.mult).then_inc(s["xn_done"], 1)

            def lead(i):
                following = norm if (i + 1) % TILES_PER_GROUP else None
                early = i % TILES < TILES_PER_GROUP
                if following and early:
                    following(i + 1)
                g, t = divmod(i % TILES, TILES_PER_GROUP)
                dve.wait_ge(s["h_hi_done"], i + 1)
                rows = (slice(None), slice(DC * g, DC * (g + 1)), slice(t * P, (t + 1) * P))
                dve.tensor_tensor(h_lo[rows], h_raw(i), h_hi[rows].bitcast(F32), ALU.subtract).then_inc(s["h_lo_done"], 1)
                if following and not early:
                    following(i + 1)

            def logits(i):
                n, t = divmod(i, TILES)
                dve.wait_ge(s["logit_ps"], i + 1)
                if n == 0:
                    dve.tensor_copy(share[:, t, :], lead_bank(i)[:, 0:EXPERTS]).then_inc(s["logit_done"], 1)
                else:
                    dve.tensor_tensor(prob[:, t % TILES_PER_GROUP, :], lead_bank(i)[:, 0:BLOCKS], b_router[:], ALU.add).then_inc(s["logit_done"], 1)

            def softmax(n, g):
                tiles = slice(TILES_PER_GROUP * g, TILES_PER_GROUP * (g + 1))
                z = prob[:] if n else share[:, tiles, :]
                step = 4 * (GROUPS * n + g)
                wide = [P, TILES_PER_GROUP, (EXPERTS, BLOCKS)[n]]
                dve.wait_ge(s["logit_done"], TILES * n + TILES_PER_GROUP * (g + 1))
                dve.tensor_reduce(soft[:, 0, tiles], z, AX.X, ALU.max).then_inc(s["soft_step"], 1)
                dve.wait_ge(s["soft_step"], step + 1)
                dve.tensor_tensor(z, z, soft[:, 0, tiles].unsqueeze(2).to_broadcast(wide), ALU.subtract).then_inc(s["soft_step"], 1)
                dve.wait_ge(s["exp_done"], GROUPS * n + g + 1)
                dve.tensor_reduce(soft[:, 1, tiles], z, AX.X, ALU.add).then_inc(s["soft_step"], 1)
                dve.wait_ge(s["soft_step"], step + 3)
                dve.reciprocal(soft[:, 1, tiles], soft[:, 1, tiles]).then_inc(s["soft_step"], 1)
                dve.wait_ge(s["soft_step"], step + 4)
                rec = soft[:, 1, tiles].unsqueeze(2).to_broadcast(wide)
                if n == 0:
                    dve.tensor_tensor(share_by[:, :, tiles].rearrange("p e t -> p t e"), z, rec, ALU.mult).then_inc(s["share_done"], 1)
                    return
                base = TOP_STEPS * g
                dve.tensor_tensor(z, z, rec, ALU.mult).then_inc(s["top_done"], 1)
                dve.wait_ge(s["top_done"], base + 1)
                for u in range(TILES_PER_GROUP):
                    a = dve.max(best[:, u, :], z[:, u, :])
                a.then_inc(s["top_done"], 1)
                dve.wait_ge(s["top_done"], base + 2)
                for u in range(TILES_PER_GROUP):
                    a = dve.max_index(best_at[:, u, :], best[:, u, :], z[:, u, :])
                a.then_inc(s["top_done"], 1)
                dve.wait_ge(s["top_done"], base + 3)
                dve.tensor_copy(spot[:], best_at[:]).then_inc(s["top_done"], 1)
                dve.wait_ge(s["top_done"], base + 4)
                dve.tensor_tensor(chosen[:], spot[:, :, 0:TOP_K].unsqueeze(2).to_broadcast([P, TILES_PER_GROUP, BLOCKS, TOP_K]),
                                  block_no[:].unsqueeze(1).unsqueeze(3).to_broadcast([P, TILES_PER_GROUP, BLOCKS, TOP_K]), ALU.is_equal).then_inc(s["top_done"], 1)
                dve.wait_ge(s["top_done"], base + 5)
                dve.tensor_reduce(z, chosen[:], AX.X, ALU.add).then_inc(s["top_done"], 1)
                dve.wait_ge(s["top_done"], base + 6)
                dve.tensor_scalar(z, z, -1.0, 1.0, ALU.mult, ALU.add).then_inc(s["out_left"], 1)

            TOP_STEPS = 6

            def group(sub, j, g, e, mixed=False, ahead=None):
                n = GROUPS * sub + g

                def hidden_lo(f):
                    dve.wait_ge(s["hid_hi_done"], FC * n + f + 1)
                    dve.tensor_tensor(hid_lo[:, f, :], hid[:, f % 2 if mixed else f, :], hid_hi[:, f, :].bitcast(F32), ALU.subtract).then_inc(s["hid_done"], 1)

                def led(step, t):
                    if ahead is not None:
                        step(ahead + t)

                hidden_lo(0)
                led(lead, 0)
                led(logits, 0)
                hidden_lo(1)
                led(lead, 1)
                led(logits, 1)
                if not (isinstance(sub, int) and sub == SUBS - 1):
                    split_weights(sub + 1, g, 1 - j % 2)
                hidden_lo(2)
                led(lead, 2)
                led(logits, 2)
                led(lead, 3)
                led(logits, 3)
                hidden_lo(3)
                if ahead is not None:
                    softmax(ahead // TILES, g + 1)
                if mixed and g < GROUPS - 2:
                    tiles = range(TILES_PER_GROUP * (g + 2), TILES_PER_GROUP * (g + 3))
                    if e is None:
                        for t in tiles:
                            statistics(t)
                        deviations(slice(tiles[0], tiles[-1] + 1), 1 + g + 3)
                    norm(TILES * (e is None) + tiles[0])
                if mixed and e is not None:
                    dve.wait_ge(s["small_in"], 16 * SMALL)
                    dve.wait_ge(s["share_done"], g + 1)
                for t in range(TILES_PER_GROUP):
                    tile = TILES_PER_GROUP * g + t
                    row = x[:, bass.ds(tile, 1), :]
                    if j == 0:
                        if e is None:
                            dve.wait_ge(s["b2_in"], 16 * EXPERTS)
                            dve.tensor_tensor(row, down_bias[:].unsqueeze(1), row, ALU.add).then_inc(s["b2_used"], 1)
                            dve.wait_ge(s["b2_used"], TILES * EXPERTS + tile + 1)
                        else:
                            if not mixed:
                                dve.wait_ge(s["b2_in"], 16 * e)
                            dve.scalar_tensor_tensor(row, down_bias[:].unsqueeze(1), share_by[:, bass.ds(e, 1), bass.ds(tile, 1)].rearrange("p a b -> p (a b)"), row, ALU.mult, ALU.add).then_inc(s["b2_used"], 1)
                            dve.wait_ge(s["b2_used"], TILES * e + tile + 1)
                    dve.wait_ge(s["down_done"], TILES_PER_GROUP * n + t + 1)
                    ps = ps_down[t][:].unsqueeze(1)
                    if e is None:
                        a = dve.tensor_tensor(row, ps, row, ALU.add)
                    else:
                        a = dve.scalar_tensor_tensor(row, ps, share_by[:, bass.ds(e, 1), bass.ds(tile, 1)].rearrange("p a b -> p (a b)"), row, ALU.mult, ALU.add)
                    a.then_inc(s["acc_done"], 1)

            def first_subset(n, sub, e):
                norm(TILES * n)
                for t in range(TILES_PER_GROUP):
                    lead(TILES * n + t)
                    logits(TILES * n + t)
                    if n:
                        statistics(TILES_PER_GROUP + t)
                    else:
                        split_weights(0, t, 0)
                softmax(n, 0)
                if n:
                    deviations(slice(TILES_PER_GROUP, 2 * TILES_PER_GROUP), 3)
                norm(TILES * n + TILES_PER_GROUP)
                for g in range(GROUPS):
                    group(sub, 0, g, e, True, TILES * n + TILES_PER_GROUP * (g + 1) if g < GROUPS - 1 else None)

            deviations(slice(0, TILES), 1)
            first_subset(0, 0, 0)
            sub_loops(dve, group)
            if experts_only:
                return
            dve.wait_ge(s["acc_done"], TILES * MOE_SUBS)
            for t in range(TILES_PER_GROUP):
                statistics(t)
            deviations(slice(0, TILES_PER_GROUP), 2)
            first_subset(1, MOE_SUBS, None)
            ffn_loops(dve, group)


def build(nc, dram, out, phases=4):
    with ExitStack() as stack:
        fr = Frame(nc, stack)
        dram = {**dram, "x2": nc.dram_tensor("x2_scratch", [TILES, P, D], F32, kind="Internal").ap()}
        keep = {
            "x": fr.sbuf("x_res", [P, TILES, D]),
            "r_hi": fr.sbuf("r_hi", [P, FEAT_CHUNKS, D], F32R),
            "r_lo": fr.sbuf("r_lo", [P, FEAT_CHUNKS, D], F32R),
            "mean_var": fr.sbuf("x2_mean_var", [P, TILES, 2]),
            "ident": fr.sbuf("identity", [P, P]),
        }
        cross_attention(nc, dram, keep)
        if phases == 1:
            dump(nc, keep["x"], out)
            return
        linear_attention(nc, dram, keep)
        if phases == 2:
            dump(nc, keep["x"], out)
            return
        feed_forwards(nc, dram, keep, out, phases == 3)


def dump(nc, x, out):
    with nc.semaphore("dump") as s, nc.Block() as block:
        @block.sync
        def _(sp):
            sp.dma_start(out.rearrange("(t p) d -> p t d", p=P), x[:]).then_inc(s, 16)
            sp.wait_ge(s, 16)


def layouts(v):
    c = np.ascontiguousarray
    ctx = v["ctx_1024"]
    tiles = ctx.reshape(TILES, PER_TILE, CTX, D)
    full = CTX_CHUNKS * P
    a = {
        "x": c(v["x"].reshape(TOKENS, D)),
        "ctxT": c(tiles.reshape(TILES, PER_TILE, CTX, DC, P).transpose(0, 4, 3, 1, 2)),
        "ctxN": c(tiles[:, :, :full].reshape(TILES, PER_TILE, CTX_CHUNKS, P, D).transpose(0, 3, 1, 2, 4)),
        "ctxR": c(tiles[:, :, full]),
        "w_sim": c(v["L0_xattn_w_sim"].reshape(3, DC, P).transpose(2, 0, 1)),
        "b_sim": c(v["L0_xattn_b_sim"]),
        "W_qv": c(v["L0_xattn_W_qv"]),
        "b_qv": c(v["L0_xattn_b_qv"]),
        "ident": np.eye(P, dtype=np.float32),
        "seq_of": np.repeat(np.eye(PER_TILE, dtype=np.float32), SEQ, axis=0),
    }
    pos = np.arange(SEQ, dtype=np.float32)
    inv_freq = np.float32(1.0) / np.float32(10000.0) ** (np.arange(0, HEAD, 2, dtype=np.float32) / np.float32(HEAD))
    theta = pos[:, None] * inv_freq[None, :].astype(np.float32)
    pair = np.arange(P) % HEAD // 2
    sign = np.where(np.arange(P) % 2 == 0, -1.0, 1.0).astype(np.float32)
    at = np.arange(P)
    qkv = v["L0_attn_w_qkv"].reshape(3, D, D)
    a |= {
        "attn_w": c(np.stack([v["L0_attn_w_pw"], qkv[0], qkv[1], qkv[2], v["L0_attn_w_gate"], v["L0_attn_w_o"]]).transpose(0, 2, 1)),
        "cos": c(np.cos(theta).astype(np.float32).T[pair]),
        "sin": c(np.sin(theta).astype(np.float32).T[pair] * sign[:, None]),
        "causal": ((at[:, None] // SEQ == at[None, :] // SEQ) & (at[:, None] <= at[None, :])).astype(np.float32),
        "w_dw": c(v["L0_attn_w_dw"].reshape(DC, P, 3).transpose(1, 0, 2)),
        "ones_strip": np.tile((np.arange(HEAD + DC - 1) == DC - 1).astype(np.float32), (P, 1)),
        "spread": (at[:, None, None] == at // HEAD * HEAD + np.arange(DC)[:, None]).astype(np.float32),
        "b_gate": c(v["L0_attn_b_gate"].reshape(DC, P).T),
    }
    moe_up = v["L0_attn_w1"].reshape(MOE_SUBS, SUB, DC, P)
    ffn_up = v["L0_ffn_w1"].reshape(FFN_SUBS, SUB, DC, P)
    moe_down = v["L0_attn_w2"].reshape(EXPERTS, D, SUBS_PER_EXPERT, FC, P).transpose(0, 2, 4, 3, 1).reshape(MOE_SUBS, P, FC, D)
    ffn_down = v["L0_ffn_w2"].reshape(D, FFN_SUBS, FC, P).transpose(1, 3, 2, 0)
    a |= {
        "up_w": c(np.concatenate([moe_up, ffn_up]).transpose(0, 3, 2, 1)),
        "down_w": c(np.concatenate([moe_down, ffn_down])),
        "up_bias": c(np.concatenate([v["L0_attn_b1"].reshape(-1), v["L0_ffn_b1"]]).reshape(SUBS * FC, P).T),
        "down_bias": c(np.concatenate([v["L0_attn_b2"], v["L0_ffn_b2"][None]])),
        "ln_g": c(v["L0_attn_ln_g"].reshape(DC, P).T),
        "ln_b": c(v["L0_attn_ln_b"].reshape(DC, P).T),
        "w_moe": c(v["L0_attn_w_moe_gate"].reshape(EXPERTS, DC, P).transpose(2, 1, 0)),
        "w_router": c(v["L0_ffn_w_router"].reshape(DC, P, BLOCKS).transpose(1, 0, 2)),
        "b_router": c(v["L0_ffn_b_router"]),
        "shut": c((np.arange(P)[:, None, None] == SEQ * np.arange(GROUPS)[:, None] + np.arange(BLOCKS)).astype(np.float32) * np.float32(SHUT)),
        "block_no": np.tile(np.arange(BLOCKS, dtype=np.float32), (P, 1)),
    }
    return a


def kernel(**inputs):
    import concourse.bacc as bacc
    from concourse.bass_utils import run_bass_kernel_spmd

    arrays = layouts({name: np.asarray(a) for name, a in inputs.items()})
    nc = bacc.Bacc("TRN2", target_bir_lowering=False, num_devices=1)
    dram = {name: nc.dram_tensor(name, a.shape, mybir.dt.from_np(a.dtype), kind="ExternalInput").ap()
            for name, a in arrays.items()}
    out = nc.dram_tensor("out", (TOKENS, D), F32, kind="ExternalOutput").ap()
    build(nc, dram, out)
    r = run_bass_kernel_spmd(nc, [arrays], core_ids=[0])
    return r.results[0]["out"].reshape(BATCH, SEQ, D)
```

```python
from contextlib import ExitStack

import concourse.bass as bass
import numpy as np
from concourse import mybir

F32 = mybir.dt.float32
F32R = mybir.dt.float32r
BF16 = mybir.dt.bfloat16
U32 = mybir.dt.uint32
ALU = mybir.AluOpType
ACT = mybir.ActivationFunctionType
AX = mybir.AxisListType

P = 128
D = 512
DC = D // P
SEQ = 32
BATCH = 64
TOKENS = BATCH * SEQ
TILES = TOKENS // P
PER_TILE = P // SEQ
CTX = 257
CTX_CHUNKS = CTX // P
GROUP = 512
GROUPS = TOKENS // GROUP
TILES_PER_GROUP = GROUP // P
FEATS = 4 * D
FEAT_CHUNKS = FEATS // P
HEADS = 16
HEAD = D // HEADS
HEADS_PER_CHUNK = P // HEAD
CHUNK = 256
CHUNKS = TOKENS // CHUNK
CT = CHUNK // P
CSEQ = CHUNK // SEQ
EXPERTS = 4
HIDDEN = 2048
SUB = 512
FC = SUB // P
SUBS_PER_EXPERT = HIDDEN // SUB
MOE_SUBS = EXPERTS * SUBS_PER_EXPERT
FFN_SUBS = HIDDEN // SUB
SUBS = MOE_SUBS + FFN_SUBS
BLOCKS = 16
TOP_K = 4
EPS = 1e-5
DEN_EPS = 1e-6
SHUT = -(2.0 ** 127)


class Frame:

    def __init__(self, nc, stack, tag=""):
        self.nc, self.stack, self.tag = nc, stack, tag

    def sbuf(self, name, shape, dt=F32):
        return self.stack.enter_context(self.nc.sbuf_tensor(self.tag + name, shape, dt))

    def psum(self, name, shape=(P, 512)):
        return self.stack.enter_context(self.nc.psum_tensor(self.tag + name, list(shape), F32))

    def sem(self, name):
        return self.stack.enter_context(self.nc.semaphore(self.tag + name))


def three_products(pe, out, w_hi, w_lo, m_hi, m_lo, first, last):
    pe.matmul(out, w_hi, m_hi, start=first, stop=False)
    pe.matmul(out, w_hi, m_lo, start=False, stop=False)
    return pe.matmul(out, w_lo, m_hi, start=False, stop=last)


def staged(keep, n):
    return keep["passing"][:, n % 2 * DC * D:(n % 2 + 1) * DC * D].rearrange("p (k n) -> p k n", n=D)


def cross_attention(nc, dram, keep):
    with ExitStack() as stack:
        fr = Frame(nc, stack, "xa_")
        x, wq_hi, wq_lo = keep["x"], keep["r_hi"], keep["r_lo"]
        ident = keep["ident"]
        ctxT = [fr.sbuf(f"ctxT{i}", [P, DC, PER_TILE, CTX]) for i in range(2)]
        ctxN = [keep["passing"][:].rearrange("p (b c d) -> p b c d", b=PER_TILE, c=CTX_CHUNKS),
                fr.sbuf("ctxN1", [P, PER_TILE, CTX_CHUNKS, D])[:]]
        ctxR = [fr.sbuf(f"ctxR{i}", [PER_TILE, D]) for i in range(2)]
        hcT = [fr.sbuf(f"hcT{i}", [P, DC, P]) for i in range(2)]
        feats = fr.sbuf("feats", [P, FEAT_CHUNKS - DC, P])
        feats_hi = fr.sbuf("feats_hi", [P, FEAT_CHUNKS, P], F32R)
        feats_lo = fr.sbuf("feats_lo", [P, FEAT_CHUNKS, P], F32R)
        xn = [fr.sbuf(f"xn{i}", [P, D]) for i in range(2)]
        hq = fr.sbuf("hq", [P, D])
        sim_w = fr.sbuf("sim_w", [P, DC, P])
        probs = fr.sbuf("probs", [P, CTX])
        probs_rest = fr.sbuf("probs_rest", [P, PER_TILE])
        probsT = fr.sbuf("probsT", [P, CTX_CHUNKS, P])
        probsT_rest = fr.sbuf("probsT_rest", [PER_TILE, P])
        b_qv = fr.sbuf("b_qv", [P, D])
        w_sim = fr.sbuf("w_sim", [P, 3, DC])
        b_sim = fr.sbuf("b_sim", [P, 1])
        seq_of = fr.sbuf("seq_of", [P, PER_TILE])
        stats = fr.sbuf("stats", [P, 6])
        mean_var = fr.sbuf("mean_var", [P, TILES, 2])
        rstd = fr.sbuf("rstd", [P, TILES])
        neg_max = fr.sbuf("neg_max", [P, 1])
        row_sum = fr.sbuf("row_sum", [P, 1])
        row_rec = fr.sbuf("row_rec", [P, 1])
        top = fr.sbuf("top", [P, 1])
        top_wide = fr.sbuf("top_wide", [P, SEQ])
        top_seq = fr.sbuf("top_seq", [P, SEQ])
        neg_top = fr.sbuf("neg_top", [P, 1])
        top_exp = fr.sbuf("top_exp", [P, SEQ])
        own_exp = fr.sbuf("own_exp", [P, 1])
        top_sum = fr.sbuf("top_sum", [P, 1])
        top_rec = fr.sbuf("top_rec", [P, 1])
        batt = fr.sbuf("batt", [P, PER_TILE])
        bar = fr.sbuf("bar", [P, DC, PER_TILE])
        eps = fr.sbuf("eps", [P, 1])
        x1_stats = fr.sbuf("x1_stats", [P, 6])
        x1_mean_var = fr.sbuf("x1_mean_var", [P, 2])

        ps_t = fr.psum("ps_t")
        ps_sim = fr.psum("ps_sim")
        ps_p = fr.psum("ps_p")
        ps_hq = fr.psum("ps_hq")
        ps_hqt = fr.psum("ps_hqt")
        ps_m = fr.psum("ps_m")
        ps_out = [fr.psum(f"ps_out{i}") for i in range(2)]

        x_in = [fr.sem(f"x_in{g}") for g in range(GROUPS)]
        small_in = fr.sem("small_in")
        wq_in = [fr.sem(f"wq_in{q}") for q in range(4)]
        wq_hi_done = fr.sem("wq_hi_done")
        wq_split = fr.sem("wq_split")
        ctxT_in = [fr.sem(f"ctxT_in{i}") for i in range(2)]
        ctxN_in = [fr.sem(f"ctxN_in{i}") for i in range(2)]
        attn_w_in = fr.sem("attn_w_in")
        x1_stats_done = fr.sem("x1_stats_done")
        x1_aggr_done = fr.sem("x1_aggr_done")
        stats_done = fr.sem("stats_done")
        aggr_done = fr.sem("aggr_done")
        eps_set = fr.sem("eps_set")
        std_done = fr.sem("std_done")
        rstd_done = fr.sem("rstd_done")
        xn_done = fr.sem("xn_done")
        xnT_done = fr.sem("xnT_done")
        hcT_done = fr.sem("hcT_done")
        sim_w_done = fr.sem("sim_w_done")
        sim_done = fr.sem("sim_done")
        neg_max_done = fr.sem("neg_max_done")
        probs_done = fr.sem("probs_done")
        rest_done = fr.sem("rest_done")
        probsT_ps = fr.sem("probsT_ps")
        probsT_done = fr.sem("probsT_done")
        hq_ps = fr.sem("hq_ps")
        hq_done = fr.sem("hq_done")
        hqT_ps = fr.sem("hqT_ps")
        hqT_done = fr.sem("hqT_done")
        top_step = fr.sem("top_step")
        own_done = fr.sem("own_done")
        batt_done = fr.sem("batt_done")
        bar_ps = fr.sem("bar_ps")
        bar_done = fr.sem("bar_done")
        prod_done = fr.sem("prod_done")
        hi_done = fr.sem("hi_done")
        split_done = fr.sem("split_done")
        quarter_used = fr.sem("quarter_used")
        out_done = fr.sem("out_done")
        rec_done = fr.sem("rec_done")
        bias_done = fr.sem("bias_done")
        x_done = fr.sem("x_done")
        block = stack.enter_context(nc.Block())

        QUARTERS = 4
        halves = [ctxT[1][:].rearrange("p c b j -> p (c b j)"), ctxN[1].rearrange("p b c d -> p (b c d)")]
        wq_raw = [halves[q // 2][:, q % 2 * DC * D:(q % 2 + 1) * DC * D].rearrange("p (k n) -> p k n", n=D) for q in range(QUARTERS)]
        w1_at = CTX_CHUNKS * P + P

        def raw(q, par):
            return hcT[par][:] if q == 0 else feats[:, DC * (q - 1):DC * q, :]

        @block.sync
        def _(sp):
            sp.dma_start(x[:, 0:TILES_PER_GROUP, :],
                         dram["x"][0:GROUP, :].rearrange("(t p) d -> p t d", p=P)).then_inc(x_in[0], 16)
            sp.dma_start(ident[:], dram["ident"]).then_inc(small_in, 16)
            sp.dma_start(w_sim[:], dram["w_sim"]).then_inc(small_in, 16)
            sp.dma_start(b_sim[:], dram["b_sim"].partition_broadcast(P)).then_inc(small_in, 16)
            sp.dma_start(seq_of[:], dram["seq_of"]).then_inc(small_in, 16)
            sp.dma_start(b_qv[:], dram["b_qv"].partition_broadcast(P)).then_inc(small_in, 16)

            def load_ctxT(t, par):
                sp.dma_start(ctxT[par][:], dram["ctxT"][bass.ds(t, 1)].rearrange("o p c b j -> p (o c) b j")).then_inc(ctxT_in[par], 16)

            def load_ctxN(t, par):
                sp.dma_start(ctxN[par], dram["ctxN"][bass.ds(t, 1)].rearrange("o p b c d -> p (o b) c d")).then_inc(ctxN_in[par], 16)
                sp.dma_start(ctxR[par][:], dram["ctxR"][bass.ds(t, 1)].rearrange("o b d -> (o b) d")).then_inc(ctxN_in[par], 16)

            load_ctxT(0, 0)
            load_ctxN(0, 0)
            for q in range(QUARTERS):
                sp.dma_start(wq_raw[q], dram["W_qv"][q * D:(q + 1) * D, :].rearrange("(k p) n -> p k n", p=P)).then_inc(wq_in[q], 16)

            def load_x(g):
                rows = slice(g * GROUP, (g + 1) * GROUP)
                sp.dma_start(x[:, g * TILES_PER_GROUP:(g + 1) * TILES_PER_GROUP, :],
                             dram["x"][rows, :].rearrange("(t p) d -> p t d", p=P)).then_inc(x_in[g], 16)

            load_x(1)
            sp.wait_ge(wq_split, QUARTERS // 2)
            load_ctxT(1, 1)
            load_x(2)
            sp.wait_ge(wq_split, QUARTERS)
            load_ctxN(1, 1)
            load_x(3)
            with sp.Fori(0, TILES // 2 - 1) as pair:
                for par in range(2):
                    sp.wait_ge(hq_ps, 2 * pair + par + 1)
                    load_ctxT(2 * pair + par + 2, par)
                    load_ctxN(2 * pair + par + 2, par)
            sp.wait_ge(hq_ps, TILES - 1)
            for n in range(2):
                sp.dma_start(staged(keep, n), dram["attn_w"][n].rearrange("(k p) n -> p k n", p=P)).then_inc(attn_w_in, 16)
            sp.wait_ge(attn_w_in, 32)

        def in_pairs(eng, tile):
            tile(0, 0, True, False)
            tile(1, 1, False, False)
            with eng.Fori(1, TILES // 2 - 1) as pair:
                tile(2 * pair, 0, False, False)
                tile(2 * pair + 1, 1, False, False)
            tile(TILES - 2, 0, False, False)
            tile(TILES - 1, 1, False, True)

        def is_second(t):
            return isinstance(t, int) and t == 1

        @block.tensor
        def _(pe):
            pe.wait_ge(small_in, 16 * 5)

            def project(t, par, q, first=False):
                pe.wait_ge(split_done, QUARTERS * t + q + 1)
                if first:
                    pe.wait_ge(wq_split, QUARTERS if q else 1)
                for k in range(DC * q, DC * q + DC):
                    last = three_products(pe, ps_out[par][:], feats_hi[:, k, :], feats_lo[:, k, :],
                                          wq_hi[:, k, :], wq_lo[:, k, :], k == 0, k == FEAT_CHUNKS - 1)
                last.then_inc(quarter_used, 1)

            def norm_transposed(t, par):
                pe.wait_ge(xn_done, t + 1)
                for c in range(DC):
                    last = pe.transpose(ps_t[:, c * P:(c + 1) * P], xn[par][:, c * P:(c + 1) * P], ident[:])
                last.then_inc(xnT_done, 1)

            def similarities(t, par):
                pe.wait_ge(sim_w_done, t + 1)
                pe.wait_ge(ctxT_in[par], 8 * (t - par) + 16)
                for c in range(DC):
                    for b in range(PER_TILE):
                        rows = slice(b * SEQ, (b + 1) * SEQ)
                        pe.matmul(ps_sim[rows, 0:CTX], sim_w[:, c, rows], ctxT[par][:, c, b, :],
                                  start=c == 0, stop=c == DC - 1)
                for c in range(DC):
                    last = pe.matmul(ps_p[:, w1_at:w1_at + 1], hcT[par][:, c, :], w_sim[:, 0, c:c + 1],
                                     start=c == 0, stop=c == DC - 1)
                last.then_inc(sim_done, 1)

            norm_transposed(0, 0)
            similarities(0, 0)

            def tile(t, par, first, last_tile):
                if not first:
                    project(t - 1, 1 - par, 1)
                pe.wait_ge(rest_done, t + 1)
                for c in range(CTX_CHUNKS):
                    pe.transpose(ps_p[:, c * P:(c + 1) * P], probs[:, c * P:(c + 1) * P], ident[:])
                pe.transpose(ps_p[0:PER_TILE, CTX_CHUNKS * P:(CTX_CHUNKS + 1) * P], probs_rest[:], ident[:]).then_inc(probsT_ps, 1)
                if not first:
                    project(t - 1, 1 - par, 2)
                    project(t - 1, 1 - par, 3)
                pe.wait_ge(probsT_done, t + 1)
                pe.wait_ge(ctxN_in[par], 16 * (t - par) + 32)
                for c in range(CTX_CHUNKS):
                    for b in range(PER_TILE):
                        rows = slice(b * SEQ, (b + 1) * SEQ)
                        pe.matmul(ps_hq[rows, :], probsT[:, c, rows], ctxN[par][:, b, c, :],
                                  start=c == 0, stop=False)
                pe.matmul(ps_hq[:], probsT_rest[:], ctxR[par][:], start=False, stop=True).then_inc(hq_ps, 1)
                if not last_tile:
                    norm_transposed(t + 1, 1 - par)
                project(t, par, 0, first)
                pe.wait_ge(hq_done, t + 1)
                for c in range(DC):
                    last = pe.transpose(ps_hqt[:, c * P:(c + 1) * P], hq[:, c * P:(c + 1) * P], ident[:])
                last.then_inc(hqT_ps, 1)
                pe.wait_ge(batt_done, t + 1)
                for c in range(DC):
                    last = pe.matmul(ps_m[:, 4 * c:4 * c + 4], xn[par][:, c * P:(c + 1) * P], batt[:], start=True, stop=True)
                last.then_inc(bar_ps, 1)
                if not last_tile:
                    similarities(t + 1, 1 - par)
                if first:
                    pe.wait_ge(wq_split, QUARTERS)

            in_pairs(pe, tile)
            for q in range(1, QUARTERS):
                project(TILES - 1, 1, q)

        @block.scalar
        def _(act):
            def deviations(tiles):
                act.wait_ge(aggr_done, tiles.stop)
                act.activation(rstd[:, tiles], mean_var[:, tiles, 1], ACT.Sqrt, bias=eps[:]).then_inc(std_done, 1)

            def split_hi(t, par, q, fresh=False):
                if not fresh:
                    act.wait_ge(quarter_used, QUARTERS * (t - 1) + q + 1)
                act.activation(feats_hi[:, DC * q:DC * (q + 1), :], raw(q, par), ACT.Copy).then_inc(hi_done, 1)

            def norm_copy(t, par):
                act.wait_ge(xnT_done, t + 1)
                act.activation(hcT[par][:], ps_t[:].rearrange("p (c n) -> p c n", c=DC), ACT.Copy).then_inc(hcT_done, 1)

            act.wait_ge(eps_set, 1)
            deviations(slice(0, TILES_PER_GROUP))
            norm_copy(0, 0)
            act.wait_ge(hcT_done, 1)
            split_hi(0, 0, 0, True)

            def tile(t, par, first, last_tile):
                act.wait_ge(neg_max_done, t + 1)
                act.activation(probs[:], ps_sim[:, 0:CTX], ACT.Exp, bias=neg_max[:], accum_out=row_sum[:]).then_inc(probs_done, 1)
                act.wait_ge(probsT_ps, t + 1)
                act.activation(probsT[:], ps_p[:, 0:CTX_CHUNKS * P].rearrange("p (c n) -> p c n", c=CTX_CHUNKS), ACT.Copy)
                act.activation(probsT_rest[:], ps_p[0:PER_TILE, CTX_CHUNKS * P:(CTX_CHUNKS + 1) * P], ACT.Copy).then_inc(probsT_done, 1)
                act.wait_ge(top_step, 4 * t + 4)
                act.activation(top_exp[:], top_seq[:], ACT.Exp, bias=neg_top[:], accum_out=top_sum[:]).then_inc(own_done, 1)
                act.activation(own_exp[:], top[:], ACT.Exp, bias=neg_top[:]).then_inc(own_done, 1)
                act.wait_ge(hq_ps, t + 1)
                act.activation(hq[:], ps_hq[:], ACT.Copy, scale=row_rec[:]).then_inc(hq_done, 1)
                if not first:
                    act.wait_ge(split_done, QUARTERS * t)
                if not last_tile:
                    norm_copy(t + 1, 1 - par)
                if first:
                    for q in range(QUARTERS):
                        act.wait_ge(wq_in[q], 16)
                        act.activation(wq_hi[:, DC * q:DC * (q + 1), :], wq_raw[q], ACT.Copy).then_inc(wq_hi_done, 1)
                act.wait_ge(hqT_ps, t + 1)
                act.activation(raw(1, par), ps_hqt[:].rearrange("p (c n) -> p c n", c=DC), ACT.Copy).then_inc(hqT_done, 1)
                act.wait_ge(hqT_done, t + 1)
                split_hi(t, par, 1, first)
                act.wait_ge(bar_ps, t + 1)
                act.activation(bar[:], ps_m[:, 0:DC * PER_TILE].rearrange("p (c b) -> p c b", c=DC), ACT.Copy).then_inc(bar_done, 1)
                act.wait_ge(prod_done, 2 * t + 1)
                split_hi(t, par, 2, first)
                act.wait_ge(prod_done, 2 * t + 2)
                split_hi(t, par, 3, first)
                if not last_tile:
                    split_hi(t + 1, 1 - par, 0)
                if is_second(t):
                    deviations(slice(TILES_PER_GROUP, TILES))

            in_pairs(act, tile)

        @block.vector
        def _(dve):
            dve.memset(eps[:], EPS).then_inc(eps_set, 1)

            def statistics(g):
                dve.wait_ge(x_in[g], 16)
                for t in range(g * TILES_PER_GROUP, (g + 1) * TILES_PER_GROUP):
                    if t:
                        dve.wait_ge(aggr_done, t)
                    dve.bn_stats(stats[:], x[:, t, :]).then_inc(stats_done, 1)
                    dve.wait_ge(stats_done, t + 1)
                    dve.bn_aggr(mean_var[:, t, :], stats[:]).then_inc(aggr_done, 1)

            def deviations(tiles, count):
                dve.wait_ge(std_done, count)
                dve.reciprocal(rstd[:, tiles], rstd[:, tiles]).then_inc(rstd_done, 1)
                dve.wait_ge(rstd_done, count)

            def split_lo(t, par, q):
                dve.wait_ge(hi_done, QUARTERS * t + q + 1)
                quarter = slice(DC * q, DC * (q + 1))
                dve.tensor_tensor(feats_lo[:, quarter, :], raw(q, par), feats_hi[:, quarter, :].bitcast(F32), ALU.subtract).then_inc(split_done, 1)

            def norm(t, par):
                dve.tensor_scalar(xn[par][:].rearrange("p (o n) -> p o n", o=1), x[:, bass.ds(t, 1), :], mean_var[:, bass.ds(t, 1), 0], rstd[:, bass.ds(t, 1)], ALU.subtract, ALU.mult).then_inc(xn_done, 1)
                dve.wait_ge(xn_done, t + 1)
                dve.tensor_tensor(x[:, bass.ds(t, 1), :], x[:, bass.ds(t, 1), :], b_qv[:].rearrange("p (o n) -> p o n", o=1), ALU.add).then_inc(bias_done, 1)

            def weigh(t, par):
                dve.wait_ge(hcT_done, t + 1)
                for c in range(DC):
                    last = dve.tensor_scalar(sim_w[:, c, :], hcT[par][:, c, :], w_sim[:, 2, c:c + 1], w_sim[:, 1, c:c + 1], ALU.mult, ALU.add)
                last.then_inc(sim_w_done, 1)

            def finish(t, par):
                dve.wait_ge(quarter_used, QUARTERS * (t + 1))
                dve.tensor_tensor(x[:, bass.ds(t, 1), :], ps_out[par][:].rearrange("p (o n) -> p o n", o=1), x[:, bass.ds(t, 1), :], ALU.add).then_inc(x_done, 1)

            def statistics_after(t):
                dve.bn_stats(x1_stats[:], x[:, bass.ds(t, 1), :].rearrange("p o n -> p (o n)")).then_inc(x1_stats_done, 1)

            def gather_statistics(t):
                dve.bn_aggr(x1_mean_var[:], x1_stats[:]).then_inc(x1_aggr_done, 1)
                dve.wait_ge(x1_aggr_done, t + 1)
                dve.tensor_copy(keep["mean_var"][:, bass.ds(t, 1), :], x1_mean_var[:].unsqueeze(1))

            statistics(0)
            deviations(slice(0, TILES_PER_GROUP), 1)
            dve.wait_ge(small_in, 16 * 5)
            norm(0, 0)
            weigh(0, 0)
            split_lo(0, 0, 0)

            def tile(t, par, first, last_tile):
                dve.wait_ge(sim_done, t + 1)
                dve.tensor_reduce(neg_max[:], ps_sim[:, 0:CTX], AX.X, ALU.max, negate=True).then_inc(neg_max_done, 1)
                dve.wait_ge(neg_max_done, t + 1)
                dve.scalar_tensor_tensor(top[:], ps_p[:, w1_at:w1_at + 1], b_sim[:], neg_max[:], ALU.add, ALU.subtract).then_inc(top_step, 1)
                dve.wait_ge(probs_done, t + 1)
                dve.reciprocal(row_rec[:], row_sum[:])
                dve.tensor_scalar(probs_rest[:], seq_of[:], probs[:, CTX - 1:CTX], None, ALU.mult).then_inc(rest_done, 1)
                dve.wait_ge(top_step, 4 * t + 1)
                dve.tensor_copy(top_wide[:], top[:].to_broadcast([P, SEQ])).then_inc(top_step, 1)
                dve.wait_ge(top_step, 4 * t + 2)
                dve.transpose(top_seq[:], top_wide[:]).then_inc(top_step, 1)
                dve.wait_ge(top_step, 4 * t + 3)
                dve.tensor_reduce(neg_top[:], top_seq[:], AX.X, ALU.max, negate=True).then_inc(top_step, 1)
                if not last_tile:
                    norm(t + 1, 1 - par)
                dve.wait_ge(own_done, 2 * t + 2)
                dve.reciprocal(top_rec[:], top_sum[:]).then_inc(rec_done, 1)
                dve.wait_ge(rec_done, t + 1)
                dve.tensor_scalar(batt[:], seq_of[:], own_exp[:], top_rec[:], ALU.mult, ALU.mult).then_inc(batt_done, 1)
                if is_second(t):
                    statistics(2)
                if not first:
                    finish(t - 1, 1 - par)
                if is_second(t):
                    statistics(3)
                if not first:
                    dve.wait_ge(x_done, t)
                if not last_tile:
                    weigh(t + 1, 1 - par)
                if not first:
                    statistics_after(t - 1)
                if first:
                    for q in range(QUARTERS):
                        dve.wait_ge(wq_hi_done, q + 1)
                        dve.tensor_tensor(wq_lo[:, DC * q:DC * (q + 1), :], wq_raw[q], wq_hi[:, DC * q:DC * (q + 1), :].bitcast(F32), ALU.subtract).then_inc(wq_split, 1)
                    statistics(1)
                dve.wait_ge(hqT_done, t + 1)
                if not first:
                    dve.wait_ge(x1_stats_done, t)
                dve.tensor_tensor(raw(2, par), raw(0, par), raw(1, par), ALU.mult).then_inc(prod_done, 1)
                split_lo(t, par, 1)
                if not first:
                    gather_statistics(t - 1)
                dve.wait_ge(bar_done, t + 1)
                bars = bar[:].rearrange("p c b -> p (c b)").unsqueeze(2).to_broadcast([P, DC * PER_TILE, SEQ])
                dve.tensor_tensor(raw(3, par).rearrange("p c (b s) -> p (c b) s", s=SEQ),
                                  raw(0, par).rearrange("p c (b s) -> p (c b) s", s=SEQ), bars, ALU.mult).then_inc(prod_done, 1)
                split_lo(t, par, 2)
                split_lo(t, par, 3)
                if not last_tile:
                    split_lo(t + 1, 1 - par, 0)
                if is_second(t):
                    deviations(slice(TILES_PER_GROUP, TILES), 2)

            in_pairs(dve, tile)
            finish(TILES - 1, 1)
            dve.wait_ge(x_done, TILES)
            statistics_after(TILES - 1)
            dve.wait_ge(x1_stats_done, TILES)
            gather_statistics(TILES - 1)


def linear_attention(nc, dram, keep):
    with ExitStack() as stack:
        fr = Frame(nc, stack, "la_")
        x, ident = keep["x"], keep["ident"]
        PW, WQ, WK, WV, WG, WO = range(6)
        late_hi = fr.sbuf("late_hi", [P, 2 * DC, D], F32R)
        late_lo = fr.sbuf("late_lo", [P, 2 * DC, D], F32R)

        def weight(n):
            if n < WG:
                return keep["r_hi"][:, DC * n:DC * (n + 1), :], keep["r_lo"][:, DC * n:DC * (n + 1), :]
            n -= WG
            return late_hi[:, DC * n:DC * (n + 1), :], late_lo[:, DC * n:DC * (n + 1), :]

        xn = fr.sbuf("xn", [P, CT, D])
        xc = [fr.sbuf(f"xc{i}", [P, DC, CHUNK]) for i in range(2)]
        main_hi = fr.sbuf("main_hi", [P, DC, CHUNK], F32R)
        main_lo = fr.sbuf("main_lo", [P, DC, CHUNK], F32R)
        part = fr.sbuf("part", [P, DC, CHUNK])
        side_hi = fr.sbuf("side_hi", [P, DC, CHUNK], F32R)
        side_lo = fr.sbuf("side_lo", [P, DC, CHUNK], F32R)
        q = fr.sbuf("q", [P, DC, CHUNK])
        k = fr.sbuf("k", [P, DC, CHUNK])
        exq = fr.sbuf("exq", [P, DC, CHUNK])
        swap = fr.sbuf("swap", [P, DC, CHUNK])
        gate = fr.sbuf("gate", [P, DC, CHUNK])
        heads = keep["passing"][:].rearrange("p (c t j n) -> p c t j n", c=DC, t=CT, j=HEADS_PER_CHUNK)
        v = fr.sbuf("v", [P, CT, D])
        scores = [fr.sbuf(f"scores{i}", [P, HEADS_PER_CHUNK, P]) for i in range(2)]
        causal = fr.sbuf("causal", [P, P])
        cos = fr.sbuf("cos", [P, SEQ])
        sin = fr.sbuf("sin", [P, SEQ])
        w_dw = fr.sbuf("w_dw", [P, DC, 3])
        ones_strip = fr.sbuf("ones_strip", [P, HEAD + DC - 1])
        spread = fr.sbuf("spread", [P, DC, P])
        half_b_gate = fr.sbuf("half_b_gate", [P, DC])
        mean_var = keep["mean_var"]
        rstd = fr.sbuf("rstd", [P, TILES])
        eps = fr.sbuf("eps", [P, 1])
        x2_mv = fr.sbuf("x2_mv", [P, CT, 2])
        x2_stats = fr.sbuf("x2_stats", [P, CT, 6])
        den = scores[0][:, 0:CT, :].rearrange("p t n -> p (t n)")
        stage = [staged(keep, n) for n in range(2)]

        ps_a = fr.psum("ps_a", [P, 2, 512])
        ps_b = fr.psum("ps_b", [P, 2, 512])
        ps_c = fr.psum("ps_c", [P, 2, 512])
        ps_d = fr.psum("ps_d", [P, 2, 512])

        def wide(ps):
            return ps[:].rearrange("p a n -> p (a n)").rearrange("p (c n) -> p c n", c=DC)

        names = ("small_in moe_w_in stage_hi stage_lo eps_set std_done rstd_done heads_zero "
                 "half_done xn_done xnT_ps xT_done conv_step y_hi_done y_lo_done pw_ps xc_done xc_hi_done xc_lo_done "
                 "delta_done d_hi_done d_lo_done q_ps q_raw k_ps k_raw v_ps v_done rope_step cos_done rope_q rope_k "
                 "relu_k exq_step exk_step phi_q phi_k gate_ps gate_done scores_ps masked heads_ps den_done rec_done spread_ps "
                 "num_done norm_done a_hi_done a_lo_done wo_ps mix_step x2_ps x2_stats x2_done x2_out x_done").split()
        s = {n: fr.sem(n) for n in names}
        stage_in = [fr.sem(f"stage_in{i}") for i in range(2)]
        block = stack.enter_context(nc.Block())
        STEPS = CT * DC
        SMALL = 7

        def chunks(eng, step):
            step(0, 0, True, False)
            with eng.Fori(0, CHUNKS // 2 - 1) as pair:
                step(2 * pair + 1, 1, False, False)
                step(2 * pair + 2, 0, False, False)
            step(CHUNKS - 1, 1, False, True)

        def by_seq(buf, c):
            return buf[:, c, :].rearrange("p (q s) -> p q s", s=SEQ)

        def all_seq(buf):
            return buf[:, :, :].rearrange("p c n -> p (c n)").rearrange("p (q s) -> p q s", s=SEQ)

        def every_seq(table):
            return table[:].unsqueeze(1).to_broadcast([P, DC * CSEQ, SEQ])

        def z_cos(eng, z, cs):
            n = (cs.stop - cs.start) * CSEQ
            return eng.tensor_tensor(gate[:, cs, :].rearrange("p c n -> p (c n)").rearrange("p (q s) -> p q s", s=SEQ),
                                     z[:, cs, :].rearrange("p c n -> p (c n)").rearrange("p (q s) -> p q s", s=SEQ),
                                     cos[:].unsqueeze(1).to_broadcast([P, n, SEQ]), ALU.mult)

        def phi_heads(eng, j):
            rows = slice(j * HEAD, (j + 1) * HEAD)
            return eng.scalar_tensor_tensor(
                heads[rows, :, :, j, :].rearrange("p c t n -> p (c t) n"),
                q[rows].rearrange("p c (t n) -> p (c t) n", n=P), 0.0,
                exq[rows].rearrange("p c (t n) -> p (c t) n", n=P), ALU.max, ALU.add)

        @block.sync
        def _(sp):
            for n in range(1, 6):
                if n >= 2:
                    sp.wait_ge(s["stage_lo"], n - 1)
                    sp.dma_start(stage[n % 2], dram["attn_w"][n].rearrange("(k p) n -> p k n", p=P)).then_inc(stage_in[n % 2], 16)
                else:
                    for t, name in ((w_dw, "w_dw"), (cos, "cos"), (sin, "sin"), (half_b_gate, "b_gate"), (causal, "causal"),
                                    (ones_strip, "ones_strip"), (spread, "spread")):
                        sp.dma_start(t[:], dram[name]).then_inc(s["small_in"], 16)

            def x2_out(i):
                sp.wait_ge(s["x2_done"], i + 1)
                sp.dma_start(dram["x2"][bass.ds(CT * i, CT)].rearrange("t p d -> p t d"), xn[:]).then_inc(s["x2_out"], 16)

            with sp.Fori(0, CHUNKS - 1) as i:
                x2_out(i)
            sp.wait_ge(s["scores_ps"], CT * CHUNKS)
            sp.dma_start(keep["passing"][:, 0:DC * SUB].rearrange("p (c f) -> p c f", c=DC), dram["up_w"][0]).then_inc(s["moe_w_in"], 16)
            sp.dma_start(keep["passing"][:, DC * SUB:].rearrange("p (c d) -> p c d", c=FC), dram["down_w"][0]).then_inc(s["moe_w_in"], 16)
            x2_out(CHUNKS - 1)
            sp.wait_ge(s["moe_w_in"], 32)
            sp.wait_ge(s["x2_out"], 16 * CHUNKS)

        @block.gpsimd
        def _(pool):
            pool.wait_ge(s["small_in"], 16 * SMALL)

            def step(i, par, first, last):
                pool.wait_ge(s["xc_done"], i + 1)
                pool.wait_ge(s["y_lo_done"], i + 1)
                d, z = all_seq(part), all_seq(xc[par])
                nc.gpsimd.tensor_tensor(d[:, :, 1:], z[:, :, 1:], z[:, :, :SEQ - 1], ALU.subtract).then_inc(s["delta_done"], 1)
                nc.gpsimd.memset(d[:, :, 0:1], 0.0).then_inc(s["delta_done"], 1)
                pool.wait_ge(s["d_hi_done"], i + 1)
                pool.wait_ge(s["delta_done"], 2 * i + 2)
                nc.gpsimd.tensor_tensor(side_lo[:], part[:], side_hi[:].bitcast(F32), ALU.subtract).then_inc(s["d_lo_done"], 1)
                pool.wait_ge(s["q_raw"], i + 1)
                if not first:
                    pool.wait_ge(s["x2_ps"], i)
                z_cos(nc.gpsimd, q, slice(1, DC)).then_inc(s["cos_done"], 1)
                if first:
                    pool.wait_ge(s["stage_lo"], 6)
                    nc.gpsimd.memset(heads, 0.0).then_inc(s["heads_zero"], 1)
                pool.wait_ge(s["k_raw"], i + 1)
                pool.wait_ge(s["rope_q"], i + 1)
                z_cos(nc.gpsimd, k, slice(1, DC)).then_inc(s["cos_done"], 1)
                pool.wait_ge(s["relu_k"], i + 1)
                pool.wait_ge(s["exk_step"], 2 * i + 2)
                nc.gpsimd.tensor_tensor(k[:, 2:, :], k[:, 2:, :], swap[:, 2:, :], ALU.add).then_inc(s["phi_k"], 1)

            chunks(pool, step)

        @block.tensor
        def _(pe):
            def transpose_norm(i):
                pe.wait_ge(s["xn_done"], i + 1)
                for c in range(DC):
                    for t in range(CT):
                        last = pe.transpose(wide(ps_a)[:, c, t * P:(t + 1) * P], xn[:, t, c * P:(c + 1) * P], ident[:])
                last.then_inc(s["xnT_ps"], 1)

            def project_part(n, ps, m_hi, m_lo, e):
                w_hi, w_lo = weight(n)
                cols = slice(e * P, (e + 1) * P)
                for c in range(DC):
                    last = three_products(pe, wide(ps)[:, e, :], w_hi[:, c, cols], w_lo[:, c, cols],
                                          m_hi[:, c, :], m_lo[:, c, :], c == 0, c == DC - 1)
                return last

            def project(n, ps, m_hi, m_lo, done):
                for e in range(DC):
                    last = project_part(n, ps, m_hi, m_lo, e)
                last.then_inc(done, 1)

            def spread_reciprocals(i):
                pe.wait_ge(s["rec_done"], i + 1)
                for c in range(DC):
                    mm = pe.matmul(wide(ps_c)[:, c, :], spread[:, c, :], den, start=True, stop=True)
                mm.then_inc(s["spread_ps"], 1)

            def x2_transposed(i):
                pe.wait_ge(s["mix_step"], 2 * i + 2)
                for t in range(CT):
                    for c in range(DC):
                        mm = pe.transpose(ps_a[:, t, c * P:(c + 1) * P], gate[:, c, t * P:(t + 1) * P], ident[:])
                mm.then_inc(s["x2_ps"], 1)

            transpose_norm(0)
            pe.wait_ge(s["stage_lo"], PW + 1)
            pe.wait_ge(s["y_lo_done"], 1)
            project(PW, ps_b, main_hi, main_lo, s["pw_ps"])

            def step(i, par, first, last):
                def weight_split(n):
                    if first:
                        pe.wait_ge(s["stage_lo"], n + 1)

                if not last:
                    transpose_norm(i + 1)
                pe.wait_ge(s["xc_lo_done"], i + 1)
                weight_split(WQ)
                project(WQ, ps_b, main_hi, main_lo, s["q_ps"])
                if not first:
                    if not last:
                        pe.wait_ge(s["xT_done"], i + 2)
                    x2_transposed(i - 1)
                weight_split(WK)
                project(WK, ps_c, main_hi, main_lo, s["k_ps"])
                weight_split(WV)
                w_hi, w_lo = weight(WV)
                for t in range(CT):
                    toks = slice(t * P, (t + 1) * P)
                    for c in range(DC):
                        mm = three_products(pe, ps_d[:, t, :], main_hi[:, c, toks], main_lo[:, c, toks],
                                            w_hi[:, c, :], w_lo[:, c, :], c == 0, c == DC - 1)
                mm.then_inc(s["v_ps"], 1)
                pe.wait_ge(s["d_lo_done"], i + 1)
                pe.wait_ge(s["q_raw"], i + 1)
                weight_split(WG)
                project(WG, ps_b, side_hi, side_lo, s["gate_ps"])
                pe.wait_ge(s["phi_q"], i + 1)
                pe.wait_ge(s["phi_k"], 2 * i + 2)
                for t in range(CT):
                    for c in range(DC):
                        for b in range(PER_TILE):
                            rows = slice(b * SEQ, (b + 1) * SEQ)
                            mm = pe.matmul(ps_c[rows, t, c * P:(c + 1) * P], k[:, c, t * P + b * SEQ:t * P + (b + 1) * SEQ],
                                           heads[:, c, t, :, rows], start=True, stop=True)
                    mm.then_inc(s["scores_ps"], 1)
                pe.wait_ge(s["v_done"], i + 1)
                for n in range(STEPS):
                    t, c = n // DC, n % DC
                    toks = slice(t * P, (t + 1) * P)
                    pe.wait_ge(s["masked"], STEPS * i + n + 1)
                    if n == 0 and not first:
                        pe.wait_ge(s["x2_done"], i)
                    if n == 0 and first:
                        pe.wait_ge(s["xT_done"], i + 2)
                    for j in range(HEADS_PER_CHUNK):
                        h = HEADS_PER_CHUNK * c + j
                        rows = slice(j * HEAD, (j + 1) * HEAD)
                        pe.matmul(wide(ps_d)[rows, c, toks], v[:, t, h * HEAD:(h + 1) * HEAD], scores[n % 2][:, j, :],
                                  start=True, stop=True)
                    for j in range(HEADS_PER_CHUNK):
                        rows = slice(j * HEAD, (j + 1) * HEAD)
                        mm = pe.matmul(ps_a[rows, 0, toks], ones_strip[:, DC - 1 - c:DC - 1 - c + HEAD], scores[n % 2][:, j, :],
                                       start=c == 0, stop=c == DC - 1)
                    mm.then_inc(s["heads_ps"], 1)
                if last:
                    spread_reciprocals(i)
                else:
                    pe.wait_ge(s["y_lo_done"], i + 2)
                    pe.wait_ge(s["gate_done"], i + 1)
                    for e in range(DC):
                        mm = project_part(PW, ps_b, main_hi, main_lo, e)
                        if e == 1:
                            spread_reciprocals(i)
                    mm.then_inc(s["pw_ps"], 1)
                pe.wait_ge(s["a_lo_done"], i + 1)
                weight_split(WO)
                project(WO, ps_d, side_hi, side_lo, s["wo_ps"])

            chunks(pe, step)
            x2_transposed(CHUNKS - 1)

        @block.scalar
        def _(act):
            copy = ACT.Copy

            def weight_hi(n):
                if n >= 2:
                    act.wait_ge(stage_in[n % 2], 16 * (n // 2))
                act.activation(weight(n)[0], stage[n % 2], copy).then_inc(s["stage_hi"], 1)

            def norm_copy(i, par):
                act.wait_ge(s["xnT_ps"], i + 1)
                act.activation(xc[par][:], wide(ps_a), copy).then_inc(s["xT_done"], 1)

            def own_tap(i, par):
                act.wait_ge(s["xT_done"], i + 1)
                for c in range(DC):
                    a = act.activation(part[:, c, :], xc[par][:, c, :], copy, scale=w_dw[:, c, 2:3])
                a.then_inc(s["conv_step"], 1)

            def conv_hi(i):
                act.wait_ge(s["conv_step"], 3 * i + 3)
                act.activation(main_hi[:], part[:], copy).then_inc(s["y_hi_done"], 1)

            def xc_high(i, par):
                act.wait_ge(s["xc_done"], i + 1)
                act.activation(main_hi[:], xc[par][:], copy).then_inc(s["xc_hi_done"], 1)

            def x2_copy(i):
                act.wait_ge(s["x2_ps"], i + 1)
                act.activation(xn[:], ps_a[:], copy).then_inc(s["x2_done"], 1)

            def negative_exp(buf, src, ready, steps, i):
                act.wait_ge(ready, i + 1)
                act.activation(buf[:], src[:], ACT.Relu, scale=-1.0).then_inc(steps, 1)
                act.wait_ge(steps, 2 * i + 1)
                act.activation(buf[:], buf[:], ACT.Exp, scale=-1.0).then_inc(steps, 1)

            act.wait_ge(s["eps_set"], 1)
            act.activation(rstd[:], mean_var[:, :, 1], ACT.Sqrt, bias=eps[:]).then_inc(s["std_done"], 1)
            weight_hi(PW)
            norm_copy(0, 0)
            act.wait_ge(s["small_in"], 16 * SMALL)
            own_tap(0, 0)
            conv_hi(0)
            weight_hi(WQ)
            xc_high(0, 0)
            act.wait_ge(s["half_done"], 1)

            def step(i, par, first, last):
                if first:
                    weight_hi(WK)
                act.wait_ge(s["delta_done"], 2 * i + 2)
                if not first:
                    act.wait_ge(s["wo_ps"], i)
                act.activation(side_hi[:], part[:], copy).then_inc(s["d_hi_done"], 1)
                if not last:
                    if not first:
                        act.wait_ge(s["mix_step"], 2 * i)
                    norm_copy(i + 1, 1 - par)
                    act.wait_ge(s["d_lo_done"], i + 1)
                    own_tap(i + 1, 1 - par)
                if first:
                    for n in (WV, WG):
                        weight_hi(n)
                act.wait_ge(s["q_ps"], i + 1)
                act.activation(q[:], wide(ps_b), copy).then_inc(s["q_raw"], 1)
                if not first:
                    x2_copy(i - 1)
                if first:
                    weight_hi(WO)
                negative_exp(exq, q, s["rope_q"], s["exq_step"], i)
                act.wait_ge(s["k_ps"], i + 1)
                act.activation(k[:], wide(ps_c), copy).then_inc(s["k_raw"], 1)
                act.wait_ge(s["v_ps"], i + 1)
                act.activation(v[:], ps_d[:], copy).then_inc(s["v_done"], 1)
                negative_exp(swap, k, s["rope_k"], s["exk_step"], i)
                act.activation(k[:, 2:, :], k[:, 2:, :], ACT.Relu).then_inc(s["relu_k"], 1)
                if not last:
                    conv_hi(i + 1)
                act.wait_ge(s["gate_ps"], i + 1)
                for c in range(DC):
                    a = act.activation(gate[:, c, :], wide(ps_b)[:, c, :], ACT.Tanh, bias=half_b_gate[:, c:c + 1], scale=0.5)
                a.then_inc(s["gate_done"], 1)
                act.wait_ge(s["heads_ps"], STEPS * (i + 1))
                act.activation(q[:], wide(ps_d), copy).then_inc(s["num_done"], 1)
                act.wait_ge(s["norm_done"], i + 1)
                act.activation(side_hi[:], q[:], copy).then_inc(s["a_hi_done"], 1)
                if not last:
                    xc_high(i + 1, 1 - par)

            chunks(act, step)
            act.wait_ge(s["x2_out"], 16 * (CHUNKS - 1))
            x2_copy(CHUNKS - 1)

        @block.vector
        def _(dve):
            def lo(out, raw, hi, ready, count, done):
                dve.wait_ge(ready, count)
                dve.tensor_tensor(out[:], raw[:], hi[:].bitcast(F32), ALU.subtract).then_inc(done, 1)

            def weight_lo(n):
                w_hi, w_lo = weight(n)
                dve.wait_ge(s["stage_hi"], n + 1)
                dve.tensor_tensor(w_lo, stage[n % 2], w_hi.bitcast(F32), ALU.subtract).then_inc(s["stage_lo"], 1)

            def norm(i):
                for t in range(CT):
                    tile = CT * i + t
                    a = dve.tensor_scalar(xn[:, t:t + 1, :], x[:, bass.ds(tile, 1), :], mean_var[:, bass.ds(tile, 1), 0],
                                          rstd[:, bass.ds(tile, 1)], ALU.subtract, ALU.mult)
                a.then_inc(s["xn_done"], 1)

            def taps(i, par):
                dve.wait_ge(s["xT_done"], i + 1)
                for tap in range(1, 3):
                    dve.wait_ge(s["conv_step"], 3 * i + tap)
                    for c in range(DC):
                        y, z = by_seq(part, c), by_seq(xc[par], c)
                        w = w_dw[:, c, 2 - tap:3 - tap]
                        a = dve.scalar_tensor_tensor(y[:, :, tap:], z[:, :, :SEQ - tap], w, y[:, :, tap:], ALU.mult, ALU.add)
                    a.then_inc(s["conv_step"], 1)

            def residual(i, par, between=None):
                dve.wait_ge(s["pw_ps"], i + 1)
                dve.tensor_tensor(xc[par][:], wide(ps_b), xc[par][:], ALU.add).then_inc(s["xc_done"], 1)
                if between:
                    between()
                lo(main_lo, xc[par], main_hi, s["xc_hi_done"], i + 1, s["xc_lo_done"])

            def rope(i, z, n, first):
                dve.wait_ge(s[("q_raw", "k_raw")[n]], i + 1)
                if n:
                    dve.wait_ge(s["rope_q"], i + 1)
                if not first:
                    dve.wait_ge(s["x2_ps"], i)
                z_cos(dve, z, slice(0, 1)).then_inc(s["cos_done"], 1)
                dve.stream_shuffle(swap[:], z[:], [a ^ 1 for a in range(32)]).then_inc(s["rope_step"], 1)
                dve.wait_ge(s["rope_step"], 4 * i + 2 * n + 1)
                dve.tensor_tensor(all_seq(swap), all_seq(swap), every_seq(sin), ALU.mult).then_inc(s["rope_step"], 1)
                dve.wait_ge(s["rope_step"], 4 * i + 2 * n + 2)
                dve.wait_ge(s["cos_done"], 4 * i + 2 * n + 2)
                dve.tensor_tensor(z[:], gate[:], swap[:], ALU.add).then_inc(s[("rope_q", "rope_k")[n]], 1)

            def mix(i, par):
                dve.wait_ge(s["wo_ps"], i + 1)
                dve.wait_ge(s["gate_done"], i + 1)
                dve.scalar_tensor_tensor(gate[:], gate[:], 1.0, wide(ps_d), ALU.add, ALU.mult).then_inc(s["mix_step"], 1)
                dve.wait_ge(s["mix_step"], 2 * i + 1)
                dve.scalar_tensor_tensor(gate[:], gate[:], 0.5, xc[par][:], ALU.mult, ALU.add).then_inc(s["mix_step"], 1)

            def x2_statistics(i):
                dve.wait_ge(s["x2_done"], i + 1)
                for t in range(CT):
                    dve.bn_stats(x2_stats[:, t, :], xn[:, t, :]).then_inc(s["x2_stats"], 1)

            def x2_add(i):
                tiles = bass.ds(CT * i, CT)
                dve.wait_ge(s["x2_stats"], 2 * CT * i + CT)
                dve.tensor_tensor(x[:, tiles, :], xn[:], x[:, tiles, :], ALU.add).then_inc(s["x_done"], 1)

            def x2_gather(i):
                for t in range(CT):
                    dve.bn_aggr(x2_mv[:, t, :], x2_stats[:, t, :]).then_inc(s["x2_stats"], 1)
                dve.wait_ge(s["x2_stats"], 2 * CT * (i + 1))
                dve.wait_ge(s["x_done"], i + 1)
                dve.tensor_copy(keep["mean_var"][:, bass.ds(CT * i, CT), :], x2_mv[:])

            dve.memset(eps[:], EPS).then_inc(s["eps_set"], 1)
            dve.wait_ge(s["std_done"], 1)
            dve.reciprocal(rstd[:], rstd[:]).then_inc(s["rstd_done"], 1)
            dve.wait_ge(s["rstd_done"], 1)
            norm(0)
            weight_lo(PW)
            dve.wait_ge(s["small_in"], 16 * SMALL)
            dve.tensor_scalar(half_b_gate[:], half_b_gate[:], 0.5, None, ALU.mult).then_inc(s["half_done"], 1)
            taps(0, 0)
            lo(main_lo, part, main_hi, s["y_hi_done"], 1, s["y_lo_done"])
            weight_lo(WQ)
            residual(0, 0)

            def step(i, par, first, last):
                if not last:
                    norm(i + 1)
                if first:
                    for n in (WK, WV, WG):
                        weight_lo(n)
                else:
                    mix(i - 1, 1 - par)
                rope(i, q, 0, first)
                if first:
                    weight_lo(WO)
                if not last:
                    taps(i + 1, 1 - par)
                rope(i, k, 1, first)
                dve.wait_ge(s["exq_step"], 2 * i + 2)
                if first:
                    dve.wait_ge(s["heads_zero"], 1)
                for j in range(HEADS_PER_CHUNK):
                    a = phi_heads(dve, j)
                a.then_inc(s["phi_q"], 1)
                dve.wait_ge(s["exk_step"], 2 * i + 2)
                dve.scalar_tensor_tensor(k[:, 0:2, :], k[:, 0:2, :], 0.0, swap[:, 0:2, :], ALU.max, ALU.add).then_inc(s["phi_k"], 1)
                if not last:
                    lo(main_lo, part, main_hi, s["y_hi_done"], i + 2, s["y_lo_done"])
                for n in range(STEPS):
                    t, c = divmod(n, DC)
                    dve.wait_ge(s["scores_ps"], CT * i + t + 1)
                    if n >= 2:
                        dve.wait_ge(s["heads_ps"], STEPS * i + n - 1)
                    dve.tensor_tensor(scores[n % 2][:].rearrange("p j (b s) -> p j b s", b=PER_TILE),
                                      ps_c[:, t, c * P:(c + 1) * P].rearrange("p (j s) -> p j s", s=SEQ).unsqueeze(2).to_broadcast([P, HEADS_PER_CHUNK, PER_TILE, SEQ]),
                                      causal[:].rearrange("p (b s) -> p b s", b=PER_TILE).unsqueeze(1).to_broadcast([P, HEADS_PER_CHUNK, PER_TILE, SEQ]),
                                      ALU.mult).then_inc(s["masked"], 1)
                dve.wait_ge(s["heads_ps"], STEPS * (i + 1))
                dve.tensor_scalar(den, ps_a[:, 0, 0:CHUNK], DEN_EPS, None, ALU.add).then_inc(s["den_done"], 1)
                dve.wait_ge(s["den_done"], i + 1)
                dve.reciprocal(den, den).then_inc(s["rec_done"], 1)
                dve.wait_ge(s["spread_ps"], i + 1)
                dve.wait_ge(s["num_done"], i + 1)
                dve.tensor_tensor(q[:], wide(ps_c), q[:], ALU.mult).then_inc(s["norm_done"], 1)
                if not first:
                    x2_statistics(i - 1)
                lo(side_lo, q, side_hi, s["a_hi_done"], i + 1, s["a_lo_done"])
                if not last:
                    if not first:
                        dve.wait_ge(s["x2_out"], 16 * i)
                    residual(i + 1, 1 - par, None if first else lambda: x2_add(i - 1))
                else:
                    x2_add(i - 1)
                if not first:
                    x2_gather(i - 1)

            chunks(dve, step)
            mix(CHUNKS - 1, 1)
            x2_statistics(CHUNKS - 1)
            x2_add(CHUNKS - 1)
            x2_gather(CHUNKS - 1)
            dve.wait_ge(s["x_done"], CHUNKS)


def feed_forwards(nc, dram, keep, out, experts_only=False):
    with ExitStack() as stack:
        fr = Frame(nc, stack, "ff_")
        x, ident, mean_var = keep["x"], keep["ident"], keep["mean_var"]
        h_hi, h_lo = keep["r_hi"], keep["r_lo"]
        up_hi = [fr.sbuf(f"up_hi{i}", [P, DC, SUB], F32R) for i in range(2)]
        up_lo = [fr.sbuf(f"up_lo{i}", [P, DC, SUB], F32R) for i in range(2)]
        down_hi = [fr.sbuf(f"down_hi{i}", [P, FC, D], F32R) for i in range(2)]
        down_lo = [fr.sbuf(f"down_lo{i}", [P, FC, D], F32R) for i in range(2)]
        up_raw = keep["passing"][:, 0:DC * SUB].rearrange("p (c f) -> p c f", c=DC)
        down_raw = keep["passing"][:, DC * SUB:].rearrange("p (c d) -> p c d", c=FC)
        hid = fr.sbuf("hid", [P, FC, GROUP])
        hid_hi = fr.sbuf("hid_hi", [P, FC, GROUP], F32R)
        hid_lo = fr.sbuf("hid_lo", [P, FC, GROUP], F32R)
        up_bias = fr.sbuf("up_bias", [P, SUBS * FC])
        down_bias = fr.sbuf("down_bias", [P, D])
        ln_g = fr.sbuf("ln_g", [P, DC])
        ln_b = fr.sbuf("ln_b", [P, DC])
        w_moe = fr.sbuf("w_moe", [P, DC, EXPERTS])
        w_router = fr.sbuf("w_router", [P, DC, BLOCKS])
        b_router = fr.sbuf("b_router", [P, BLOCKS])
        rstd = fr.sbuf("rstd", [P, TILES])
        stats = fr.sbuf("stats", [P, 6])
        eps = fr.sbuf("eps", [P, 1])
        share = fr.sbuf("share", [P, TILES, EXPERTS])
        share_by = fr.sbuf("share_by", [P, EXPERTS, TILES])
        soft = fr.sbuf("soft", [P, 2, TILES])
        shut_in = fr.sbuf("shut_in", [P, GROUPS, BLOCKS])
        shut = fr.sbuf("shut", [P, GROUPS * BLOCKS], BF16)
        left_outT = fr.sbuf("left_outT", [P, GROUP], BF16)
        block_no = fr.sbuf("block_no", [P, BLOCKS])
        prob = fr.sbuf("prob", [P, TILES_PER_GROUP, BLOCKS])
        best = fr.sbuf("best", [P, TILES_PER_GROUP, 8])
        best_at = fr.sbuf("best_at", [P, TILES_PER_GROUP, 8], U32)
        spot = fr.sbuf("spot", [P, TILES_PER_GROUP, 8])
        chosen = fr.sbuf("chosen", [P, TILES_PER_GROUP, BLOCKS, TOP_K])
        left_out = prob
        def slot(i):
            return 0 if i in (1, 3) else 2

        def xn(i):
            return hid[:, slot(i), :]

        def h_raw(i):
            return hid[:, slot(i) + 1, :].rearrange("p (c n) -> p c n", c=DC)

        def x2_arrival(t):
            return (x_in[0], 16 * (t // 2 + 1)) if slot(t) == 0 else (x_in[1], 16 * (t // 2 + 1 if t <= TILES_PER_GROUP else t - 1))

        ps_up = [fr.psum(f"ps_up{f}") for f in range(FC)]
        ps_down = [fr.psum(f"ps_down{t}") for t in range(TILES_PER_GROUP)]

        names = ("small_in first_in w_in w_hi_done w_split b2_in b2_used xn_done xT_ps h_raw_done h_hi_done h_lo_done logit_ps "
                 "logit_done soft_step exp_done share_done up_done hid_hi_done hid_done down_done acc_done eps_set "
                 "std_done rstd_done stats_done aggr_done top_done out_left left_ps leftT_done leftT_zero x_out").split()
        s = {n: fr.sem(n) for n in names}
        x_in = [fr.sem(f"x_in{i}") for i in range(2)]
        block = stack.enter_context(nc.Block())
        last_sub = MOE_SUBS if experts_only else SUBS
        SMALL = 6

        def weights_in(sp, sub):
            sp.dma_start(up_raw, dram["up_w"][bass.ds(sub, 1)].rearrange("o p c f -> p (o c) f")).then_inc(s["w_in"], 16)
            sp.dma_start(down_raw, dram["down_w"][bass.ds(sub, 1)].rearrange("o p c d -> p (o c) d")).then_inc(s["w_in"], 16)

        @block.sync
        def _(sp):
            sp.dma_start(xn(0), dram["x2"][0]).then_inc(x2_arrival(0)[0], 16)
            for t, name in ((ln_g, "ln_g"), (ln_b, "ln_b"), (w_moe, "w_moe")):
                sp.dma_start(t[:], dram[name]).then_inc(s["first_in"], 16)
            sp.dma_start(xn(1), dram["x2"][1]).then_inc(x2_arrival(1)[0], 16)
            for t, name in ((up_bias, "up_bias"), (w_router, "w_router"),
                            (shut_in, "shut"), (block_no, "block_no")):
                sp.dma_start(t[:], dram[name]).then_inc(s["small_in"], 16)
            sp.dma_start(b_router[:], dram["b_router"].partition_broadcast(P)).then_inc(s["small_in"], 16)
            sp.dma_start(down_bias[:], dram["down_bias"][0].partition_broadcast(P)).then_inc(s["small_in"], 16)
            for t in range(2, TILES):
                sp.wait_ge(s["xT_ps"], t - 1 if t <= TILES_PER_GROUP else t)
                sp.dma_start(xn(t), dram["x2"][t]).then_inc(x2_arrival(t)[0], 16)
                if t == TILES_PER_GROUP:
                    sp.wait_ge(s["w_split"], DC)
                    weights_in(sp, 1)
            with sp.Fori(0, EXPERTS) as e:
                for j in range(SUBS_PER_EXPERT):
                    sub = SUBS_PER_EXPERT * e + j
                    sp.wait_ge(s["w_split"], DC * sub + 2 * DC)
                    weights_in(sp, sub + 2)
                    if j == 1:
                        sp.wait_ge(s["b2_used"], TILES * e + TILES)
                        sp.dma_start(down_bias[:], dram["down_bias"][bass.ds(e + 1, 1)].rearrange("o d -> (o d)").partition_broadcast(P)).then_inc(s["b2_in"], 16)
            if not experts_only:
                for sub in range(MOE_SUBS, SUBS - 2):
                    sp.wait_ge(s["w_split"], DC * sub + 2 * DC)
                    weights_in(sp, sub + 2)
            for g in range(GROUPS):
                sp.wait_ge(s["acc_done"], TILES * (last_sub - 1) + TILES_PER_GROUP * (g + 1))
                sp.dma_start(out[g * GROUP:(g + 1) * GROUP, :].rearrange("(t p) d -> p t d", p=P),
                             x[:, TILES_PER_GROUP * g:TILES_PER_GROUP * (g + 1), :]).then_inc(s["x_out"], 16)
            sp.wait_ge(s["x_out"], 16 * GROUPS)

        @block.gpsimd
        def _(pool):
            nc.gpsimd.memset(left_outT[:], 0.0).then_inc(s["leftT_zero"], 1)

        def sub_loops(eng, group):
            for j in range(1, SUBS_PER_EXPERT):
                with eng.Fori(0, GROUPS) as g:
                    group(j, j, g, 0)
            with eng.Fori(1, EXPERTS - 1) as e:
                for j in range(SUBS_PER_EXPERT):
                    with eng.Fori(0, GROUPS) as g:
                        group(SUBS_PER_EXPERT * e + j, j, g, e)
            for j in range(SUBS_PER_EXPERT):
                with eng.Fori(0, GROUPS - (j == SUBS_PER_EXPERT - 1)) as g:
                    group(SUBS_PER_EXPERT * (EXPERTS - 1) + j, j, g, EXPERTS - 1)

        def last_group(group, ahead):
            group(MOE_SUBS - 1, SUBS_PER_EXPERT - 1, GROUPS - 1, EXPERTS - 1, ahead is not None, ahead)

        ahead_of_ffn = None if experts_only else TILES

        def ffn_loops(eng, group):
            for j in range(1, FFN_SUBS):
                with eng.Fori(0, GROUPS) as g:
                    group(MOE_SUBS + j, j, g, None)

        def up_bank(f, mixed):
            return ps_up[f % (FC - 1)] if mixed else ps_up[f]

        def lead_bank(i):
            return ps_up[min(i, TILES_PER_GROUP - 1)]

        def logit_bank(i, logits):
            u = i % TILES_PER_GROUP
            if i >= TILES_PER_GROUP and u < 2:
                return ps_down[u][:, 0:logits]
            return lead_bank(i)[:, 0:logits]

        @block.tensor
        def _(pe):
            routers = ((EXPERTS, w_moe), (BLOCKS, w_router))

            def lead_turn(i):
                pe.wait_ge(s["xn_done"], i + 1)
                if i >= TILES_PER_GROUP and i % TILES_PER_GROUP in (0, 3):
                    pe.wait_ge(s["logit_done"], i)
                for c in range(DC):
                    mm = pe.transpose(lead_bank(i)[:, c * P:(c + 1) * P], xn(i)[:, c * P:(c + 1) * P], ident[:])
                mm.then_inc(s["xT_ps"], 1)

            def lead_logits(i):
                logits, w = routers[i // TILES]
                pe.wait_ge(s["h_raw_done"], i + 1)
                for c in range(DC):
                    mm = pe.matmul(logit_bank(i, logits), h_raw(i)[:, c, :], w[:, c, :], start=c == 0, stop=c == DC - 1)
                mm.then_inc(s["logit_ps"], 1)

            def left_transposed(g):
                pe.wait_ge(s["out_left"], g + 1)
                for u in range(TILES_PER_GROUP):
                    mm = pe.transpose(ps_up[3][0:BLOCKS, u * P:(u + 1) * P], left_out[:, u, :], ident[:])
                mm.then_inc(s["left_ps"], 1)

            def group(sub, j, g, e, mixed=False, ahead=None):
                par = j % 2
                n = GROUPS * sub + g
                pe.wait_ge(s["w_split"], DC * sub + DC)
                if mixed:
                    pe.wait_ge(s["h_lo_done"], TILES * (e is None) + TILES_PER_GROUP * (g + 1))

                def up(f):
                    cols = slice(f * P, (f + 1) * P)
                    bank = up_bank(f, mixed)
                    for c in range(DC):
                        at = bass.ds(DC * g + c, 1)
                        mm = three_products(pe, bank[:], up_hi[par][:, c, cols], up_lo[par][:, c, cols],
                                            h_hi[:, at, :].rearrange("p o n -> p (o n)"), h_lo[:, at, :].rearrange("p o n -> p (o n)"),
                                            c == 0, c == DC - 1 and e is not None)
                    if e is None:
                        if mixed and f == 0:
                            pe.wait_ge(s["leftT_done"], g + 1)
                        mm = pe.matmul(bank[:], shut[:, bass.ds(BLOCKS * g + FC * j + f, 1)].to_broadcast([P, P]),
                                       left_outT[:], start=False, stop=True)
                    mm.then_inc(s["up_done"], 1)

                def down(f):
                    pe.wait_ge(s["hid_done"], FC * n + f + 1)
                    if ahead is not None and f == 0:
                        pe.wait_ge(s["logit_done"], ahead + 2)
                    for t in range(TILES_PER_GROUP):
                        if mixed and f == 0 and n:
                            pe.wait_ge(s["acc_done"], TILES_PER_GROUP * (n - 1) + t + 1)
                        toks = slice(t * P, (t + 1) * P)
                        mm = three_products(pe, ps_down[t][:], hid_hi[:, f, toks], hid_lo[:, f, toks],
                                            down_hi[par][:, f, :], down_lo[par][:, f, :], f == 0, f == FC - 1)
                        if f == FC - 1:
                            mm.then_inc(s["down_done"], 1)

                def lead(step, t):
                    if ahead is not None:
                        step(ahead + t)

                up(0)
                lead(lead_turn, 0)
                up(1)
                if ahead is not None and n:
                    pe.wait_ge(s["acc_done"], TILES_PER_GROUP * (n - 1) + 2)
                lead(lead_logits, 0)
                lead(lead_turn, 1)
                up(2)
                lead(lead_logits, 1)
                lead(lead_turn, 2)
                down(0)
                lead(lead_logits, 2)
                lead(lead_turn, 3)
                up(3)
                lead(lead_logits, 3)
                down(1)
                down(2)
                down(3)

            def first_subset(n, sub, e):
                if n == 0:
                    lead_turn(0)
                    for t in range(TILES_PER_GROUP):
                        if t + 1 < TILES_PER_GROUP:
                            lead_turn(t + 1)
                        if t == 0:
                            pe.wait_ge(s["first_in"], 16 * 3)
                        lead_logits(t)
                    pe.wait_ge(s["logit_done"], TILES_PER_GROUP)
                for g in range(GROUPS):
                    if e is None:
                        left_transposed(g)
                    group(sub, 0, g, e, True, TILES * n + TILES_PER_GROUP * (g + 1) if g < GROUPS - 1 else None)

            first_subset(0, 0, 0)
            pe.wait_ge(s["logit_done"], TILES)
            sub_loops(pe, group)
            pe.wait_ge(s["small_in"], 16 * SMALL)
            last_group(group, ahead_of_ffn)
            if experts_only:
                return
            first_subset(1, MOE_SUBS, None)
            ffn_loops(pe, group)

        @block.scalar
        def _(act):
            copy = ACT.Copy

            def split_weights(sub, c, par):
                at = bass.ds(c, 1)
                if not isinstance(sub, int) or sub:
                    act.wait_ge(s["w_in"], 32 * sub)
                act.activation(up_hi[par][:, at, :], up_raw[:, at, :], copy)
                act.activation(down_hi[par][:, at, :], down_raw[:, at, :], copy).then_inc(s["w_hi_done"], 1)

            def deviations(tiles):
                act.activation(rstd[:, tiles], mean_var[:, tiles, 1], ACT.Sqrt, bias=eps[:]).then_inc(s["std_done"], 1)

            def group_deviations(g):
                act.wait_ge(s["aggr_done"], TILES_PER_GROUP * (g + 1))
                deviations(slice(TILES_PER_GROUP * g, TILES_PER_GROUP * (g + 1)))

            def lead(i):
                g, t = divmod(i % TILES, TILES_PER_GROUP)
                act.wait_ge(s["xT_ps"], i + 1)
                before = i - 2 if i <= TILES_PER_GROUP else i - 1
                if before >= 0:
                    act.wait_ge(s["h_lo_done"], before + 1)
                    act.wait_ge(s["logit_ps"], before + 1)
                if i < TILES:
                    for c in range(DC):
                        a = act.activation(h_raw(i)[:, c, :], lead_bank(i)[:, c * P:(c + 1) * P], ACT.Identity,
                                           bias=ln_b[:, c:c + 1], scale=ln_g[:, c:c + 1])
                else:
                    a = act.activation(h_raw(i), lead_bank(i)[:].rearrange("p (c n) -> p c n", c=DC), copy)
                a.then_inc(s["h_raw_done"], 1)
                act.wait_ge(s["h_raw_done"], i + 1)
                act.activation(h_hi[:, DC * g:DC * (g + 1), t * P:(t + 1) * P], h_raw(i), copy).then_inc(s["h_hi_done"], 1)

            def router_exp(n, g):
                tiles = slice(TILES_PER_GROUP * g, TILES_PER_GROUP * (g + 1))
                act.wait_ge(s["soft_step"], 4 * (GROUPS * n + g) + 2)
                z = prob[:] if n else share[:, tiles, :]
                act.activation(z, z, ACT.Exp).then_inc(s["exp_done"], 1)

            def left_transposed(g):
                act.wait_ge(s["left_ps"], g + 1)
                act.activation(left_outT[SEQ * g:SEQ * g + BLOCKS, :], ps_up[3][0:BLOCKS, :], copy).then_inc(s["leftT_done"], 1)

            def group(sub, j, g, e, mixed=False, ahead=None):
                n = GROUPS * sub + g

                def hidden(f):
                    act.wait_ge(s["up_done"], FC * n + f + 1)
                    func = ACT.Relu if e is None else ACT.Silu
                    bias = up_bias[:, bass.ds(FC * sub + f, 1)]
                    bank = up_bank(f, mixed)
                    if mixed and f >= 2:
                        act.wait_ge(s["hid_done"], FC * n + f - 1)
                    act.activation(hid[:, f % 2 if mixed else f, :], bank[:], func, bias=bias)
                    act.activation(hid_hi[:, f, :], bank[:], func, bias=bias).then_inc(s["hid_hi_done"], 1)

                def lead_tile(t):
                    if ahead is not None:
                        lead(ahead + t)

                if mixed:
                    act.wait_ge(s["h_lo_done"], TILES * (e is None) + TILES_PER_GROUP)
                hidden(0)
                lead_tile(0)
                hidden(1)
                lead_tile(1)
                if not sub_is_last(sub):
                    if mixed and ahead is None:
                        act.wait_ge(s["logit_ps"], TILES * (1 + (e is None)))
                        act.wait_ge(s["h_lo_done"], TILES * (1 + (e is None)))
                    split_weights(sub + 1, g, 1 - j % 2)
                hidden(2)
                lead_tile(2)
                lead_tile(3)
                hidden(3)
                if ahead is not None:
                    router_exp(ahead // TILES, ahead % TILES // TILES_PER_GROUP)
                    if TILES <= ahead < 2 * TILES - TILES_PER_GROUP:
                        group_deviations((ahead - TILES) // TILES_PER_GROUP + 1)

            def sub_is_last(sub):
                return isinstance(sub, int) and sub == SUBS - 1

            def first_subset(n, sub, e):
                if n == 0:
                    for c in range(DC):
                        split_weights(0, c, 0)
                    act.wait_ge(s["first_in"], 16 * 3)
                    for t in range(TILES_PER_GROUP):
                        lead(t)
                    router_exp(0, 0)
                    act.wait_ge(s["small_in"], 16 * SMALL)
                    act.activation(shut[:], shut_in[:].rearrange("p g b -> p (g b)"), copy)
                for g in range(GROUPS):
                    if e is None:
                        left_transposed(g)
                    group(sub, 0, g, e, True, TILES * n + TILES_PER_GROUP * (g + 1) if g < GROUPS - 1 else None)

            act.wait_ge(s["eps_set"], 1)
            deviations(slice(0, TILES))
            first_subset(0, 0, 0)
            sub_loops(act, group)
            if not experts_only:
                group_deviations(0)
            last_group(group, ahead_of_ffn)
            if experts_only:
                return
            act.wait_ge(s["leftT_zero"], 1)
            first_subset(1, MOE_SUBS, None)
            ffn_loops(act, group)

        @block.vector
        def _(dve):
            dve.memset(eps[:], EPS).then_inc(s["eps_set"], 1)

            def split_weights(sub, c, par):
                at = bass.ds(c, 1)
                dve.wait_ge(s["w_hi_done"], DC * sub + c + 1)
                dve.tensor_tensor(up_lo[par][:, at, :], up_raw[:, at, :], up_hi[par][:, at, :].bitcast(F32), ALU.subtract)
                dve.tensor_tensor(down_lo[par][:, at, :], down_raw[:, at, :], down_hi[par][:, at, :].bitcast(F32), ALU.subtract).then_inc(s["w_split"], 1)

            def deviations(tiles, count):
                dve.wait_ge(s["std_done"], count)
                dve.reciprocal(rstd[:, tiles], rstd[:, tiles]).then_inc(s["rstd_done"], 1)

            def statistics(t):
                if t:
                    dve.wait_ge(s["aggr_done"], t)
                dve.bn_stats(stats[:], x[:, t, :]).then_inc(s["stats_done"], 1)
                dve.wait_ge(s["stats_done"], t + 1)
                dve.bn_aggr(mean_var[:, t, :], stats[:]).then_inc(s["aggr_done"], 1)

            def group_statistics(g):
                for t in range(TILES_PER_GROUP * g, TILES_PER_GROUP * (g + 1)):
                    statistics(t)
                deviations(slice(TILES_PER_GROUP * g, TILES_PER_GROUP * (g + 1)), 2 + g)

            def norm(i):
                n, t = divmod(i, TILES)
                if n == 0:
                    dve.wait_ge(s["rstd_done"], 1)
                    dve.wait_ge(*x2_arrival(i))
                    src = xn(i)
                else:
                    dve.wait_ge(s["rstd_done"], 2 + t // TILES_PER_GROUP)
                    dve.wait_ge(s["xT_ps"], i)
                    src = x[:, t, :]
                dve.tensor_scalar(xn(i), src, mean_var[:, t, 0:1], rstd[:, t:t + 1], ALU.subtract, ALU.mult).then_inc(s["xn_done"], 1)

            def lead(i):
                g, t = divmod(i % TILES, TILES_PER_GROUP)
                dve.wait_ge(s["h_hi_done"], i + 1)
                rows = (slice(None), slice(DC * g, DC * (g + 1)), slice(t * P, (t + 1) * P))
                dve.tensor_tensor(h_lo[rows], h_raw(i), h_hi[rows].bitcast(F32), ALU.subtract).then_inc(s["h_lo_done"], 1)

            def logits(i):
                n, t = divmod(i, TILES)
                dve.wait_ge(s["logit_ps"], i + 1)
                if n == 0:
                    dve.tensor_copy(share[:, t, :], logit_bank(i, EXPERTS)).then_inc(s["logit_done"], 1)
                else:
                    dve.tensor_tensor(prob[:, t % TILES_PER_GROUP, :], logit_bank(i, BLOCKS), b_router[:], ALU.add).then_inc(s["logit_done"], 1)

            def softmax(n, g):
                tiles = slice(TILES_PER_GROUP * g, TILES_PER_GROUP * (g + 1))
                z = prob[:] if n else share[:, tiles, :]
                step = 4 * (GROUPS * n + g)
                wide = [P, TILES_PER_GROUP, (EXPERTS, BLOCKS)[n]]
                dve.wait_ge(s["logit_done"], TILES * n + TILES_PER_GROUP * (g + 1))
                dve.tensor_reduce(soft[:, 0, tiles], z, AX.X, ALU.max).then_inc(s["soft_step"], 1)
                dve.wait_ge(s["soft_step"], step + 1)
                dve.tensor_tensor(z, z, soft[:, 0, tiles].unsqueeze(2).to_broadcast(wide), ALU.subtract).then_inc(s["soft_step"], 1)
                dve.wait_ge(s["exp_done"], GROUPS * n + g + 1)
                dve.tensor_reduce(soft[:, 1, tiles], z, AX.X, ALU.add).then_inc(s["soft_step"], 1)
                dve.wait_ge(s["soft_step"], step + 3)
                dve.reciprocal(soft[:, 1, tiles], soft[:, 1, tiles]).then_inc(s["soft_step"], 1)
                dve.wait_ge(s["soft_step"], step + 4)
                rec = soft[:, 1, tiles].unsqueeze(2).to_broadcast(wide)
                if n == 0:
                    dve.tensor_tensor(share_by[:, :, tiles].rearrange("p e t -> p t e"), z, rec, ALU.mult).then_inc(s["share_done"], 1)
                    return
                base = TOP_STEPS * g
                dve.tensor_tensor(z, z, rec, ALU.mult).then_inc(s["top_done"], 1)
                dve.wait_ge(s["top_done"], base + 1)
                for u in range(TILES_PER_GROUP):
                    a = dve.max(best[:, u, :], z[:, u, :])
                a.then_inc(s["top_done"], 1)
                dve.wait_ge(s["top_done"], base + 2)
                for u in range(TILES_PER_GROUP):
                    a = dve.max_index(best_at[:, u, :], best[:, u, :], z[:, u, :])
                a.then_inc(s["top_done"], 1)
                dve.wait_ge(s["top_done"], base + 3)
                dve.tensor_copy(spot[:], best_at[:]).then_inc(s["top_done"], 1)
                dve.wait_ge(s["top_done"], base + 4)
                dve.tensor_tensor(chosen[:], spot[:, :, 0:TOP_K].unsqueeze(2).to_broadcast([P, TILES_PER_GROUP, BLOCKS, TOP_K]),
                                  block_no[:].unsqueeze(1).unsqueeze(3).to_broadcast([P, TILES_PER_GROUP, BLOCKS, TOP_K]), ALU.is_equal).then_inc(s["top_done"], 1)
                dve.wait_ge(s["top_done"], base + 5)
                dve.tensor_reduce(z, chosen[:], AX.X, ALU.add).then_inc(s["top_done"], 1)
                dve.wait_ge(s["top_done"], base + 6)
                dve.tensor_scalar(z, z, -1.0, 1.0, ALU.mult, ALU.add).then_inc(s["out_left"], 1)

            TOP_STEPS = 6

            def group(sub, j, g, e, mixed=False, ahead=None):
                n = GROUPS * sub + g

                def hidden_lo(f):
                    dve.wait_ge(s["hid_hi_done"], FC * n + f + 1)
                    dve.tensor_tensor(hid_lo[:, f, :], hid[:, f % 2 if mixed else f, :], hid_hi[:, f, :].bitcast(F32), ALU.subtract).then_inc(s["hid_done"], 1)

                def led(step, t):
                    if ahead is not None:
                        step(ahead + t)

                hidden_lo(0)
                led(lead, 0)
                led(norm, 1)
                led(logits, 0)
                hidden_lo(1)
                led(lead, 1)
                led(norm, 2)
                led(logits, 1)
                if not (isinstance(sub, int) and sub == SUBS - 1):
                    split_weights(sub + 1, g, 1 - j % 2)
                hidden_lo(2)
                led(lead, 2)
                led(norm, 3)
                led(logits, 2)
                led(lead, 3)
                led(logits, 3)
                hidden_lo(3)
                if ahead is not None:
                    softmax(ahead // TILES, ahead % TILES // TILES_PER_GROUP)
                    following = ahead + TILES_PER_GROUP
                    if following % TILES:
                        if following > TILES:
                            group_statistics(following // TILES_PER_GROUP - GROUPS)
                        norm(following)
                if mixed and e is not None:
                    dve.wait_ge(s["small_in"], 16 * SMALL)
                    dve.wait_ge(s["share_done"], g + 1)
                for t in range(TILES_PER_GROUP):
                    tile = TILES_PER_GROUP * g + t
                    row = x[:, bass.ds(tile, 1), :]
                    if j == 0:
                        if e is None:
                            dve.wait_ge(s["b2_in"], 16 * EXPERTS)
                            dve.tensor_tensor(row, down_bias[:].unsqueeze(1), row, ALU.add).then_inc(s["b2_used"], 1)
                            dve.wait_ge(s["b2_used"], TILES * EXPERTS + tile + 1)
                        else:
                            if not mixed:
                                dve.wait_ge(s["b2_in"], 16 * e)
                            dve.scalar_tensor_tensor(row, down_bias[:].unsqueeze(1), share_by[:, bass.ds(e, 1), bass.ds(tile, 1)].rearrange("p a b -> p (a b)"), row, ALU.mult, ALU.add).then_inc(s["b2_used"], 1)
                            dve.wait_ge(s["b2_used"], TILES * e + tile + 1)
                    dve.wait_ge(s["down_done"], TILES_PER_GROUP * n + t + 1)
                    ps = ps_down[t][:].unsqueeze(1)
                    if e is None:
                        a = dve.tensor_tensor(row, ps, row, ALU.add)
                    else:
                        a = dve.scalar_tensor_tensor(row, ps, share_by[:, bass.ds(e, 1), bass.ds(tile, 1)].rearrange("p a b -> p (a b)"), row, ALU.mult, ALU.add)
                    a.then_inc(s["acc_done"], 1)

            def first_subset(n, sub, e):
                if n == 0:
                    norm(0)
                    norm(1)
                    for c in range(2):
                        split_weights(0, c, 0)
                    for t in range(TILES_PER_GROUP):
                        lead(t)
                        if t < 2:
                            split_weights(0, 2 + t, 0)
                            norm(2 + t)
                        logits(t)
                    softmax(0, 0)
                    norm(TILES_PER_GROUP)
                for g in range(GROUPS):
                    group(sub, 0, g, e, True, TILES * n + TILES_PER_GROUP * (g + 1) if g < GROUPS - 1 else None)

            deviations(slice(0, TILES), 1)
            first_subset(0, 0, 0)
            sub_loops(dve, group)
            if not experts_only:
                dve.wait_ge(s["acc_done"], TILES * MOE_SUBS - TILES_PER_GROUP)
                group_statistics(0)
                norm(TILES)
            last_group(group, ahead_of_ffn)
            if experts_only:
                return
            first_subset(1, MOE_SUBS, None)
            ffn_loops(dve, group)


def build(nc, dram, out, phases=4):
    with ExitStack() as stack:
        fr = Frame(nc, stack)
        dram = {**dram, "x2": nc.dram_tensor("x2_scratch", [TILES, P, D], F32, kind="Internal").ap()}
        keep = {
            "x": fr.sbuf("x_res", [P, TILES, D]),
            "r_hi": fr.sbuf("r_hi", [P, FEAT_CHUNKS, D], F32R),
            "r_lo": fr.sbuf("r_lo", [P, FEAT_CHUNKS, D], F32R),
            "mean_var": fr.sbuf("x2_mean_var", [P, TILES, 2]),
            "passing": fr.sbuf("passing", [P, DC * SUB + FC * D]),
            "ident": fr.sbuf("identity", [P, P]),
        }
        cross_attention(nc, dram, keep)
        if phases == 1:
            dump(nc, keep["x"], out)
            return
        linear_attention(nc, dram, keep)
        if phases == 2:
            dump(nc, keep["x"], out)
            return
        feed_forwards(nc, dram, keep, out, phases == 3)


def dump(nc, x, out):
    with nc.semaphore("dump") as s, nc.Block() as block:
        @block.sync
        def _(sp):
            sp.dma_start(out.rearrange("(t p) d -> p t d", p=P), x[:]).then_inc(s, 16)
            sp.wait_ge(s, 16)


def layouts(v):
    c = np.ascontiguousarray
    ctx = v["ctx_1024"]
    tiles = ctx.reshape(TILES, PER_TILE, CTX, D)
    full = CTX_CHUNKS * P
    a = {
        "x": c(v["x"].reshape(TOKENS, D)),
        "ctxT": c(tiles.reshape(TILES, PER_TILE, CTX, DC, P).transpose(0, 4, 3, 1, 2)),
        "ctxN": c(tiles[:, :, :full].reshape(TILES, PER_TILE, CTX_CHUNKS, P, D).transpose(0, 3, 1, 2, 4)),
        "ctxR": c(tiles[:, :, full]),
        "w_sim": c(v["L0_xattn_w_sim"].reshape(3, DC, P).transpose(2, 0, 1)),
        "b_sim": c(v["L0_xattn_b_sim"]),
        "W_qv": c(v["L0_xattn_W_qv"]),
        "b_qv": c(v["L0_xattn_b_qv"]),
        "ident": np.eye(P, dtype=np.float32),
        "seq_of": np.repeat(np.eye(PER_TILE, dtype=np.float32), SEQ, axis=0),
    }
    pos = np.arange(SEQ, dtype=np.float32)
    inv_freq = np.float32(1.0) / np.float32(10000.0) ** (np.arange(0, HEAD, 2, dtype=np.float32) / np.float32(HEAD))
    theta = pos[:, None] * inv_freq[None, :].astype(np.float32)
    pair = np.arange(P) % HEAD // 2
    sign = np.where(np.arange(P) % 2 == 0, -1.0, 1.0).astype(np.float32)
    at = np.arange(P)
    qkv = v["L0_attn_w_qkv"].reshape(3, D, D)
    a |= {
        "attn_w": c(np.stack([v["L0_attn_w_pw"], qkv[0], qkv[1], qkv[2], v["L0_attn_w_gate"], v["L0_attn_w_o"]]).transpose(0, 2, 1)),
        "cos": c(np.cos(theta).astype(np.float32).T[pair]),
        "sin": c(np.sin(theta).astype(np.float32).T[pair] * sign[:, None]),
        "causal": ((at[:, None] // SEQ == at[None, :] // SEQ) & (at[:, None] <= at[None, :])).astype(np.float32),
        "w_dw": c(v["L0_attn_w_dw"].reshape(DC, P, 3).transpose(1, 0, 2)),
        "ones_strip": np.tile((np.arange(HEAD + DC - 1) == DC - 1).astype(np.float32), (P, 1)),
        "spread": (at[:, None, None] == at // HEAD * HEAD + np.arange(DC)[:, None]).astype(np.float32),
        "b_gate": c(v["L0_attn_b_gate"].reshape(DC, P).T),
    }
    moe_up = v["L0_attn_w1"].reshape(MOE_SUBS, SUB, DC, P)
    ffn_up = v["L0_ffn_w1"].reshape(FFN_SUBS, SUB, DC, P)
    moe_down = v["L0_attn_w2"].reshape(EXPERTS, D, SUBS_PER_EXPERT, FC, P).transpose(0, 2, 4, 3, 1).reshape(MOE_SUBS, P, FC, D)
    ffn_down = v["L0_ffn_w2"].reshape(D, FFN_SUBS, FC, P).transpose(1, 3, 2, 0)
    a |= {
        "up_w": c(np.concatenate([moe_up, ffn_up]).transpose(0, 3, 2, 1)),
        "down_w": c(np.concatenate([moe_down, ffn_down])),
        "up_bias": c(np.concatenate([v["L0_attn_b1"].reshape(-1), v["L0_ffn_b1"]]).reshape(SUBS * FC, P).T),
        "down_bias": c(np.concatenate([v["L0_attn_b2"], v["L0_ffn_b2"][None]])),
        "ln_g": c(v["L0_attn_ln_g"].reshape(DC, P).T),
        "ln_b": c(v["L0_attn_ln_b"].reshape(DC, P).T),
        "w_moe": c(v["L0_attn_w_moe_gate"].reshape(EXPERTS, DC, P).transpose(2, 1, 0)),
        "w_router": c(v["L0_ffn_w_router"].reshape(DC, P, BLOCKS).transpose(1, 0, 2)),
        "b_router": c(v["L0_ffn_b_router"]),
        "shut": c((np.arange(P)[:, None, None] == SEQ * np.arange(GROUPS)[:, None] + np.arange(BLOCKS)).astype(np.float32) * np.float32(SHUT)),
        "block_no": np.tile(np.arange(BLOCKS, dtype=np.float32), (P, 1)),
    }
    return a


def kernel(**inputs):
    import concourse.bacc as bacc
    from concourse.bass_utils import run_bass_kernel_spmd

    arrays = layouts({name: np.asarray(a) for name, a in inputs.items()})
    nc = bacc.Bacc("TRN2", target_bir_lowering=False, num_devices=1)
    dram = {name: nc.dram_tensor(name, a.shape, mybir.dt.from_np(a.dtype), kind="ExternalInput").ap()
            for name, a in arrays.items()}
    out = nc.dram_tensor("out", (TOKENS, D), F32, kind="ExternalOutput").ap()
    build(nc, dram, out)
    r = run_bass_kernel_spmd(nc, [arrays], core_ids=[0])
    return r.results[0]["out"].reshape(BATCH, SEQ, D)
```
